# Optimizing a Trainium2 kernel written in Bass

```python
import numpy as np
import jax
import jax.numpy as jnp

def _softmax(x, axis=-1):
    return jax.nn.softmax(x, axis=axis)

def _gelu(x):
    return jax.nn.gelu(x, approximate=True)

def _silu(x):
    return jax.nn.silu(x)

def _sigmoid(x):
    return jax.nn.sigmoid(x)

def _layernorm(x, axis=-1, eps=1e-05):
    m = jnp.mean(x, axis=axis, keepdims=True)
    v = jnp.var(x, axis=axis, keepdims=True)
    return (x - m) / jnp.sqrt(v + eps)

def _scatter_add(tgt, idx, src, axis=0):
    return tgt.at[idx].add(src)

def _segment_sum(src, seg, n):
    return jax.ops.segment_sum(src, seg, n)
kernel_name = 'mk_prb_d4_jaxref_r8_84dbbe'

def setup_inputs(seed: int=0):
    np.random.seed(seed)
    _w = jnp.asarray

    def _L0_attn_setup():
        import jax, jax.numpy as jnp
        import numpy as np
        key = jax.random.key(seed)
        k1, k2, k3 = jax.random.split(key, 3)
        N, S, D = (8, 256, 128)
        x = jax.random.normal(k1, (N, S, D), dtype=jnp.float32)
        std = np.sqrt(2.0 / D).astype(np.float32)
        w_lhs = jax.random.normal(k2, (1, 1, D), dtype=jnp.float32) * std
        w_rhs = jax.random.normal(k3, (1, 1, D), dtype=jnp.float32) * std
        return {'x': x, 'w_lhs': w_lhs, 'w_rhs': w_rhs}
    _L0_attn_in = _L0_attn_setup()

    def _L0_ffn_setup():
        import jax, jax.numpy as jnp
        import numpy as np
        EPS = 1e-06
        LN_EPS = 1e-05

        def _absmean_core(W):
            gamma = jnp.mean(jnp.abs(W)) + EPS
            Ws = W / gamma
            Wq = jnp.sign(Ws) * jnp.minimum(jnp.round(jnp.abs(Ws)), 1.0)
            return (Wq, gamma)

        @jax.custom_vjp
        def absmean(W):
            return _absmean_core(W)[0]

        def _absmean_fwd(W):
            Wq, gamma = _absmean_core(W)
            return (Wq, gamma)

        def _absmean_bwd(gamma, g):
            return (g / gamma,)
        absmean.defvjp(_absmean_fwd, _absmean_bwd)

        def layernorm(x, w, b, eps=LN_EPS):
            mu = jnp.mean(x, axis=-1, keepdims=True)
            var = jnp.mean((x - mu) ** 2, axis=-1, keepdims=True)
            return (x - mu) * jax.lax.rsqrt(var + eps) * w + b
        key = jax.random.key(seed)
        k1, k2, k3 = jax.random.split(key, 3)
        d, h = (128, 512)
        B, T = (8, 256)
        return {'x': jax.random.normal(k1, (B, T, d), jnp.float32), 'W_fc': jax.random.normal(k2, (h, d), jnp.float32), 'ln_w': jnp.ones((h,), jnp.float32), 'ln_b': jnp.zeros((h,), jnp.float32), 'W_proj': jax.random.normal(k3, (d, h), jnp.float32)}
    _L0_ffn_in = _L0_ffn_setup()

    def _L1_attn_setup():
        import jax, jax.numpy as jnp
        import numpy as np
        import math
        N_HEAD = 16
        V_HEAD = 32
        NOPE = 32
        ROPE_D = 64
        KEEP = 32
        EPS = 1e-06

        def _freqs(T, dim=ROPE_D, theta=10000.0):
            f = 1.0 / theta ** (jnp.arange(0, dim, 2, dtype=jnp.float32) / dim)
            t = jnp.arange(T, dtype=jnp.float32)
            a = jnp.outer(t, f)
            return (jnp.cos(a), jnp.sin(a))

        def _rope(x, cos, sin):
            S = x.shape[-2]
            c = cos[:S][None, None]
            s = sin[:S][None, None]
            x1, x2 = jnp.split(x, 2, axis=-1)
            return jnp.concatenate([x1 * c - x2 * s, x1 * s + x2 * c], axis=-1)

        def _rms(x, g, eps=EPS):
            return x * jax.lax.rsqrt(jnp.mean(x * x, axis=-1, keepdims=True) + eps) * g

        def _attn(q, k, v, causal):
            scale = 1.0 / math.sqrt(q.shape[-1])
            s = jnp.einsum('bhqd,bhkd->bhqk', q, k) * scale
            if causal:
                Tq, Tk = (s.shape[-2], s.shape[-1])
                mask = jnp.tril(jnp.ones((Tq, Tk), dtype=bool))
                s = jnp.where(mask, s, jnp.finfo(s.dtype).min)
            return jnp.einsum('bhqk,bhkd->bhqd', jax.nn.softmax(s, axis=-1), v)

        def _forward(x, w_cq, g_qnorm, w_dq_nope, w_dq_rope, w_ckv, g_kvnorm, w_dk_nope, w_dv, w_krope, w_imp, w_selk, w_selv, w_wink, w_winv, w_gate, w_proj):
            B, T, C = x.shape
            cos, sin = _freqs(T)
            nq = _rms(x @ w_cq, g_qnorm)
            q_nope = (nq @ w_dq_nope).reshape(B, T, N_HEAD, NOPE).transpose(0, 2, 1, 3)
            q_rope = (nq @ w_dq_rope).reshape(B, T, N_HEAD, ROPE_D).transpose(0, 2, 1, 3)
            q_rope = _rope(q_rope, cos, sin)
            q = jnp.concatenate([q_nope, q_rope], axis=-1)
            gate = jax.nn.softmax((x @ w_gate).mean(axis=1), axis=-1)
            ckv = _rms(x @ w_ckv, g_kvnorm)
            k_nope = (ckv @ w_dk_nope).reshape(B, T, N_HEAD, NOPE).transpose(0, 2, 1, 3)
            v1 = (ckv @ w_dv).reshape(B, T, N_HEAD, V_HEAD).transpose(0, 2, 1, 3)
            k_rope = (x @ w_krope).reshape(B, T, 1, ROPE_D).transpose(0, 2, 1, 3) / N_HEAD
            k_rope = _rope(k_rope, cos, sin)
            k1 = jnp.concatenate([k_nope, jnp.broadcast_to(k_rope, (B, N_HEAD, T, ROPE_D))], axis=-1)
            scores = (x @ w_imp)[..., 0]
            _, idx = jax.lax.top_k(scores, KEEP)
            idx = jnp.sort(idx, axis=1)
            sel = jnp.take_along_axis(x, idx[:, :, None], axis=1)
            ks = (sel @ w_selk).reshape(B, KEEP, N_HEAD, NOPE + ROPE_D).transpose(0, 2, 1, 3)
            vs = (sel @ w_selv).reshape(B, KEEP, N_HEAD, V_HEAD).transpose(0, 2, 1, 3)
            ks = jnp.concatenate([ks[..., :NOPE], _rope(ks[..., NOPE:], cos, sin)], axis=-1)
            kw = (x @ w_wink).reshape(B, T, N_HEAD, NOPE + ROPE_D).transpose(0, 2, 1, 3)
            vw = (x @ w_winv).reshape(B, T, N_HEAD, V_HEAD).transpose(0, 2, 1, 3)
            kw = jnp.concatenate([kw[..., :NOPE], _rope(kw[..., NOPE:], cos, sin)], axis=-1)
            a1 = _attn(q, k1, v1, causal=True)
            a2 = _attn(q, ks, vs, causal=False)
            a3 = _attn(q, kw, vw, causal=True)
            g = gate[:, :, None, None, None]
            out = g[:, 0] * a1 + g[:, 1] * a2 + g[:, 2] * a3
            out = out.transpose(0, 2, 1, 3).reshape(B, T, N_HEAD * V_HEAD)
            return out @ w_proj
        key = jax.random.key(seed)
        ks = jax.random.split(key, 20)
        B, T, C = (2, 128, 128)
        q_lora, kv_lora = (96, 32)
        std = 0.02

        def w(k, shape):
            return jax.random.normal(k, shape, dtype=jnp.float32) * std
        return {'x': jax.random.normal(ks[0], (B, T, C), dtype=jnp.float32), 'w_cq': w(ks[1], (C, q_lora)), 'g_qnorm': jnp.ones((q_lora,), jnp.float32), 'w_dq_nope': w(ks[2], (q_lora, N_HEAD * NOPE)), 'w_dq_rope': w(ks[3], (q_lora, N_HEAD * ROPE_D)), 'w_ckv': w(ks[4], (C, kv_lora)), 'g_kvnorm': jnp.ones((kv_lora,), jnp.float32), 'w_dk_nope': w(ks[5], (kv_lora, N_HEAD * NOPE)), 'w_dv': w(ks[6], (kv_lora, N_HEAD * V_HEAD)), 'w_krope': w(ks[7], (C, ROPE_D)), 'w_imp': w(ks[8], (C, 1)), 'w_selk': w(ks[9], (C, N_HEAD * (NOPE + ROPE_D))), 'w_selv': w(ks[10], (C, N_HEAD * V_HEAD)), 'w_wink': w(ks[11], (C, N_HEAD * (NOPE + ROPE_D))), 'w_winv': w(ks[12], (C, N_HEAD * V_HEAD)), 'w_gate': w(ks[13], (C, 3)), 'w_proj': w(ks[14], (N_HEAD * V_HEAD, C))}
    _L1_attn_in = _L1_attn_setup()

    def _L1_ffn_setup():
        import jax, jax.numpy as jnp
        import numpy as np
        D_MODEL = 128
        M = 64
        INNER = 16
        key = jax.random.key(seed)
        ks = jax.random.split(key, 9)

        def init(k, shape, fan_in):
            bound = 1.0 / np.sqrt(fan_in)
            return jax.random.uniform(k, shape, jnp.float32, -bound, bound)
        x = jax.random.normal(ks[0], (16, 512, D_MODEL), dtype=jnp.float32)
        Win = init(ks[1], (D_MODEL, M), D_MODEL)
        bin_ = init(ks[2], (M,), D_MODEL)
        W1 = init(ks[3], (M, INNER), 1)
        b1 = init(ks[4], (M, INNER), 1)
        W2 = init(ks[5], (M, INNER), INNER)
        b2 = init(ks[6], (M,), INNER)
        Wout = init(ks[7], (M, D_MODEL), M)
        bout = init(ks[8], (D_MODEL,), M)
        return {'x': x, 'Win': Win, 'bin_': bin_, 'W1': W1, 'b1': b1, 'W2': W2, 'b2': b2, 'Wout': Wout, 'bout': bout}
    _L1_ffn_in = _L1_ffn_setup()

    def _L2_attn_setup():
        import jax, jax.numpy as jnp
        import numpy as np
        KEY_DIM = 128
        SCALE = KEY_DIM ** (-0.5)
        key = jax.random.key(seed)
        k1, k2, k3, k4 = jax.random.split(key, 4)
        B, S, E = (4, 256, 128)
        x = jax.random.normal(k1, (B, S, E), dtype=jnp.float32)
        WQ = jax.random.normal(k2, (KEY_DIM, E), dtype=jnp.float32) * E ** (-0.5)
        WK = jax.random.normal(k3, (KEY_DIM, E), dtype=jnp.float32) * E ** (-0.5)
        WV = jax.random.normal(k4, (KEY_DIM, E), dtype=jnp.float32) * E ** (-0.5)
        return {'x': x, 'WQ': WQ, 'WK': WK, 'WV': WV}
    _L2_attn_in = _L2_attn_setup()

    def _L2_ffn_setup():
        import jax, jax.numpy as jnp
        import numpy as np
        DIM = 128
        N_EXPERTS = 16
        TOP_K = 4
        N_GROUP = 4
        TOPK_GROUP = 2
        MOE_INTER = 64
        SHARED_INTER = 256
        ROUTED_SCALE = 2.5

        def relu2(x):
            return jnp.square(jax.nn.relu(x))

        def _router(x2, gate_w, bias_e):
            T = x2.shape[0]
            logits = x2 @ gate_w.T
            scores = jax.nn.sigmoid(logits)
            sc = jax.lax.stop_gradient(scores + bias_e[None, :])
            grp = sc.reshape(T, N_GROUP, N_EXPERTS // N_GROUP)
            top2, _ = jax.lax.top_k(grp, 2)
            group_scores = top2.sum(-1)
            _, gidx = jax.lax.top_k(group_scores, TOPK_GROUP)
            rows = jnp.arange(T)[:, None]
            gmask = jnp.zeros((T, N_GROUP), dtype=sc.dtype).at[rows, gidx].set(1.0)
            smask = jnp.repeat(gmask, N_EXPERTS // N_GROUP, axis=1)
            masked = jnp.where(smask > 0, sc, 0.0)
            _, topk_idx = jax.lax.top_k(masked, TOP_K)
            topk_w = jnp.take_along_axis(scores, topk_idx, axis=1)
            topk_w = topk_w / (topk_w.sum(-1, keepdims=True) + 1e-20)
            topk_w = topk_w * ROUTED_SCALE
            return (topk_idx, topk_w)
        key = jax.random.key(seed)
        ks = jax.random.split(key, 6)
        hidden_states = jax.random.normal(ks[0], (2, 256, DIM), dtype=jnp.float32)
        gate_w = jax.random.normal(ks[1], (N_EXPERTS, DIM), dtype=jnp.float32) * 0.02
        bias_e = jnp.zeros((N_EXPERTS,), dtype=jnp.float32)
        up_w = jax.random.normal(ks[2], (N_EXPERTS, MOE_INTER, DIM), dtype=jnp.float32) * 0.02
        down_w = jax.random.normal(ks[3], (N_EXPERTS, DIM, MOE_INTER), dtype=jnp.float32) * 0.02
        shared_up = jax.random.normal(ks[4], (SHARED_INTER, DIM), dtype=jnp.float32) * 0.02
        shared_down = jax.random.normal(ks[5], (DIM, SHARED_INTER), dtype=jnp.float32) * 0.02
        return {'hidden_states': hidden_states, 'gate_w': gate_w, 'bias_e': bias_e, 'up_w': up_w, 'down_w': down_w, 'shared_up': shared_up, 'shared_down': shared_down}
    _L2_ffn_in = _L2_ffn_setup()

    def _L3_attn_setup():
        import jax, jax.numpy as jnp
        import numpy as np
        D_MODEL, D_K, D_V, N_HEADS = (128, 64, 64, 16)
        B, T = (4, 256)

        def _xavier(key, shape, gain):
            fan_in, fan_out = (shape[0], shape[1])
            a = gain * np.sqrt(6.0 / (fan_in + fan_out))
            return jax.random.uniform(key, shape, jnp.float32, -a, a)
        key = jax.random.key(seed)
        ks = jax.random.split(key, 6)
        H, dk, dv, d = (N_HEADS, D_K, D_V, D_MODEL)
        return {'x': jax.random.normal(ks[0], (B, T, d), jnp.float32), 'W_q': _xavier(ks[1], (d, H * dk), 0.1), 'W_k': _xavier(ks[2], (d, H * dk), 0.1), 'W_v': _xavier(ks[3], (d, H * dv), 0.1), 'W_gate': _xavier(ks[4], (d, H * dk), 0.01), 'b_gate': jnp.full((H * dk,), 3.0, jnp.float32), 'W_o': _xavier(ks[5], (H * dv, d), 0.1)}
    _L3_attn_in = _L3_attn_setup()

    def _L3_ffn_setup():
        import math
        import jax, jax.numpy as jnp
        import numpy as np
        B, L, D, FF, E, K = (4, 256, 128, 512, 8, 2)
        CAPACITY_FACTOR = 1.25
        T = B * L
        CAP = math.ceil(CAPACITY_FACTOR * T * K / E)
        key = jax.random.key(seed)
        ks = jax.random.split(key, 7)
        return {'h': jax.random.normal(ks[0], (B, L, D), dtype=jnp.float32), 'gate_w': 0.02 * jax.random.normal(ks[1], (E, D), dtype=jnp.float32), 'gate_b': jnp.zeros((E,), dtype=jnp.float32), 'W1': 0.02 * jax.random.normal(ks[2], (E, D, FF), dtype=jnp.float32), 'b1': jnp.zeros((E, FF), dtype=jnp.float32), 'W2': 0.02 * jax.random.normal(ks[3], (E, FF, D), dtype=jnp.float32), 'b2': jnp.zeros((E, D), dtype=jnp.float32)}
    _L3_ffn_in = _L3_ffn_setup()
    _d = {'L0_attn_x': _L0_attn_in['x'], 'L0_attn_w_lhs': _L0_attn_in['w_lhs'], 'L0_attn_w_rhs': _L0_attn_in['w_rhs'], 'L0_ffn_W_fc': _L0_ffn_in['W_fc'], 'L0_ffn_ln_w': _L0_ffn_in['ln_w'], 'L0_ffn_ln_b': _L0_ffn_in['ln_b'], 'L0_ffn_W_proj': _L0_ffn_in['W_proj'], 'L1_attn_w_cq': _L1_attn_in['w_cq'], 'L1_attn_g_qnorm': _L1_attn_in['g_qnorm'], 'L1_attn_w_dq_nope': _L1_attn_in['w_dq_nope'], 'L1_attn_w_dq_rope': _L1_attn_in['w_dq_rope'], 'L1_attn_w_ckv': _L1_attn_in['w_ckv'], 'L1_attn_g_kvnorm': _L1_attn_in['g_kvnorm'], 'L1_attn_w_dk_nope': _L1_attn_in['w_dk_nope'], 'L1_attn_w_dv': _L1_attn_in['w_dv'], 'L1_attn_w_krope': _L1_attn_in['w_krope'], 'L1_attn_w_imp': _L1_attn_in['w_imp'], 'L1_attn_w_selk': _L1_attn_in['w_selk'], 'L1_attn_w_selv': _L1_attn_in['w_selv'], 'L1_attn_w_wink': _L1_attn_in['w_wink'], 'L1_attn_w_winv': _L1_attn_in['w_winv'], 'L1_attn_w_gate': _L1_attn_in['w_gate'], 'L1_attn_w_proj': _L1_attn_in['w_proj'], 'L1_ffn_Win': _L1_ffn_in['Win'], 'L1_ffn_bin_': _L1_ffn_in['bin_'], 'L1_ffn_W1': _L1_ffn_in['W1'], 'L1_ffn_b1': _L1_ffn_in['b1'], 'L1_ffn_W2': _L1_ffn_in['W2'], 'L1_ffn_b2': _L1_ffn_in['b2'], 'L1_ffn_Wout': _L1_ffn_in['Wout'], 'L1_ffn_bout': _L1_ffn_in['bout'], 'L2_attn_WQ': _L2_attn_in['WQ'], 'L2_attn_WK': _L2_attn_in['WK'], 'L2_attn_WV': _L2_attn_in['WV'], 'L2_ffn_gate_w': _L2_ffn_in['gate_w'], 'L2_ffn_bias_e': _L2_ffn_in['bias_e'], 'L2_ffn_up_w': _L2_ffn_in['up_w'], 'L2_ffn_down_w': _L2_ffn_in['down_w'], 'L2_ffn_shared_up': _L2_ffn_in['shared_up'], 'L2_ffn_shared_down': _L2_ffn_in['shared_down'], 'L3_attn_W_q': _L3_attn_in['W_q'], 'L3_attn_W_k': _L3_attn_in['W_k'], 'L3_attn_W_v': _L3_attn_in['W_v'], 'L3_attn_W_gate': _L3_attn_in['W_gate'], 'L3_attn_b_gate': _L3_attn_in['b_gate'], 'L3_attn_W_o': _L3_attn_in['W_o'], 'L3_ffn_gate_w': _L3_ffn_in['gate_w'], 'L3_ffn_gate_b': _L3_ffn_in['gate_b'], 'L3_ffn_W1': _L3_ffn_in['W1'], 'L3_ffn_b1': _L3_ffn_in['b1'], 'L3_ffn_W2': _L3_ffn_in['W2'], 'L3_ffn_b2': _L3_ffn_in['b2']}
    _x0 = _d['L0_attn_x']
    _d['L0_attn_x'] = jax.random.normal(jax.random.fold_in(jax.random.key(seed), 1), (8, 256, 128), dtype=_x0.dtype)
    del _x0
    return _d

def reference(L0_attn_x, L0_attn_w_lhs, L0_attn_w_rhs, L0_ffn_W_fc, L0_ffn_ln_w, L0_ffn_ln_b, L0_ffn_W_proj, L1_attn_w_cq, L1_attn_g_qnorm, L1_attn_w_dq_nope, L1_attn_w_dq_rope, L1_attn_w_ckv, L1_attn_g_kvnorm, L1_attn_w_dk_nope, L1_attn_w_dv, L1_attn_w_krope, L1_attn_w_imp, L1_attn_w_selk, L1_attn_w_selv, L1_attn_w_wink, L1_attn_w_winv, L1_attn_w_gate, L1_attn_w_proj, L1_ffn_Win, L1_ffn_bin_, L1_ffn_W1, L1_ffn_b1, L1_ffn_W2, L1_ffn_b2, L1_ffn_Wout, L1_ffn_bout, L2_attn_WQ, L2_attn_WK, L2_attn_WV, L2_ffn_gate_w, L2_ffn_bias_e, L2_ffn_up_w, L2_ffn_down_w, L2_ffn_shared_up, L2_ffn_shared_down, L3_attn_W_q, L3_attn_W_k, L3_attn_W_v, L3_attn_W_gate, L3_attn_b_gate, L3_attn_W_o, L3_ffn_gate_w, L3_ffn_gate_b, L3_ffn_W1, L3_ffn_b1, L3_ffn_W2, L3_ffn_b2):

    def _L0_attn_ref(x, w_lhs, w_rhs):
        import jax, jax.numpy as jnp
        import numpy as np
        lhs = x * w_lhs
        rhs = x * w_rhs
        scores = jnp.einsum('nsd,ntd->nst', lhs, rhs)
        attn = jax.nn.softmax(scores, axis=2)
        return jnp.einsum('nst,ntd->nsd', attn, x)

    def _L0_ffn_ref(x, W_fc, ln_w, ln_b, W_proj):
        import jax, jax.numpy as jnp
        import numpy as np
        EPS = 1e-06
        LN_EPS = 1e-05

        def _absmean_core(W):
            gamma = jnp.mean(jnp.abs(W)) + EPS
            Ws = W / gamma
            Wq = jnp.sign(Ws) * jnp.minimum(jnp.round(jnp.abs(Ws)), 1.0)
            return (Wq, gamma)

        @jax.custom_vjp
        def absmean(W):
            return _absmean_core(W)[0]

        def _absmean_fwd(W):
            Wq, gamma = _absmean_core(W)
            return (Wq, gamma)

        def _absmean_bwd(gamma, g):
            return (g / gamma,)
        absmean.defvjp(_absmean_fwd, _absmean_bwd)

        def layernorm(x, w, b, eps=LN_EPS):
            mu = jnp.mean(x, axis=-1, keepdims=True)
            var = jnp.mean((x - mu) ** 2, axis=-1, keepdims=True)
            return (x - mu) * jax.lax.rsqrt(var + eps) * w + b
        h = jnp.einsum('btd,hd->bth', x, absmean(W_fc))
        h = jax.nn.gelu(h, approximate=False)
        h = layernorm(h, ln_w, ln_b)
        return jnp.einsum('bth,dh->btd', h, absmean(W_proj))

    def _L1_attn_ref(x, w_cq, g_qnorm, w_dq_nope, w_dq_rope, w_ckv, g_kvnorm, w_dk_nope, w_dv, w_krope, w_imp, w_selk, w_selv, w_wink, w_winv, w_gate, w_proj):
        import jax, jax.numpy as jnp
        import numpy as np
        import math
        N_HEAD = 16
        V_HEAD = 32
        NOPE = 32
        ROPE_D = 64
        KEEP = 32
        EPS = 1e-06

        def _freqs(T, dim=ROPE_D, theta=10000.0):
            f = 1.0 / theta ** (jnp.arange(0, dim, 2, dtype=jnp.float32) / dim)
            t = jnp.arange(T, dtype=jnp.float32)
            a = jnp.outer(t, f)
            return (jnp.cos(a), jnp.sin(a))

        def _rope(x, cos, sin):
            S = x.shape[-2]
            c = cos[:S][None, None]
            s = sin[:S][None, None]
            x1, x2 = jnp.split(x, 2, axis=-1)
            return jnp.concatenate([x1 * c - x2 * s, x1 * s + x2 * c], axis=-1)

        def _rms(x, g, eps=EPS):
            return x * jax.lax.rsqrt(jnp.mean(x * x, axis=-1, keepdims=True) + eps) * g

        def _attn(q, k, v, causal):
            scale = 1.0 / math.sqrt(q.shape[-1])
            s = jnp.einsum('bhqd,bhkd->bhqk', q, k) * scale
            if causal:
                Tq, Tk = (s.shape[-2], s.shape[-1])
                mask = jnp.tril(jnp.ones((Tq, Tk), dtype=bool))
                s = jnp.where(mask, s, jnp.finfo(s.dtype).min)
            return jnp.einsum('bhqk,bhkd->bhqd', jax.nn.softmax(s, axis=-1), v)

        def _forward(x, w_cq, g_qnorm, w_dq_nope, w_dq_rope, w_ckv, g_kvnorm, w_dk_nope, w_dv, w_krope, w_imp, w_selk, w_selv, w_wink, w_winv, w_gate, w_proj):
            B, T, C = x.shape
            cos, sin = _freqs(T)
            nq = _rms(x @ w_cq, g_qnorm)
            q_nope = (nq @ w_dq_nope).reshape(B, T, N_HEAD, NOPE).transpose(0, 2, 1, 3)
            q_rope = (nq @ w_dq_rope).reshape(B, T, N_HEAD, ROPE_D).transpose(0, 2, 1, 3)
            q_rope = _rope(q_rope, cos, sin)
            q = jnp.concatenate([q_nope, q_rope], axis=-1)
            gate = jax.nn.softmax((x @ w_gate).mean(axis=1), axis=-1)
            ckv = _rms(x @ w_ckv, g_kvnorm)
            k_nope = (ckv @ w_dk_nope).reshape(B, T, N_HEAD, NOPE).transpose(0, 2, 1, 3)
            v1 = (ckv @ w_dv).reshape(B, T, N_HEAD, V_HEAD).transpose(0, 2, 1, 3)
            k_rope = (x @ w_krope).reshape(B, T, 1, ROPE_D).transpose(0, 2, 1, 3) / N_HEAD
            k_rope = _rope(k_rope, cos, sin)
            k1 = jnp.concatenate([k_nope, jnp.broadcast_to(k_rope, (B, N_HEAD, T, ROPE_D))], axis=-1)
            scores = (x @ w_imp)[..., 0]
            _, idx = jax.lax.top_k(scores, KEEP)
            idx = jnp.sort(idx, axis=1)
            sel = jnp.take_along_axis(x, idx[:, :, None], axis=1)
            ks = (sel @ w_selk).reshape(B, KEEP, N_HEAD, NOPE + ROPE_D).transpose(0, 2, 1, 3)
            vs = (sel @ w_selv).reshape(B, KEEP, N_HEAD, V_HEAD).transpose(0, 2, 1, 3)
            ks = jnp.concatenate([ks[..., :NOPE], _rope(ks[..., NOPE:], cos, sin)], axis=-1)
            kw = (x @ w_wink).reshape(B, T, N_HEAD, NOPE + ROPE_D).transpose(0, 2, 1, 3)
            vw = (x @ w_winv).reshape(B, T, N_HEAD, V_HEAD).transpose(0, 2, 1, 3)
            kw = jnp.concatenate([kw[..., :NOPE], _rope(kw[..., NOPE:], cos, sin)], axis=-1)
            a1 = _attn(q, k1, v1, causal=True)
            a2 = _attn(q, ks, vs, causal=False)
            a3 = _attn(q, kw, vw, causal=True)
            g = gate[:, :, None, None, None]
            out = g[:, 0] * a1 + g[:, 1] * a2 + g[:, 2] * a3
            out = out.transpose(0, 2, 1, 3).reshape(B, T, N_HEAD * V_HEAD)
            return out @ w_proj
        return _forward(x, w_cq, g_qnorm, w_dq_nope, w_dq_rope, w_ckv, g_kvnorm, w_dk_nope, w_dv, w_krope, w_imp, w_selk, w_selv, w_wink, w_winv, w_gate, w_proj)

    def _L1_ffn_ref(x, Win, bin_, W1, b1, W2, b2, Wout, bout):
        import jax, jax.numpy as jnp
        import numpy as np
        D_MODEL = 128
        M = 64
        INNER = 16
        s = jnp.einsum('btd,dm->btm', x, Win) + bin_
        h = jax.nn.relu(s[..., None] * W1 + b1)
        g = jnp.einsum('btmh,mh->btm', h, W2) + b2
        out = jnp.einsum('btm,md->btd', g, Wout) + bout
        return out

    def _L2_attn_ref(x, WQ, WK, WV):
        import jax, jax.numpy as jnp
        import numpy as np
        KEY_DIM = 128
        SCALE = KEY_DIM ** (-0.5)
        q = jnp.einsum('bse,ke->bsk', x, WQ)
        k = jnp.einsum('bse,ke->bsk', x, WK)
        v = jnp.einsum('bse,ve->bsv', x, WV)
        scores = jnp.einsum('bsk,btk->bst', q, k) * SCALE
        masked = jnp.where(jnp.tril(scores) == 0, -jnp.inf, scores)
        attn = jax.nn.softmax(masked, axis=-1)
        return jnp.einsum('bst,btv->bsv', attn, v)

    def _L2_ffn_ref(hidden_states, gate_w, bias_e, up_w, down_w, shared_up, shared_down):
        import jax, jax.numpy as jnp
        import numpy as np
        DIM = 128
        N_EXPERTS = 16
        TOP_K = 4
        N_GROUP = 4
        TOPK_GROUP = 2
        MOE_INTER = 64
        SHARED_INTER = 256
        ROUTED_SCALE = 2.5

        def relu2(x):
            return jnp.square(jax.nn.relu(x))

        def _router(x2, gate_w, bias_e):
            T = x2.shape[0]
            logits = x2 @ gate_w.T
            scores = jax.nn.sigmoid(logits)
            sc = jax.lax.stop_gradient(scores + bias_e[None, :])
            grp = sc.reshape(T, N_GROUP, N_EXPERTS // N_GROUP)
            top2, _ = jax.lax.top_k(grp, 2)
            group_scores = top2.sum(-1)
            _, gidx = jax.lax.top_k(group_scores, TOPK_GROUP)
            rows = jnp.arange(T)[:, None]
            gmask = jnp.zeros((T, N_GROUP), dtype=sc.dtype).at[rows, gidx].set(1.0)
            smask = jnp.repeat(gmask, N_EXPERTS // N_GROUP, axis=1)
            masked = jnp.where(smask > 0, sc, 0.0)
            _, topk_idx = jax.lax.top_k(masked, TOP_K)
            topk_w = jnp.take_along_axis(scores, topk_idx, axis=1)
            topk_w = topk_w / (topk_w.sum(-1, keepdims=True) + 1e-20)
            topk_w = topk_w * ROUTED_SCALE
            return (topk_idx, topk_w)
        B, S, D = hidden_states.shape
        x2 = hidden_states.reshape(-1, D)
        T = x2.shape[0]
        topk_idx, topk_w = _router(x2, gate_w, bias_e)
        rows = jnp.arange(T)[:, None]
        combine = jnp.zeros((T, N_EXPERTS), dtype=topk_w.dtype).at[rows, topk_idx].add(topk_w)

        def body(acc, inp):
            wu, wd, cw = inp
            y = relu2(x2 @ wu.T) @ wd.T
            return (acc + cw[:, None] * y, None)
        routed, _ = jax.lax.scan(body, jnp.zeros_like(x2), (up_w, down_w, combine.T))
        shared = relu2(x2 @ shared_up.T) @ shared_down.T
        out = routed + shared
        return out.reshape(B, S, D)

    def _L3_attn_ref(x, W_q, W_k, W_v, W_gate, b_gate, W_o):
        import jax, jax.numpy as jnp
        import numpy as np
        D_MODEL, D_K, D_V, N_HEADS = (128, 64, 64, 16)
        B, T = (4, 256)

        def _xavier(key, shape, gain):
            fan_in, fan_out = (shape[0], shape[1])
            a = gain * np.sqrt(6.0 / (fan_in + fan_out))
            return jax.random.uniform(key, shape, jnp.float32, -a, a)
        Bn, Tn, d = x.shape
        H, dk, dv = (N_HEADS, D_K, D_V)
        q = (x @ W_q).reshape(Bn, Tn, H, dk)
        k = (x @ W_k).reshape(Bn, Tn, H, dk)
        v = (x @ W_v).reshape(Bn, Tn, H, dv)
        a = jax.nn.sigmoid(x @ W_gate + b_gate).reshape(Bn, Tn, H, dk)

        def step(S, qkva):
            q_t, k_t, v_t, a_t = qkva
            S = a_t[..., None] * S + k_t[..., None] * v_t[..., None, :]
            o_t = jnp.einsum('bhk,bhkv->bhv', q_t, S)
            return (S, o_t)
        S0 = jnp.zeros((Bn, H, dk, dv), x.dtype)
        qs = jnp.moveaxis(q, 1, 0)
        ks_ = jnp.moveaxis(k, 1, 0)
        vs = jnp.moveaxis(v, 1, 0)
        as_ = jnp.moveaxis(a, 1, 0)
        _, outs = jax.lax.scan(step, S0, (qs, ks_, vs, as_))
        out = jnp.moveaxis(outs, 0, 1).reshape(Bn, Tn, H * dv)
        return out @ W_o

    def _L3_ffn_ref(h, gate_w, gate_b, W1, b1, W2, b2):
        import math
        import jax, jax.numpy as jnp
        import numpy as np
        B, L, D, FF, E, K = (4, 256, 128, 512, 8, 2)
        CAPACITY_FACTOR = 1.25
        T = B * L
        CAP = math.ceil(CAPACITY_FACTOR * T * K / E)
        Bb, Ll, Dm = h.shape
        Tt = Bb * Ll
        x = h.reshape(Tt, Dm)
        logits = x @ gate_w.T + gate_b
        probs = jax.nn.softmax(logits, axis=-1)
        topk_prob, topk_idx = jax.lax.top_k(probs, K)
        y = jnp.zeros((Tt, Dm), dtype=h.dtype)
        n_slots = E * CAP
        for c in range(K):
            idx = topk_idx[:, c]
            prb = topk_prob[:, c]
            oh = jax.nn.one_hot(idx, E, dtype=jnp.int32)
            pos = jnp.take_along_axis(jnp.cumsum(oh, axis=0) - 1, idx[:, None], axis=1)[:, 0]
            keep = pos < CAP
            buf_idx = jnp.where(keep, idx * CAP + pos, n_slots)
            xbuf = jnp.zeros((n_slots, Dm), x.dtype).at[buf_idx].set(x, mode='drop')
            xb = xbuf.reshape(E, CAP, Dm)
            hmid = jax.nn.relu(jnp.einsum('ecd,edf->ecf', xb, W1) + b1[:, None, :])
            yb = jnp.einsum('ecf,efd->ecd', hmid, W2) + b2[:, None, :]
            ytok = yb.reshape(n_slots, Dm)[jnp.clip(buf_idx, 0, n_slots - 1)]
            y = y + ytok * (prb * keep.astype(prb.dtype))[:, None]
        return y.reshape(Bb, Ll, Dm)
    x = L0_attn_x
    xn = _layernorm(x, axis=-1)
    x = x + _L0_attn_ref(xn, L0_attn_w_lhs, L0_attn_w_rhs) + _L0_ffn_ref(xn, L0_ffn_W_fc, L0_ffn_ln_w, L0_ffn_ln_b, L0_ffn_W_proj)
    xn = _layernorm(x, axis=-1)
    x = x + _L1_attn_ref(xn, L1_attn_w_cq, L1_attn_g_qnorm, L1_attn_w_dq_nope, L1_attn_w_dq_rope, L1_attn_w_ckv, L1_attn_g_kvnorm, L1_attn_w_dk_nope, L1_attn_w_dv, L1_attn_w_krope, L1_attn_w_imp, L1_attn_w_selk, L1_attn_w_selv, L1_attn_w_wink, L1_attn_w_winv, L1_attn_w_gate, L1_attn_w_proj) + _L1_ffn_ref(xn, L1_ffn_Win, L1_ffn_bin_, L1_ffn_W1, L1_ffn_b1, L1_ffn_W2, L1_ffn_b2, L1_ffn_Wout, L1_ffn_bout)
    xn = _layernorm(x, axis=-1)
    x = x + _L2_attn_ref(xn, L2_attn_WQ, L2_attn_WK, L2_attn_WV) + _L2_ffn_ref(xn, L2_ffn_gate_w, L2_ffn_bias_e, L2_ffn_up_w, L2_ffn_down_w, L2_ffn_shared_up, L2_ffn_shared_down)
    xn = _layernorm(x, axis=-1)
    x = x + _L3_attn_ref(xn, L3_attn_W_q, L3_attn_W_k, L3_attn_W_v, L3_attn_W_gate, L3_attn_b_gate, L3_attn_W_o) + _L3_ffn_ref(xn, L3_ffn_gate_w, L3_ffn_gate_b, L3_ffn_W1, L3_ffn_b1, L3_ffn_W2, L3_ffn_b2)
    return x

_drawn_inputs = setup_inputs


def setup_inputs(seed=0):
    import zlib

    import numpy as np

    out = dict(_drawn_inputs(seed))
    spreads = {'L0_ffn_ln_w': (1.0, 0.2),
     'L0_ffn_ln_b': (0.0, 0.1),
     'L1_attn_g_qnorm': (1.0, 0.6),
     'L1_attn_g_kvnorm': (1.0, 0.6),
     'L2_ffn_bias_e': (0.0, 2.0),
     'L3_attn_b_gate': (3.0, 0.6),
     'L3_ffn_gate_b': (0.0, 2.0),
     'L3_ffn_b1': (0.0, 2.0),
     'L3_ffn_b2': (0.0, 2.0)}
    factors = {'L0_attn_w_lhs': 8.0,
     'L0_attn_w_rhs': 8.0,
     'L1_attn_w_cq': 48.012,
     'L1_attn_w_dq_nope': 60.477,
     'L1_attn_w_dq_rope': 53.881,
     'L1_attn_w_ckv': 64.0,
     'L1_attn_w_dk_nope': 64.0,
     'L1_attn_w_dv': 64.0,
     'L1_attn_w_krope': 64.0,
     'L1_attn_w_imp': 61.367,
     'L1_attn_w_selk': 61.409,
     'L1_attn_w_selv': 57.179,
     'L1_attn_w_wink': 64.0,
     'L1_attn_w_winv': 64.0,
     'L1_attn_w_gate': 64.0,
     'L1_attn_w_proj': 45.153,
     'L1_ffn_Win': 8.0,
     'L1_ffn_bin_': 8.0,
     'L1_ffn_W1': 8.0,
     'L1_ffn_b1': 8.0,
     'L1_ffn_W2': 7.114,
     'L1_ffn_b2': 8.0,
     'L1_ffn_Wout': 6.328,
     'L1_ffn_bout': 64.0,
     'L2_attn_WQ': 24.537,
     'L2_attn_WK': 25.127,
     'L2_attn_WV': 13.88,
     'L2_ffn_gate_w': 21.403,
     'L2_ffn_up_w': 8.0,
     'L2_ffn_down_w': 8.0,
     'L2_ffn_shared_up': 8.0,
     'L2_ffn_shared_down': 8.0,
     'L3_attn_W_q': 23.627,
     'L3_attn_W_k': 22.23,
     'L3_attn_W_v': 23.591,
     'L3_attn_W_gate': 200.0,
     'L3_attn_W_o': 23.755,
     'L3_ffn_gate_w': 47.119,
     'L3_ffn_W1': 59.541,
     'L3_ffn_W2': 45.706}
    for name, (base, spread) in spreads.items():
        noise = np.random.default_rng([zlib.crc32(name.encode()), seed]).standard_normal(out[name].shape)
        drawn = base * np.exp(spread * noise) if base else spread * noise
        out[name] = jnp.asarray(drawn.astype(out[name].dtype))
    for name, factor in factors.items():
        out[name] = (out[name] * factor).astype(out[name].dtype)
    return out
```

```python
from contextlib import ExitStack

import numpy as np

import concourse.bass as bass
from concourse import mybir

F32 = mybir.dt.float32
BF16 = mybir.dt.bfloat16
U32 = mybir.dt.uint32
ALU = mybir.AluOpType
ACT = mybir.ActivationFunctionType
X = mybir.AxisListType.X

P = 128
B, S, D = 8, 256, 128
T = S // P
LN_EPS = 1e-5

H0 = 512
C0 = H0 // P
NH, NOPE, ROPE, VH = 16, 32, 64, 32
QK = NOPE + ROPE
QL, KVL = 96, 32
KEEP = 32
HG = 4
G1 = NH // HG
M1, INNER = 64, 16
J1 = P // M1
R1 = INNER // J1
NEG = -1e30
E2, K2, GR2, I2, SH2 = 16, 4, 4, 64, 256
EP2 = E2 * I2 // P
SP2 = SH2 // P
ROUTED_SCALE = 2.5
NH3, DK3 = 16, 64
PAIRS = NH3 * DK3 // P
LEVELS = [1, 2, 4, 8, 16, 32, 64]
E3, F3 = 8, 512
FC3 = F3 // P
CAP3 = -(-5 * 4 * 256 * 2 // (4 * E3))


def constants():
    i = np.arange(P)
    out = {}
    out["ident"] = np.eye(P, dtype=np.float32)
    out["causal"] = (i[:, None] >= i[None, :]).astype(np.float32)
    out["tri"] = (i[:, None] <= i[None, :]).astype(np.float32)
    out["negmask"] = np.where(i[:, None] >= i[None, :], 0.0, NEG).astype(np.float32)
    out["iota"] = np.broadcast_to(np.arange(KEEP, dtype=np.float32), (P, KEEP)).copy()
    e = np.arange(E2)
    out["before"] = np.broadcast_to((e[None, :] < e[:, None]).astype(np.float32).reshape(-1), (P, E2 * E2)).copy()
    spread = np.zeros((P, EP2, P), np.float32)
    for p in range(EP2):
        for m in range(P):
            spread[(P // I2) * p + m // I2, p, m] = 1
    out["spread"] = spread.reshape(P, -1)
    level = np.zeros((P, len(LEVELS), T, P // 2), np.uint32)
    for n, h in enumerate(LEVELS):
        right = i[(i // h) % 2 == 1]
        level[:, n, :, :] = (((i[:, None] // h) % 2 == 0) & (i[:, None] // (2 * h) == right[None, :] // (2 * h)))[:, None, :]
    out["level"] = level.reshape(P, -1)
    f = (np.float32(1.0) / np.float32(10000.0) ** (np.arange(0, ROPE, 2, dtype=np.float32) / np.float32(ROPE))).astype(np.float32)
    a = np.outer(np.arange(S, dtype=np.float32), f).astype(np.float32)
    c, s = np.cos(a), np.sin(a)
    out["cos"] = np.concatenate([c, c], 1).reshape(T, P, ROPE).transpose(1, 0, 2).reshape(P, -1).astype(np.float32)
    out["sin"] = np.concatenate([-s, s], 1).reshape(T, P, ROPE).transpose(1, 0, 2).reshape(P, -1).astype(np.float32)
    return out


class Chain:

    def __init__(self, eng, sem):
        self.eng, self.sem, self.n = eng, sem, 0

    def tell(self, ins):
        self.n += 1
        ins.then_inc(self.sem, 1)

    def wait(self):
        self.eng.wait_ge(self.sem, self.n)

    def __call__(self, ins):
        self.tell(ins)
        self.wait()


class Sems:

    def __init__(self, nc, ctx, count):
        self.free = [ctx.enter_context(nc.semaphore(f"s{n}")) for n in range(count)]
        self.named = {}

    def __call__(self, name):
        if name not in self.named:
            self.named[name] = self.free[len(self.named)]
        return self.named[name]

    def clear(self, nc):
        for s in self.named.values():
            nc.sync.sem_clear(s)
        self.named = {}


def program(nc, w, out, layers=(0, 1, 2, 3)):
    ctx = ExitStack()
    with ctx:
        def sb(name, shape, dt=F32):
            return ctx.enter_context(nc.sbuf_tensor(name, shape, dt))

        def pb(name):
            return ctx.enter_context(nc.psum_tensor(name, [P, 512], F32))

        bank = [pb(f"bank{n}") for n in range(8)]
        sem = Sems(nc, ctx, 60)
        s_load = ctx.enter_context(nc.semaphore("loaded"))
        s_out = ctx.enter_context(nc.semaphore("stored"))

        x = sb("x", [P, B * T, D])
        cst = {}
        for name, width, dt in (("ident", P, F32), ("causal", P, F32), ("tri", P, F32), ("negmask", P, F32),
                                ("iota", KEEP, F32), ("before", E2 * E2, F32), ("spread", EP2 * P, F32),
                                ("level", len(LEVELS) * T * P // 2, U32), ("cos", T * ROPE, F32), ("sin", T * ROPE, F32)):
            cst[name] = sb("c_" + name, [P, width], dt)
        ident = cst["ident"]
        cos = cst["cos"][:].rearrange("p (t r) -> p t r", t=T)
        sin = cst["sin"][:].rearrange("p (t r) -> p t r", t=T)
        level = cst["level"][:].rearrange("p (l c) -> p l c", l=len(LEVELS))
        ones = sb("ones", [P, P])
        mhalf = sb("mhalf", [P, 8])

        xn = sb("xn", [P, T, D])
        xnT = sb("xnT", [P, S])
        stats = sb("stats", [P, T, 6])
        mv = sb("mv", [P, T, 2])
        ve = sb("ve", [P, T])
        rstd = sb("rstd", [P, T])

        w_lr = sb("w_lr", [P, 2])
        w_lrp = sb("w_lrp", [P, 1])
        fcw = sb("fcw", [P, H0])
        pjw = sb("pjw", [P, C0, D + 1])
        lnw = sb("lnw", [P, C0])
        lnb = sb("lnb", [P, C0])
        wsum = sb("wsum", [P, D])
        bias0 = sb("bias0", [P, D])
        small1 = sb("small1", [P, QL + KVL + ROPE + 3])
        wdq = sb("wdq", [QL, NH * QK])
        gq = sb("gq", [P, 1])
        wdkv = sb("wdkv", [P, 2 * NH * VH])
        wimp = sb("wimp", [P, 1])
        selk = sb("selk", [P, NH * QK])
        selv = sb("selv", [P, NH * VH])
        wink = sb("wink", [P, NH * QK])
        winv = sb("winv", [P, NH * VH])
        wpj = sb("wpj", [P, 4, D])
        win = sb("win", [P, M1, J1])
        f1 = sb("f1", [P, 4, R1])
        wo1 = sb("wo1", [P, D])
        wc1 = sb("wc1", [P, R1, D])
        b2o = sb("b2o", [M1, 1])
        b2b = sb("b2b", [M1, P])
        wout1 = sb("wout1", [M1, D])
        bias1 = sb("bias1", [P, D])
        wqkv2 = sb("wqkv2", [P, 3, D])
        gate2 = sb("gate2", [P, E2])
        bias2 = sb("bias2", [P, E2])
        up2 = sb("up2", [P, E2 * I2])
        down2 = sb("down2", [P, EP2, D])
        sup2 = sb("sup2", [P, SH2])
        sdown2 = sb("sdown2", [P, SP2, D])
        carry = sb("carry", [P, 2, E3])

        loads = []

        def load(dst, src):
            loads.append((dst, src))

        load(x[:], w["x"].rearrange("b (t p) d -> p (b t) d", p=P))
        for name in cst:
            load(cst[name][:], w["c_" + name])
        load(w_lr[:, 0:1], w["w_lhs"].rearrange("a b d -> d (a b)"))
        load(w_lr[:, 1:2], w["w_rhs"].rearrange("a b d -> d (a b)"))
        load(fcw[:], w["W_fcT"])
        load(pjw[:, :, 0:D], w["W_projT"].rearrange("(c p) d -> p c d", p=P))
        load(lnw[:], w["ln_wT"])
        load(lnb[:], w["ln_bT"])
        if 1 in layers:
            for a, n, name in ((0, QL, "w_cq"), (QL, KVL, "w_ckv"), (QL + KVL, ROPE, "w_krope"), (QL + KVL + ROPE, 3, "w_gate")):
                load(small1[:, a:a + n], w[name])
            load(wdq[:], w["w_dq"])
            load(gq[0:QL, :], w["g_qnorm"].rearrange("(p a) -> p a", a=1))
            load(gq[QL:P, :], w["g_kvnorm"].rearrange("(p a) -> p a", a=1))
            load(wdkv[QL:P, 0:NH * VH], w["w_dk_nope"])
            load(wdkv[QL:P, NH * VH:], w["w_dv"])
            load(wimp[:], w["w_imp"])
            load(selk[:], w["w_selk"])
            load(selv[:], w["w_selv"])
            load(wink[:], w["w_wink"])
            load(winv[:], w["w_winv"])
            load(wpj[:], w["w_proj"].rearrange("(c p) d -> p c d", p=P))
            load(win[:], w["Win_rep"])
            load(f1[:, 0, :], w["W1"].rearrange("m (j r) -> (m j) r", j=J1))
            load(f1[:, 1, :], w["b1"].rearrange("m (j r) -> (m j) r", j=J1))
            load(f1[:, 2, :], w["W2"].rearrange("m (j r) -> (m j) r", j=J1))
            load(f1[:, 3, 0:1], w["bin_rep"])
            load(wo1[:], w["Wout_rep"])
            load(b2o[:], w["b2"].rearrange("(p a) -> p a", a=1))
            load(wout1[:], w["Wout"])
            load(bias1[:], w["bout_rep"])
        if 2 in layers:
            for n, name in enumerate(("WQT", "WKT", "WVT")):
                load(wqkv2[:, n, :], w[name])
            load(gate2[:], w["gate2T"])
            load(bias2[:], w["bias2_rep"])
            load(up2[:], w["up2T"])
            load(down2[:], w["down2"].rearrange("(c p) d -> p c d", p=P))
            load(sup2[:], w["sup2T"])
            load(sdown2[:], w["sdown2T"].rearrange("(c p) d -> p c d", p=P))
        with ExitStack() as sx:
            absum = sx.enter_context(nc.sbuf_tensor("absum", [P, 2], F32))
            gamma = sx.enter_context(nc.sbuf_tensor("gamma", [P, 4], F32))
            tern = sx.enter_context(nc.sbuf_tensor("tern", [P, 3, H0], F32))
            lnb_b = sx.enter_context(nc.sbuf_tensor("lnb_b", [P, C0, P], F32))
            block = sx.enter_context(nc.Block())

            @block.sync
            def _(sp):
                for n, (dst, src) in enumerate(loads):
                    if n % 2 == 0:
                        sp.dma_start(dst, src).then_inc(s_load, 16)

            @block.scalar
            def _(act):
                for n, (dst, src) in enumerate(loads):
                    if n % 2 == 1:
                        act.dma_start(dst, src).then_inc(s_load, 16)

            @block.gpsimd
            def _(pool):
                pool.memset(ones[:], 1.0).then_inc(sem("ones"), 1)
                pool.memset(mhalf[:], -0.5)
                pool.memset(carry[:], 0.0)

            @block.vector
            def _(dve):
                link = Chain(dve, sem("dve_chain"))
                dve.wait_ge(s_load, 16 * len(loads))
                dve.tensor_reduce(absum[:, 0:1], fcw[:], X, ALU.add, apply_absolute_value=True)
                dve.tensor_reduce(absum[:, 1:2], pjw[:, :, 0:D], mybir.AxisListType.XY, ALU.add,
                                  apply_absolute_value=True).then_inc(sem("absum"), 1)
                link(dve.tensor_tensor(w_lrp[:], w_lr[:, 0:1], w_lr[:, 1:2], ALU.mult))
                dve.wait_ge(sem("abs_all"), 1)
                link(dve.tensor_scalar(gamma[:, 0:2], bank[0][:, 0:2], 1.0 / (H0 * D), 1e-6, ALU.mult, ALU.add))
                link(dve.reciprocal(gamma[:, 2:4], gamma[:, 0:2]))
                for n, (wt, view) in enumerate(((fcw[:], tern[:, 0, :]), (pjw[:, :, 0:D], tern[:, 0, :].rearrange("p (c d) -> p c d", c=C0)))):
                    up = tern[:, 1, :] if n == 0 else tern[:, 1, :].rearrange("p (c d) -> p c d", c=C0)
                    link(dve.tensor_scalar(view, wt, gamma[:, 2 + n:3 + n], None, ALU.mult))
                    link(dve.tensor_scalar(up, view, 0.5, None, ALU.is_gt))
                    link(dve.tensor_scalar(view, view, -0.5, None, ALU.is_lt))
                    link(dve.tensor_tensor(wt, up, view, ALU.subtract))
                for c in range(C0):
                    link(dve.tensor_scalar(lnb_b[:, c, :], ident[:], 0.0, lnb[:, c:c + 1], ALU.mult, ALU.add))
                dve.sem_inc(sem("lnb_ready"), 1)
                dve.wait_ge(sem("bias0"), 1)
                dve.tensor_copy(bias0[:], bank[1][:, 0:D])
                for c in range(C0):
                    link(dve.tensor_scalar(pjw[:, c, 0:D], pjw[:, c, 0:D], lnw[:, c:c + 1], None, ALU.mult))
                link(dve.memset(pjw[:, :, D:D + 1], 1.0))
                dve.sem_inc(sem("pjw_ready"), 1)
                dve.wait_ge(sem("wsum"), 1)
                dve.tensor_copy(wsum[:], bank[2][:, 0:D])
                if 1 in layers:
                    dve.tensor_scalar(wdq[:], wdq[:], gq[0:QL, :], None, ALU.mult)
                    dve.tensor_scalar(wdkv[QL:P, :], wdkv[QL:P, :], gq[QL:P, :], None, ALU.mult)
                    link(dve.scalar_tensor_tensor(f1[:, 1, :], f1[:, 0, :], f1[:, 3, 0:1], f1[:, 1, :], ALU.mult, ALU.add))
                    for r in range(R1):
                        dve.tensor_scalar(wc1[:, r, :], wo1[:], f1[:, 2, r:r + 1], None, ALU.mult)
                    link(dve.tensor_scalar(b2b[:], ident[0:M1, :], 0.0, b2o[:], ALU.mult, ALU.add))
                    dve.sem_inc(sem("b2_ready"), 1)
                    dve.wait_ge(sem("bias1"), 1)
                    dve.tensor_tensor(bias1[:], bias1[:], bank[3][:, 0:D], ALU.add)

            @block.tensor
            def _(pe):
                pe.wait_ge(sem("ones"), 1)
                pe.wait_ge(sem("absum"), 1)
                pe.matmul(bank[0][:, 0:2], ones[:], absum[:], start=True, stop=True).then_inc(sem("abs_all"), 1)
                pe.wait_ge(sem("lnb_ready"), 1)
                for c in range(C0):
                    mm = pe.matmul(bank[1][:, 0:D], lnb_b[:, c, :], pjw[:, c, 0:D], start=c == 0, stop=c == C0 - 1)
                mm.then_inc(sem("bias0"), 1)
                pe.wait_ge(sem("pjw_ready"), 1)
                for c in range(C0):
                    mm = pe.matmul(bank[2][:, 0:D], ones[:], pjw[:, c, 0:D], start=c == 0, stop=c == C0 - 1)
                mm.then_inc(sem("wsum"), 1)
                if 1 in layers:
                    pe.wait_ge(sem("b2_ready"), 1)
                    pe.matmul(bank[3][:, 0:D], b2b[:], wout1[:], start=True, stop=True).then_inc(sem("bias1"), 1)

        nc.all_engine_barrier()
        sem.clear(nc)
        nc.all_engine_barrier()

        def norm_dve(dve, link, xb):
            for t in range(T):
                link.tell(dve.bn_stats(stats[:, t, :], xb[:, t, :]))
            link.wait()
            for t in range(T):
                link.tell(dve.bn_aggr(mv[:, t, :], stats[:, t, :]))
            link.wait()
            dve.tensor_scalar(ve[:], mv[:, :, 1], LN_EPS, None, ALU.add).then_inc(sem("var"), 1)
            dve.wait_ge(sem("rstd"), 1)
            for t in range(T):
                dve.tensor_scalar(xn[:, t, :], xb[:, t, :], mv[:, t, 0:1], rstd[:, t:t + 1],
                                  ALU.subtract, ALU.mult).then_inc(sem("xn"), 1)

        def norm_pool(pool):
            pool.wait_ge(sem("var"), 1)
            pool.tensor_tensor(rstd[:], ve[:], mhalf[:, 0:T], ALU.pow).then_inc(sem("rstd"), 1)

        def norm_pe(pe, ps):
            for t in range(T):
                pe.wait_ge(sem("xn"), t + 1)
                pe.transpose(ps[:, t * P:(t + 1) * P], xn[:, t, :], ident[:]).then_inc(sem("xnT_ps"), 1)

        def norm_act(act, ps):
            act.wait_ge(sem("xnT_ps"), T)
            act.activation(xnT[:], ps[:, 0:S], ACT.Copy).then_inc(sem("xnT"), 1)

        def layer0(b):
            with ExitStack() as lx:
                def lsb(name, shape, dt=F32):
                    return lx.enter_context(nc.sbuf_tensor(name, shape, dt))
                xwT = lsb("xwT", [P, S])
                nmax = lsb("nmax", [P, T])
                rsum = lsb("rsum", [P, T])
                rinv = lsb("rinv", [P, T])
                prob = lsb("prob", [P, T, S])
                probT = lsb("probT", [P, T, S])
                g = lsb("g", [P, C0, S])
                g2 = lsb("g2", [P, C0, S])
                x1 = lsb("x1", [P, T, D])
                y0 = lsb("y0", [P, T, D])
                s0 = lsb("s0", [P, T, 6])
                block = lx.enter_context(nc.Block())
                psX, psS, psT, psO, psH, psY = bank[0], bank[1], bank[2], bank[3], bank[4:6], bank[6:8]
                xb = x[:, bass.ds(b * T, T), :]

                @block.vector
                def _(dve):
                    link = Chain(dve, sem("dve_chain"))
                    norm_dve(dve, link, xb)
                    dve.wait_ge(sem("xnT"), 1)
                    dve.tensor_scalar(xwT[:], xnT[:], w_lrp[:], None, ALU.mult).then_inc(sem("xwT"), 1)
                    dve.wait_ge(sem("scores"), 1)
                    dve.tensor_reduce(nmax[:], psS[:].rearrange("p (t k) -> p t k", t=T), X, ALU.max, negate=True).then_inc(sem("nmax"), 1)
                    dve.wait_ge(sem("gelu"), C0)
                    dve.tensor_tensor(g2[:], g[:], g[:], ALU.mult).then_inc(sem("g2"), 1)
                    dve.wait_ge(sem("probT_ps"), 1)
                    dve.tensor_copy(probT[:], psT[:].rearrange("p (t k) -> p t k", t=T)).then_inc(sem("probT"), 1)
                    link(dve.reciprocal(rinv[:], rsum[:]))
                    dve.wait_ge(sem("pv"), T)
                    for t in range(T):
                        link(dve.scalar_tensor_tensor(x1[:, t, :], psO[:, t * D:(t + 1) * D], rinv[:, t:t + 1], xb[:, t, :], ALU.mult, ALU.add))
                    dve.wait_ge(sem("ffn"), T)
                    for t in range(T):
                        link(dve.tensor_scalar(s0[:, t, 0:2], psY[t][:, D:D + 2], 1.0 / H0, None, ALU.mult))
                    link(dve.tensor_tensor(s0[:, :, 2:3], s0[:, :, 0:1], s0[:, :, 0:1], ALU.mult))
                    link(dve.scalar_tensor_tensor(s0[:, :, 3:4], s0[:, :, 1:2], LN_EPS, s0[:, :, 2:3], ALU.add, ALU.subtract))
                    link(dve.tensor_scalar(s0[:, :, 4:5], s0[:, :, 0:1], -1.0, None, ALU.mult))
                    dve.sem_inc(sem("var2"), 1)
                    for t in range(T):
                        link(dve.scalar_tensor_tensor(y0[:, t, :], wsum[:], s0[:, t, 4:5], psY[t][:, 0:D], ALU.mult, ALU.add))
                    dve.wait_ge(sem("rstd2"), 1)
                    for t in range(T):
                        link(dve.scalar_tensor_tensor(y0[:, t, :], y0[:, t, :], s0[:, t, 5:6], x1[:, t, :], ALU.mult, ALU.add))
                        link(dve.tensor_tensor(xb[:, t, :], y0[:, t, :], bias0[:], ALU.add))

                @block.gpsimd
                def _(pool):
                    norm_pool(pool)
                    pool.wait_ge(sem("var2"), 1)
                    pool.tensor_tensor(s0[:, :, 5], s0[:, :, 3], mhalf[:, 0:T], ALU.pow).then_inc(sem("rstd2"), 1)

                @block.scalar
                def _(act):
                    norm_act(act, psX)
                    act.wait_ge(sem("nmax"), 1)
                    for t in range(T):
                        act.activation(prob[:, t, :], psS[:, t * S:(t + 1) * S], ACT.Exp, bias=nmax[:, t:t + 1],
                                       accum_out=rsum[:, t:t + 1]).then_inc(sem("prob"), 1)
                    for c in range(0, C0, 2):
                        act.wait_ge(sem("hidden"), c + 2)
                        act.activation(g[:, c:c + 2, :], psH[c // 2][:].rearrange("p (c k) -> p c k", c=2), ACT.Gelu).then_inc(sem("gelu"), 2)

                @block.tensor
                def _(pe):
                    norm_pe(pe, psX)
                    pe.wait_ge(sem("xnT"), 1)
                    pe.wait_ge(sem("xwT"), 1)
                    for t in range(T):
                        mm = pe.matmul(psS[:, t * S:(t + 1) * S], xwT[:, t * P:(t + 1) * P], xnT[:], start=True, stop=True)
                    mm.then_inc(sem("scores"), 1)
                    for c in range(C0):
                        pe.matmul(psH[c // 2][:, (c % 2) * S:(c % 2 + 1) * S], fcw[:, c * P:(c + 1) * P], xnT[:],
                                  start=True, stop=True).then_inc(sem("hidden"), 1)
                    pe.wait_ge(sem("prob"), T)
                    for t in range(T):
                        for k in range(T):
                            mm = pe.transpose(psT[:, k * S + t * P:k * S + (t + 1) * P], prob[:, t, k * P:(k + 1) * P], ident[:])
                    mm.then_inc(sem("probT_ps"), 1)
                    pe.wait_ge(sem("probT"), 1)
                    for t in range(T):
                        for k in range(T):
                            mm = pe.matmul(psO[:, t * D:(t + 1) * D], probT[:, k, t * P:(t + 1) * P], xn[:, k, :], start=k == 0, stop=k == T - 1)
                        mm.then_inc(sem("pv"), 1)
                    for t in range(T):
                        for c in range(C0):
                            pe.matmul(psY[t][:, 0:D + 1], g[:, c, t * P:(t + 1) * P], pjw[:, c, :], start=c == 0, stop=c == C0 - 1)
                        if t == 0:
                            pe.wait_ge(sem("g2"), 1)
                        for c in range(C0):
                            mm = pe.matmul(psY[t][:, D + 1:D + 2], g2[:, c, t * P:(t + 1) * P], ones[:, 0:1], start=c == 0, stop=c == C0 - 1)
                        mm.then_inc(sem("ffn"), 1)
            nc.all_engine_barrier()
            sem.clear(nc)
            nc.all_engine_barrier()

        def rank_dve(dve, link, v, n, gt, eq, rank):
            other = v.unsqueeze(2).broadcast_to([P, T, n, n])
            own = v.unsqueeze(3).broadcast_to([P, T, n, n])
            before = cst["before"][:].rearrange("p (a b) -> p a b", a=E2)[:, 0:n, 0:n]
            for t in range(T):
                link.tell(dve.tensor_tensor(gt[:, t], other[:, t], own[:, t], ALU.is_gt))
                link(dve.tensor_tensor(eq[:, t], other[:, t], own[:, t], ALU.is_equal))
                link(dve.tensor_tensor(eq[:, t], eq[:, t], before, ALU.mult))
                link(dve.tensor_tensor(gt[:, t], gt[:, t], eq[:, t], ALU.add))
                link(dve.tensor_reduce(rank[:, t, :], gt[:, t], X, ALU.add))

        def layer2(b):
            with ExitStack() as lx:
                def lsb(name, shape, dt=F32):
                    return lx.enter_context(nc.sbuf_tensor(name, shape, dt))
                SCALE = float(D) ** -0.5
                W = P + S
                qk = lsb("qk", [P, 2, S])
                v2 = lsb("v2", [P, T, D])
                sm = lsb("sm", [P, W])
                zero = lsb("zero", [P, W])
                nmax = lsb("nmax2", [P, T])
                rsum = lsb("rsum2", [P, T])
                rinv = lsb("rinv2", [P, T])
                alive = lsb("alive", [P, T])
                prob = lsb("prob2", [P, W])
                probT = lsb("probT2", [P, W])
                x1 = lsb("x12", [P, T, D])
                r = {n: lsb("r_" + n, [P, T, E2]) for n in ("e", "s", "sc", "rank", "m", "c")}
                pair = lsb("pair", [P, T, GR2, 6])
                gs = lsb("gs", [P, T, GR2])
                grank = lsb("grank", [P, T, GR2])
                gt = lsb("gt", [P, T, E2, E2])
                eq = lsb("eq", [P, T, E2, E2])
                ggt = lsb("ggt", [P, T, GR2, GR2])
                geq = lsb("geq", [P, T, GR2, GR2])
                csum = lsb("csum", [P, T])
                cT = lsb("cT", [E2, S])
                hr = lsb("hr", [P, EP2 + SP2, S])
                hc = lsb("hc", [P, EP2 + SP2, S])
                h2 = lsb("h2", [P, EP2 + SP2, S])
                block = lx.enter_context(nc.Block())
                psX, psQ, psV, psS = bank[0], bank[1], bank[2], bank[3]
                psT, psO = bank[1], bank[2]
                psG = bank[0]
                psU, psC, psD = bank[4:6], bank[6], bank[7]
                xb = x[:, bass.ds(b * T, T), :]
                NT2 = EP2 + SP2

                @block.vector
                def _(dve):
                    link = Chain(dve, sem("dve_chain"))
                    norm_dve(dve, link, xb)
                    dve.wait_ge(sem("values_ps"), 1)
                    dve.tensor_copy(v2[:], psV[:, 0:T * D].rearrange("p (t d) -> p t d", t=T)).then_inc(sem("values"), 1)
                    dve.wait_ge(sem("sig_e"), 1)
                    link(dve.tensor_scalar(r["e"][:], r["e"][:], 1.0, None, ALU.add))
                    link(dve.reciprocal(r["s"][:], r["e"][:]))
                    link(dve.tensor_tensor(r["sc"][:], r["s"][:], bias2[:].unsqueeze(1).broadcast_to([P, T, E2]), ALU.add))
                    sg = r["sc"][:].rearrange("p t (g k) -> p t g k", g=GR2)
                    link.tell(dve.tensor_tensor(pair[:, :, :, 0:3], sg[:, :, :, 0:3], sg[:, :, :, 1:4], ALU.add))
                    link.tell(dve.tensor_tensor(pair[:, :, :, 3:5], sg[:, :, :, 0:2], sg[:, :, :, 2:4], ALU.add))
                    link(dve.tensor_tensor(pair[:, :, :, 5:6], sg[:, :, :, 0:1], sg[:, :, :, 3:4], ALU.add))
                    link(dve.tensor_reduce(gs[:], pair[:], X, ALU.max))
                    rank_dve(dve, link, gs[:], GR2, ggt, geq, grank)
                    link(dve.tensor_scalar(grank[:], grank[:], 2.0, None, ALU.is_lt))
                    link(dve.tensor_tensor(r["m"][:].rearrange("p t (g k) -> p t g k", g=GR2), sg,
                                           grank[:].unsqueeze(3).broadcast_to([P, T, GR2, E2 // GR2]), ALU.mult))
                    dve.wait_ge(sem("scores"), 1)
                    for a, n in ((0, P), (2 * P, P)):
                        link.tell(dve.tensor_tensor(sm[:, a:a + n], psS[:, a:a + n], cst["causal"][:], ALU.mult))
                    link(dve.tensor_copy(sm[:, P:2 * P], psS[:, P:2 * P]))
                    link(dve.tensor_scalar(zero[:], sm[:], 0.0, -3e38, ALU.is_equal, ALU.mult))
                    link(dve.tensor_tensor(sm[:], zero[:], sm[:], ALU.add))
                    link.tell(dve.tensor_reduce(nmax[:, 0:1], sm[:, 0:P], X, ALU.max, negate=True))
                    link(dve.tensor_reduce(nmax[:, 1:2], sm[:, P:W], X, ALU.max, negate=True))
                    link(dve.tensor_scalar(alive[:], nmax[:], 1e38, None, ALU.is_lt))
                    dve.tensor_scalar(nmax[:], nmax[:], SCALE, None, ALU.mult).then_inc(sem("nmax"), 1)
                    rank_dve(dve, link, r["m"][:], E2, gt, eq, r["rank"])
                    link(dve.tensor_scalar(r["rank"][:], r["rank"][:], float(K2), None, ALU.is_lt))
                    link(dve.tensor_tensor(r["c"][:], r["rank"][:], r["s"][:], ALU.mult))
                    link(dve.tensor_reduce(csum[:], r["c"][:], X, ALU.add))
                    link(dve.tensor_scalar(csum[:], csum[:], 1e-20, None, ALU.add))
                    link(dve.reciprocal(csum[:], csum[:]))
                    for t in range(T):
                        dve.tensor_scalar(r["c"][:, t, :], r["c"][:, t, :], csum[:, t:t + 1], ROUTED_SCALE, ALU.mult, ALU.mult).then_inc(sem("combine"), 1)
                    dve.wait_ge(sem("cT_ps"), 1)
                    dve.tensor_copy(cT[:], psG[0:E2, 0:S]).then_inc(sem("cT"), 1)
                    dve.wait_ge(sem("probT_ps"), 1)
                    dve.tensor_copy(probT[:], psT[:, 0:W]).then_inc(sem("probT"), 1)
                    for c in range(EP2):
                        dve.wait_ge(sem("relu"), c + 1)
                        dve.wait_ge(sem("spread"), c + 1)
                        dve.tensor_tensor(hc[:, c, :], hr[:, c, :], psC[:, 0:S], ALU.mult).then_inc(sem("weighted"), 1)
                    link(dve.tensor_tensor(rinv[:], rsum[:], alive[:], ALU.mult))
                    link(dve.reciprocal(rinv[:], rinv[:]))
                    link(dve.tensor_tensor(rinv[:], rinv[:], alive[:], ALU.mult))
                    dve.wait_ge(sem("pv"), 1)
                    for t in range(T):
                        link(dve.scalar_tensor_tensor(x1[:, t, :], psO[:, t * D:(t + 1) * D], rinv[:, t:t + 1], xb[:, t, :], ALU.mult, ALU.add))
                    dve.wait_ge(sem("ffn"), 1)
                    dve.tensor_tensor(xb, x1[:], psD[:, 0:T * D].rearrange("p (t d) -> p t d", t=T), ALU.add)

                @block.gpsimd
                def _(pool):
                    norm_pool(pool)
                    for c in list(range(EP2, NT2)) + list(range(EP2)):
                        if c < EP2:
                            pool.wait_ge(sem("weighted"), c + 1)
                            pool.tensor_tensor(h2[:, c, :], hr[:, c, :], hc[:, c, :], ALU.mult).then_inc(sem("squared"), 1)
                        else:
                            pool.wait_ge(sem("relu_shared"), c - EP2 + 1)
                            pool.tensor_tensor(h2[:, c, :], hr[:, c, :], hr[:, c, :], ALU.mult).then_inc(sem("squared"), 1)

                @block.scalar
                def _(act):
                    norm_act(act, psX)
                    act.wait_ge(sem("qk_ps"), 1)
                    act.activation(qk[:], psQ[:].rearrange("p (a k) -> p a k", a=2), ACT.Copy).then_inc(sem("qk"), 1)
                    act.wait_ge(sem("logits"), 1)
                    act.activation(r["e"][:], psG[:, 0:T * E2].rearrange("p (t e) -> p t e", t=T), ACT.Exp, scale=-1.0).then_inc(sem("sig_e"), 1)
                    for c in list(range(EP2, NT2)) + list(range(EP2)):
                        n = (c - EP2) % NT2
                        act.wait_ge(sem("up"), n + 1)
                        act.activation(hr[:, c, :], psU[n % 2][:, 0:S], ACT.Relu).then_inc(sem("relu" if c < EP2 else "relu_shared"), 1)
                        if n == 2:
                            act.wait_ge(sem("nmax"), 1)
                            for t, (a, e) in enumerate(((0, P), (P, W))):
                                act.activation(prob[:, a:e], sm[:, a:e], ACT.Exp, bias=nmax[:, t:t + 1], scale=SCALE,
                                               accum_out=rsum[:, t:t + 1]).then_inc(sem("prob"), 1)

                @block.tensor
                def _(pe):
                    norm_pe(pe, psX)
                    pe.wait_ge(sem("xnT"), 1)
                    for n in range(2):
                        mm = pe.matmul(psQ[:, n * S:(n + 1) * S], wqkv2[:, n, :], xnT[:], start=True, stop=True)
                    mm.then_inc(sem("qk_ps"), 1)
                    for t in range(T):
                        mm = pe.matmul(psG[:, t * E2:(t + 1) * E2], xnT[:, t * P:(t + 1) * P], gate2[:], start=True, stop=True)
                    mm.then_inc(sem("logits"), 1)
                    for t in range(T):
                        mm = pe.matmul(psV[:, t * D:(t + 1) * D], xnT[:, t * P:(t + 1) * P], wqkv2[:, 2, :], start=True, stop=True)
                    mm.then_inc(sem("values_ps"), 1)
                    pe.wait_ge(sem("qk"), 1)
                    pe.matmul(psS[:, 0:P], qk[:, 0, 0:P], qk[:, 1, 0:P], start=True, stop=True)
                    pe.matmul(psS[:, P:W], qk[:, 0, P:S], qk[:, 1, :], start=True, stop=True).then_inc(sem("scores"), 1)

                    def up(c):
                        n = (c - EP2) % NT2
                        if n >= 2:
                            pe.wait_ge(sem("relu_shared"), min(n - 1, SP2))
                            if n - 1 > SP2:
                                pe.wait_ge(sem("relu"), n - 1 - SP2)
                        wt = up2[:, c * P:(c + 1) * P] if c < EP2 else sup2[:, (c - EP2) * P:(c - EP2 + 1) * P]
                        pe.matmul(psU[n % 2][:, 0:S], wt, xnT[:], start=True, stop=True).then_inc(sem("up"), 1)
                    for c in range(EP2, NT2):
                        up(c)
                    for c in range(2):
                        up(c)
                    pe.wait_ge(sem("prob"), T)
                    pe.wait_ge(sem("values"), 1)
                    for n in range(W // P):
                        mm = pe.transpose(psT[:, n * P:(n + 1) * P], prob[:, n * P:(n + 1) * P], ident[:])
                    mm.then_inc(sem("probT_ps"), 1)
                    pe.wait_ge(sem("combine"), T)
                    for t in range(T):
                        mm = pe.transpose(psG[0:E2, t * P:(t + 1) * P], r["c"][:, t, :], ident[:])
                    mm.then_inc(sem("cT_ps"), 1)
                    pe.wait_ge(sem("probT"), 1)
                    pe.matmul(psO[:, 0:D], probT[:, 0:P], v2[:, 0, :], start=True, stop=True)
                    pe.matmul(psO[:, D:2 * D], probT[:, P:2 * P], v2[:, 0, :], start=True, stop=False)
                    pe.matmul(psO[:, D:2 * D], probT[:, 2 * P:W], v2[:, 1, :], start=False, stop=True).then_inc(sem("pv"), 1)
                    pe.wait_ge(sem("cT"), 1)
                    for c in range(EP2):
                        if c + 2 < EP2:
                            up(c + 2)
                        if c >= 1:
                            pe.wait_ge(sem("weighted"), c)
                        pe.matmul(psC[:, 0:S], spread(c), cT[:], start=True, stop=True).then_inc(sem("spread"), 1)
                    pe.wait_ge(sem("squared"), NT2)
                    for t in range(T):
                        for c in range(NT2):
                            wt = down2[:, c, :] if c < EP2 else sdown2[:, c - EP2, :]
                            mm = pe.matmul(psD[:, t * D:(t + 1) * D], h2[:, c, t * P:(t + 1) * P], wt, start=c == 0, stop=c == NT2 - 1)
                    mm.then_inc(sem("ffn"), 1)
            nc.all_engine_barrier()
            sem.clear(nc)
            nc.all_engine_barrier()

        def spread(c):
            return cst["spread"][0:E2, c * P:(c + 1) * P]

        def layer3(b, wqkvg3, bg3, wo3, gate3, gb3, w13, b13, w23, b23):
            with ExitStack() as lx:
                def lsb(name, shape, dt=F32):
                    return lx.enter_context(nc.sbuf_tensor(name, shape, dt))
                r = {n: lsb("t_" + n, [P, T, E3]) for n in ("l", "e", "p", "rank", "w")}
                oh = lsb("oh", [P, 2, T, E3])
                pos = lsb("pos", [P, 2, T, E3])
                tmx = lsb("tmx", [P, T])
                tsum = lsb("tsum", [P, T])
                gt = lsb("gt3", [P, T, E3, E3])
                eq = lsb("eq3", [P, T, E3, E3])
                wT = lsb("wT", [E3, S])
                hm = lsb("hm", [P, 2, FC3, S])
                acc = lsb("acc", [P, T, D])
                v3 = lsb("v3", [P, T, NH3 * DK3])
                ga = lsb("ga", [P, PAIRS, S])
                kk = lsb("kk", [P, 2, S])
                qq = lsb("qq", [P, 2, S])
                ee = lsb("ee", [P, 2, S // 2])
                e2 = lsb("e2", [P, 2, S // 2])
                pT = lsb("pT", [P, 2, 2, T, P])
                pX = lsb("pX", [P, 2, 2, P])
                og = lsb("og", [P, 2, T, P])
                oT = lsb("oT", [P, 2, S])
                block = lx.enter_context(nc.Block())
                psX, psA, psL, psV, psO, psH, psY = bank[0], bank[1], bank[2:4], bank[4], bank[5], bank[6], bank[7]
                xb = x[:, bass.ds(b * T, T), :]
                NL = len(LEVELS)

                def halves(a, h):
                    return a.rearrange("p (n two h) -> p n two h", two=2, h=h)

                @block.vector
                def _(dve):
                    link = Chain(dve, sem("dve_chain"))
                    norm_dve(dve, link, xb)
                    dve.wait_ge(sem("logits"), 1)
                    link(dve.tensor_tensor(r["l"][:], psX[:, 0:T * E3].rearrange("p (t e) -> p t e", t=T),
                                           gb3[:].unsqueeze(1).broadcast_to([P, T, E3]), ALU.add))
                    link(dve.tensor_reduce(tmx[:], r["l"][:], X, ALU.max))
                    dve.tensor_tensor(r["l"][:], r["l"][:], tmx[:].unsqueeze(2).broadcast_to([P, T, E3]), ALU.subtract).then_inc(sem("shifted"), 1)
                    dve.wait_ge(sem("exps"), 1)
                    link(dve.tensor_reduce(tsum[:], r["e"][:], X, ALU.add))
                    link(dve.reciprocal(tsum[:], tsum[:]))
                    link(dve.tensor_tensor(r["p"][:], r["e"][:], tsum[:].unsqueeze(2).broadcast_to([P, T, E3]), ALU.mult))
                    rank_dve(dve, link, r["p"][:], E3, gt, eq, r["rank"])
                    for c in range(2):
                        dve.tensor_scalar(oh[:, c], r["rank"][:], float(c), None, ALU.is_equal).then_inc(sem("onehot"), 1)
                    dve.wait_ge(sem("places"), 1)
                    places = psX[:, 64:64 + 2 * T * E3].rearrange("p (c t e) -> p c t e", c=2, t=T)
                    link(dve.tensor_tensor(pos[:], places, carry[:].unsqueeze(2).broadcast_to([P, 2, T, E3]), ALU.add))
                    counts = psX[:, 128:128 + 2 * E3].rearrange("p (c e) -> p c e", c=2)
                    link.tell(dve.tensor_tensor(carry[:], carry[:], counts, ALU.add))
                    link(dve.tensor_scalar(pos[:], pos[:], float(CAP3), None, ALU.is_le))
                    link(dve.tensor_tensor(pos[:], pos[:], oh[:], ALU.mult))
                    link(dve.tensor_tensor(pos[:, 0], pos[:, 0], pos[:, 1], ALU.add))
                    dve.tensor_tensor(r["w"][:], pos[:, 0], r["p"][:], ALU.mult).then_inc(sem("weights"), 1)
                    dve.wait_ge(sem("wT_ps"), 1)
                    dve.tensor_copy(wT[:], psX[0:E3, 256:256 + S]).then_inc(sem("wT"), 1)
                    dve.wait_ge(sem("bias_ps"), 1)
                    link(dve.tensor_tensor(acc[:], psY[:, 0:T * D].rearrange("p (t d) -> p t d", t=T), xb, ALU.add))

                    def expert(e):
                        dve.wait_ge(sem("expert_ps"), e + 1)
                        for t in range(T):
                            link.tell(dve.scalar_tensor_tensor(acc[:, t, :], psY[:, t * D:(t + 1) * D], r["w"][:, t, e:e + 1], acc[:, t, :], ALU.mult, ALU.add))
                        link.wait()
                        dve.sem_inc(sem("expert_added"), 1)

                    for j in range(PAIRS):
                        m = j % 2
                        dve.wait_ge(sem("qk_ps"), j + 1)
                        if j >= 2:
                            dve.wait_ge(sem("scored"), (j - 1) * (NL + 2))
                            dve.wait_ge(sem("pv"), j - 1)
                        link.tell(dve.tensor_copy(qq[:, m, :], psA[:, 0:S]))
                        link.tell(dve.tensor_copy(kk[:, m, :], psA[:, S:2 * S]))
                        link.wait()
                        dve.sem_inc(sem("qk"), 1)
                        dve.wait_ge(sem("gates"), PAIRS)
                        dve.wait_ge(sem("scored"), j * (NL + 2) + 1)
                        for a in range(2):
                            dve.tensor_tensor(pT[:, m, a], psL[a][:, 0:S].rearrange("p (t q) -> p t q", t=T),
                                              ident[:].unsqueeze(1).broadcast_to([P, T, P]), ALU.mult)
                        dve.tensor_tensor(qq[:, m, :], qq[:, m, :], ga[:, j, :], ALU.mult).then_inc(sem("levelled"), 1)
                        edge = ga[:, j, :]
                        for n, h in enumerate(LEVELS + [P]):
                            dve.wait_ge(sem("levelled"), j * (NL + 2) + n + 1)
                            dve.wait_ge(sem("scored"), j * (NL + 2) + n + 2)
                            if h < P:
                                mask = level[:, n, :].rearrange("p (c h) -> p c h", h=h)
                                for a in range(2):
                                    right = halves(pT[:, m, a].rearrange("p t q -> p (t q)"), h)[:, :, 1, :]
                                    dve.copy_predicated(right, mask, psL[a][:, 0:S // 2].rearrange("p (c h) -> p c h", h=h))
                                q2, k2, ed = halves(qq[:, m, :], h), halves(kk[:, m, :], h), edge.rearrange("p (n two) -> p n two", two=2)
                                dve.tensor_tensor(q2[:, :, 1, :], q2[:, :, 1, :], ed[:, :, 0:1].broadcast_to([P, S // (2 * h), h]), ALU.mult)
                                dve.tensor_tensor(k2[:, :, 0, :], k2[:, :, 0, :], ed[:, :, 1:2].broadcast_to([P, S // (2 * h), h]), ALU.mult)
                                nxt = (ee if n % 2 == 0 else e2)[:, m, 0:S // (2 * h)]
                                dve.tensor_tensor(nxt, ed[:, :, 0], ed[:, :, 1], ALU.mult).then_inc(sem("levelled"), 1)
                                edge = nxt
                            else:
                                dve.tensor_copy(pX[:, m, 0], psL[0][:, 0:P])
                                dve.tensor_copy(pX[:, m, 1], psL[1][:, 0:P]).then_inc(sem("levelled"), 1)
                        dve.wait_ge(sem("pv"), j + 1)
                        link(dve.tensor_copy(og[:, m], psO[:, 0:T * P].rearrange("p (t c) -> p t c", t=T)))
                        dve.sem_inc(sem("og"), 1)
                        expert(j)
                    dve.wait_ge(sem("attn"), 1)
                    dve.tensor_tensor(xb, acc[:], psV[:, 0:T * D].rearrange("p (t d) -> p t d", t=T), ALU.add)

                @block.gpsimd
                def _(pool):
                    norm_pool(pool)

                @block.scalar
                def _(act):
                    norm_act(act, psX)
                    act.wait_ge(sem("shifted"), 1)
                    act.activation(r["e"][:], r["l"][:], ACT.Exp).then_inc(sem("exps"), 1)
                    for n in range(4):
                        act.wait_ge(sem("values_ps"), n + 1)
                        act.activation(v3[:, n // 2, (n % 2) * 512:(n % 2 + 1) * 512], bank[4 + n][:], ACT.Copy).then_inc(sem("values"), 1)
                    for j in range(PAIRS):
                        act.wait_ge(sem("gate_ps"), j + 1)
                        act.activation(ga[:, j, :], bank[2 + j % 2][:, 0:S], ACT.Sigmoid, bias=bg3[:, j:j + 1]).then_inc(sem("gates"), 1)
                    for e in range(E3):
                        if e >= 2:
                            act.wait_ge(sem("expert_ps"), e - 1)
                        for c in range(FC3):
                            act.wait_ge(sem("hidden_ps"), e * FC3 + c + 1)
                            act.activation(hm[:, e % 2, c, :], psH[:, 0:S], ACT.Relu, bias=b13[:, e, c:c + 1]).then_inc(sem("hidden"), 1)
                        act.wait_ge(sem("oT_ps"), e + 1)
                        act.activation(oT[:, e % 2, :], psO[:, 256:256 + S], ACT.Copy).then_inc(sem("oT"), 1)

                @block.tensor
                def _(pe):
                    norm_pe(pe, psX)
                    pe.wait_ge(sem("xnT"), 1)
                    for t in range(T):
                        mm = pe.matmul(psX[:, t * E3:(t + 1) * E3], xnT[:, t * P:(t + 1) * P], gate3[:], start=True, stop=True)
                    mm.then_inc(sem("logits"), 1)
                    for n in range(4):
                        pe.matmul(bank[4 + n][:], xnT[:, (n // 2) * P:(n // 2 + 1) * P], wqkvg3[:, 2, (n % 2) * 512:(n % 2 + 1) * 512],
                                  start=True, stop=True).then_inc(sem("values_ps"), 1)
                    for j in range(PAIRS):
                        if j >= 2:
                            pe.wait_ge(sem("gates"), j - 1)
                        pe.matmul(bank[2 + j % 2][:, 0:S], wqkvg3[:, 3, j * P:(j + 1) * P], xnT[:], start=True, stop=True).then_inc(sem("gate_ps"), 1)
                    pe.wait_ge(sem("onehot"), 2)
                    for c in range(2):
                        a = 64 + c * T * E3
                        for t in range(T):
                            pe.matmul(psX[:, a + t * E3:a + (t + 1) * E3], cst["tri"][:], oh[:, c, t, :], start=True, stop=t == 0)
                            if t:
                                pe.matmul(psX[:, a + t * E3:a + (t + 1) * E3], ones[:], oh[:, c, 0, :], start=False, stop=True)
                        for t in range(T):
                            mm = pe.matmul(psX[:, 128 + c * E3:128 + (c + 1) * E3], ones[:], oh[:, c, t, :], start=t == 0, stop=t == T - 1)
                    mm.then_inc(sem("places"), 1)
                    pe.wait_ge(sem("weights"), 1)
                    for t in range(T):
                        mm = pe.transpose(psX[0:E3, 256 + t * P:256 + (t + 1) * P], r["w"][:, t, :], ident[:])
                    mm.then_inc(sem("wT_ps"), 1)
                    pe.wait_ge(sem("wT"), 1)
                    pe.wait_ge(sem("values"), 4)
                    for t in range(T):
                        mm = pe.matmul(psY[:, t * D:(t + 1) * D], wT[:, t * P:(t + 1) * P], b23[:], start=True, stop=True)
                    mm.then_inc(sem("bias_ps"), 1)
                    pe.wait_ge(sem("gates"), PAIRS)

                    def up(e, c):
                        if e * FC3 + c >= 1:
                            pe.wait_ge(sem("hidden"), e * FC3 + c)
                        pe.matmul(psH[:, 0:S], w13[:, e, c * P:(c + 1) * P], xnT[:], start=True, stop=True).then_inc(sem("hidden_ps"), 1)

                    def down(e):
                        pe.wait_ge(sem("hidden"), (e + 1) * FC3)
                        if e >= 1:
                            pe.wait_ge(sem("expert_added"), e)
                        for t in range(T):
                            for c in range(FC3):
                                mm = pe.matmul(psY[:, t * D:(t + 1) * D], hm[:, e % 2, c, t * P:(t + 1) * P], w23[:, e, c, :], start=c == 0, stop=c == FC3 - 1)
                        mm.then_inc(sem("expert_ps"), 1)

                    for j in range(PAIRS):
                        m = j % 2
                        if j >= 1:
                            pe.wait_ge(sem("qk"), j)
                        for n in range(2):
                            mm = pe.matmul(psA[:, n * S:(n + 1) * S], wqkvg3[:, n, j * P:(j + 1) * P], xnT[:], start=True, stop=True)
                        mm.then_inc(sem("qk_ps"), 1)
                        up(j, 0)
                        pe.wait_ge(sem("qk"), j + 1)
                        if j >= 1:
                            pe.wait_ge(sem("levelled"), j * (NL + 2))
                        for a in range(2):
                            for t in range(T):
                                mm = pe.matmul(psL[a][:, t * P:(t + 1) * P], kk[64 * a:64 * a + 64, m, t * P:(t + 1) * P],
                                               qq[64 * a:64 * a + 64, m, t * P:(t + 1) * P], start=True, stop=True)
                        mm.then_inc(sem("scored"), 1)
                        for n, h in enumerate(LEVELS + [P]):
                            if n in (1, 3, 5):
                                up(j, (n + 1) // 2)
                            pe.wait_ge(sem("levelled"), j * (NL + 2) + n + 1)
                            for a in range(2):
                                rows = slice(64 * a, 64 * a + 64)
                                if h < P:
                                    for t in range(T):
                                        q = qq[rows, m, t * P:(t + 1) * P].rearrange("p (c two h) -> p c two h", two=2, h=h)[:, :, 1, :]
                                        mm = pe.matmul(psL[a][:, t * P // 2:(t + 1) * P // 2], kk[rows, m, t * P:(t + 1) * P], q, start=True, stop=True)
                                else:
                                    mm = pe.matmul(psL[a][:, 0:P], kk[rows, m, 0:P], qq[rows, m, P:S], start=True, stop=True)
                            mm.then_inc(sem("scored"), 1)
                        down(j)
                        pe.wait_ge(sem("levelled"), (j + 1) * (NL + 2))
                        if j >= 1:
                            pe.wait_ge(sem("og"), j)
                            pe.wait_ge(sem("oT"), j)
                        for a in range(2):
                            ch = slice(j * P + 64 * a, j * P + 64 * a + 64)
                            o = [psO[:, t * P + 64 * a:t * P + 64 * a + 64] for t in range(T)]
                            pe.matmul(o[0], pT[:, m, a, 0, :], v3[:, 0, ch], start=True, stop=True)
                            pe.matmul(o[1], pT[:, m, a, 1, :], v3[:, 1, ch], start=True, stop=False)
                            mm = pe.matmul(o[1], pX[:, m, a, :], v3[:, 0, ch], start=False, stop=True)
                        mm.then_inc(sem("pv"), 1)
                        pe.wait_ge(sem("og"), j + 1)
                        for t in range(T):
                            mm = pe.transpose(psO[:, 256 + t * P:256 + (t + 1) * P], og[:, m, t, :], ident[:])
                        mm.then_inc(sem("oT_ps"), 1)
                        pe.wait_ge(sem("oT"), j + 1)
                        for t in range(T):
                            mm = pe.matmul(psV[:, t * D:(t + 1) * D], oT[:, m, t * P:(t + 1) * P], wo3[:, j, :],
                                           start=j == 0 and t == 0, stop=j == PAIRS - 1, skip_group_check=True)
                    mm.then_inc(sem("attn"), 1)
            nc.all_engine_barrier()
            sem.clear(nc)
            nc.all_engine_barrier()

        def layer1(b):
            with ExitStack() as lx:
                def lsb(name, shape, dt=F32):
                    return lx.enter_context(nc.sbuf_tensor(name, shape, dt))
                SCALE = float(QK) ** -0.5
                NV = VH + 1
                cc = lsb("cc", [P, T, P])
                ss = lsb("ss", [P, T, 4])
                junk = lsb("junk", [P, T, P])
                ccT = lsb("ccT", [P, S])
                krs = lsb("krs", [P, T, ROPE])
                krt = lsb("krt", [P, T, ROPE])
                kr = lsb("kr", [P, T, ROPE])
                glog = lsb("glog", [P, T, 3])
                gate = lsb("gate", [P, 4, 3])
                imp = lsb("imp", [1, 5, S])
                top8 = lsb("top8", [1, 4, 8])
                selc = lsb("selc", [P, T])
                selm = lsb("selm", [P, T, KEEP])
                selT = lsb("selT", [P, KEEP])
                tok = lsb("tok", [P, 2, HG, QK])
                tb = lsb("tb", [P, 2, HG, ROPE])
                qT = lsb("qT", [QK, NH, S])
                kT = lsb("kT", [QK, 2, NH, S])
                kT2 = lsb("kT2", [QK, NH, KEEP])
                vv = lsb("vv", [P, 2, T, NH, NV])
                vs = lsb("vs", [KEEP, NH, NV])
                sc_ = lsb("sc_", [P, 2, 2, HG * S // 2])
                p2 = lsb("p2", [P, T, NH, KEEP])
                p2T = lsb("p2T", [KEEP, NH, S])
                mx = lsb("mx", [P, 2, HG])
                mx2 = lsb("mx2", [P, T, NH])
                pTT = lsb("pTT", [P, 2, T, HG, P])
                rr = lsb("rr", [P, 3, HG])
                oo = lsb("oo", [P, 3, HG, VH])
                ot = lsb("ot", [P, T, NH, VH])
                otT = lsb("otT", [P, 4, S])
                ri = lsb("ri", [P, R1, S])
                xr = lsb("xr", [P, T, D])
                block = lx.enter_context(nc.Block())
                xb = x[:, bass.ds(b * T, T), :]
                NS = QL + KVL + ROPE + 3
                psX, psP = bank[0], bank[1]
                PROJ = [(k, g, t) for k in ("q", "k1", "kw") for g in range(G1) for t in range(T)]
                UNITS = [(k, g, t) for g in range(G1) for t in range(T) for k in (0, 1)]
                BLOCKS = [sum(t + 1 for _, _, t in UNITS[:u]) for u in range(len(UNITS))]

                def turn(dve, link, to, tmp, ps, sn, cs, n, hg):
                    H2 = ROPE // 2
                    bc = lambda a: a.unsqueeze(1).broadcast_to([n, hg, a.shape[-1]])
                    link.tell(dve.tensor_tensor(tmp[:, :, 0:H2], ps[:, :, H2:ROPE], bc(sn[:, 0:H2]), ALU.mult))
                    link.tell(dve.tensor_tensor(tmp[:, :, H2:], ps[:, :, 0:H2], bc(sn[:, H2:]), ALU.mult))
                    link.tell(dve.tensor_copy(to[:, :, ROPE:], ps[:, :, ROPE:]))
                    link(dve.tensor_tensor(to[:, :, 0:ROPE], ps[:, :, 0:ROPE], bc(cs), ALU.mult))
                    dve.tensor_tensor(to[:, :, 0:ROPE], to[:, :, 0:ROPE], tmp, ALU.add).then_inc(sem("tok"), 1)

                def merge(dve, link, n):
                    g, t = divmod(n, T)
                    dve.wait_ge(sem("pv"), n + 1)
                    o = bank[7][:, 0:3 * HG * NV].rearrange("p (a h v) -> p a h v", a=3, h=HG)
                    link(dve.reciprocal(rr[:], o[:, :, :, VH]))
                    link(dve.tensor_tensor(rr[:], rr[:], gate[:, 3, :].unsqueeze(2).broadcast_to([P, 3, HG]), ALU.mult))
                    for a in range(3):
                        link.tell(dve.tensor_tensor(oo[:, a], o[:, a, :, 0:VH], rr[:, a].unsqueeze(2).broadcast_to([P, HG, VH]), ALU.mult))
                    link.wait()
                    link(dve.tensor_tensor(oo[:, 0], oo[:, 0], oo[:, 1], ALU.add))
                    dve.tensor_tensor(ot[:, t, g * HG:(g + 1) * HG, :], oo[:, 0], oo[:, 2], ALU.add).then_inc(sem("merged"), 1)

                @block.vector
                def _(dve):
                    link = Chain(dve, sem("dve_chain"))
                    norm_dve(dve, link, xb)
                    dve.wait_ge(sem("squares"), 2 * T)
                    link.tell(dve.tensor_scalar(ss[:, :, 2:3], ss[:, :, 0:1], 1.0 / QL, 1e-6, ALU.mult, ALU.add))
                    link(dve.tensor_scalar(ss[:, :, 3:4], ss[:, :, 1:2], 1.0 / KVL, 1e-6, ALU.mult, ALU.add))
                    dve.sem_inc(sem("ms"), 1)
                    dve.tensor_copy(glog[:], psX[:].rearrange("p (t c) -> p t c", t=T)[:, :, QL + KVL + ROPE:NS]).then_inc(sem("glog"), 1)
                    link.tell(dve.tensor_copy(krs[:], psX[:].rearrange("p (t c) -> p t c", t=T)[:, :, QL + KVL:QL + KVL + ROPE]))
                    dve.wait_ge(sem("rms"), 1)
                    for t in range(T):
                        dve.tensor_scalar(cc[:, t, 0:QL], psX[:, t * S:t * S + QL], ss[:, t, 0:1], None, ALU.mult)
                        dve.tensor_scalar(cc[:, t, QL:P], psX[:, t * S + QL:t * S + P], ss[:, t, 1:2], None, ALU.mult).then_inc(sem("latents"), 1)
                    link.wait()
                    link(dve.tensor_scalar(krs[:], krs[:], 1.0 / NH, None, ALU.mult))
                    H2 = ROPE // 2
                    link.tell(dve.tensor_tensor(krt[:, :, 0:H2], krs[:, :, H2:], sin[:, :, 0:H2], ALU.mult))
                    link.tell(dve.tensor_tensor(krt[:, :, H2:], krs[:, :, 0:H2], sin[:, :, H2:], ALU.mult))
                    link(dve.tensor_tensor(kr[:], krs[:], cos, ALU.mult))
                    link(dve.tensor_tensor(kr[:], kr[:], krt[:], ALU.add))
                    dve.wait_ge(sem("imp_ps"), 1)
                    link(dve.tensor_copy(imp[:, 0, :], psP[0:1, 0:S]))
                    for n in range(KEEP // 8):
                        link(dve.max(top8[:, n, :], imp[:, n, :]))
                        link(dve.match_replace(imp[:, n + 1, :], top8[:, n, :], imp[:, n, :], -3e38))
                    link(dve.tensor_scalar(imp[:, 0, :], imp[:, 4, :], -2.9e38, None, ALU.is_lt))
                    link(dve.memset(imp[:, 1, :], 0.0))
                    link(dve.tensor_tensor_scan(imp[:, 2, :], imp[:, 0, :], imp[:, 1, :], 0.0, ALU.add, ALU.add))
                    link(dve.tensor_tensor(imp[:, 3, :], imp[:, 2, :], imp[:, 0, :], ALU.mult))
                    dve.tensor_scalar(imp[:, 3, :], imp[:, 3, :], -1.0, None, ALU.add).then_inc(sem("places"), 1)
                    dve.wait_ge(sem("places_ps"), 1)
                    link(dve.tensor_copy(selc[:], psP[:, 0:T]))
                    for t in range(T):
                        dve.tensor_scalar(selm[:, t, :], cst["iota"][:], selc[:, t:t + 1], None, ALU.is_equal).then_inc(sem("selm"), 1)
                    dve.wait_ge(sem("gate_ps"), 1)
                    link(dve.tensor_scalar(gate[:, 0, :], psP[:, 64:67], 1.0 / S, None, ALU.mult))
                    link(dve.tensor_reduce(mx[:, 0, 0:1], gate[:, 0, :], X, ALU.max, negate=True))
                    dve.tensor_scalar(gate[:, 1, :], gate[:, 0, :], mx[:, 0, 0:1], None, ALU.add).then_inc(sem("gate_in"), 1)
                    dve.wait_ge(sem("gate_exp"), 1)
                    link(dve.tensor_reduce(mx[:, 0, 0:1], gate[:, 2, :], X, ALU.add))
                    link(dve.reciprocal(mx[:, 0, 0:1], mx[:, 0, 0:1]))
                    link(dve.tensor_scalar(gate[:, 3, :], gate[:, 2, :], mx[:, 0, 0:1], None, ALU.mult))
                    for n, (kind, g, t) in enumerate(PROJ):
                        m = n % 2
                        ps = bank[2 + m]
                        if n >= 2:
                            dve.wait_ge(sem("headsT_ps"), n - 1)
                        dve.wait_ge(sem("heads_ps"), n + 1)
                        if kind == "k1":
                            dve.tensor_copy(tok[:, m, :, 0:ROPE], kr[:, t, :].unsqueeze(1).broadcast_to([P, HG, ROPE]))
                            dve.tensor_copy(tok[:, m, :, ROPE:], ps[:, 0:HG * NOPE].rearrange("p (h c) -> p h c", h=HG)).then_inc(sem("tok"), 1)
                        else:
                            turn(dve, link, tok[:, m], tb[:, m], ps[:, 0:HG * QK].rearrange("p (h c) -> p h c", h=HG),
                                 sin[:, t, :], cos[:, t, :], P, HG)
                    for n in range(G1):
                        m = n % 2
                        dve.wait_ge(sem("heads_ps"), len(PROJ) + n + 1)
                        dve.wait_ge(sem("headsT_ps"), len(PROJ) + n - 1)
                        turn(dve, link, tok[0:KEEP, m], tb[0:KEEP, m], bank[2 + m][0:KEEP, 0:HG * QK].rearrange("p (h c) -> p h c", h=HG),
                             sin[0:KEEP, 0, :], cos[0:KEEP, 0, :], KEEP, HG)
                    for t in range(T):
                        dve.wait_ge(sem("scores2"), t + 1)
                        s2 = bank[2 + t][:].rearrange("p (h k) -> p h k", h=NH)
                        link(dve.tensor_reduce(mx2[:, t, :], s2, X, ALU.max))
                        dve.tensor_tensor(p2[:, t], s2, mx2[:, t, :].unsqueeze(2).broadcast_to([P, NH, KEEP]), ALU.subtract).then_inc(sem("shift2"), 1)
                    for u, (k, g, t) in enumerate(UNITS):
                        m = u % 2
                        kn = (t + 1) * P
                        dve.wait_ge(sem("scores"), u + 1)
                        if u >= 2:
                            dve.wait_ge(sem("probT_blk"), BLOCKS[u - 1])
                        for h2 in range(2):
                            sview = bank[2 + 2 * m + h2][:, 0:2 * kn].rearrange("p (h k) -> p h k", h=2)
                            hs = slice(2 * h2, 2 * h2 + 2)
                            link(dve.tensor_reduce(mx[:, m, hs], sview, X, ALU.max))
                            ins = dve.tensor_tensor(sc_[:, m, h2, 0:2 * kn].rearrange("p (h k) -> p h k", h=2), sview,
                                                    mx[:, m, hs].unsqueeze(2).broadcast_to([P, 2, kn]), ALU.subtract)
                        ins.then_inc(sem("shift"), 1)
                        if u >= 2 and u % 2 == 1:
                            merge(dve, link, u // 2 - 1)
                    merge(dve, link, len(UNITS) // 2 - 1)
                    dve.wait_ge(sem("out_ps"), 1)
                    link(dve.tensor_tensor(xr[:], bank[1][:, 0:T * D].rearrange("p (t d) -> p t d", t=T), xb, ALU.add))
                    dve.tensor_tensor(xb, xr[:], bias1[:].unsqueeze(1).broadcast_to([P, T, D]), ALU.add)

                @block.gpsimd
                def _(pool):
                    norm_pool(pool)
                    pool.memset(vv[:, :, :, :, VH:NV], 1.0).then_inc(sem("v_ones"), 1)
                    pool.memset(vs[:, :, VH:NV], 1.0).then_inc(sem("v_ones"), 1)
                    pool.wait_ge(sem("ms"), 1)
                    pool.tensor_tensor(ss[:, :, 0:2], ss[:, :, 2:4], mhalf[:, 0:4].rearrange("p (t a) -> p t a", t=T), ALU.pow).then_inc(sem("rms"), 1)

                @block.scalar
                def _(act):
                    norm_act(act, psX)
                    act.wait_ge(sem("small"), 1)
                    for t in range(T):
                        act.activation(junk[:, t, 0:QL], psX[:, t * S:t * S + QL], ACT.Square, accum_out=ss[:, t, 0:1]).then_inc(sem("squares"), 1)
                        act.activation(junk[:, t, QL:P], psX[:, t * S + QL:t * S + P], ACT.Square, accum_out=ss[:, t, 1:2]).then_inc(sem("squares"), 1)
                    act.wait_ge(sem("units_ps"), 1)
                    for r in range(R1):
                        act.activation(ri[:, r, :], bank[4][:, 0:S], ACT.Relu, scale=f1[:, 0, r:r + 1], bias=f1[:, 1, r:r + 1]).then_inc(sem("inner"), 1)
                    act.wait_ge(sem("latT_ps"), 1)
                    act.activation(ccT[:], bank[5][:, 0:S], ACT.Copy).then_inc(sem("latT"), 1)
                    act.wait_ge(sem("gate_in"), 1)
                    act.activation(gate[:, 2, :], gate[:, 1, :], ACT.Exp).then_inc(sem("gate_exp"), 1)
                    act.wait_ge(sem("sel_ps"), 1)
                    act.activation(selT[:], bank[6][:, 0:KEEP], ACT.Copy).then_inc(sem("selT"), 1)
                    for n in range(2 * T):
                        act.wait_ge(sem("values_ps"), n + 1)
                        act.activation(vv[:, n // T, n % T, :, 0:VH], bank[4 + n % 2][:].rearrange("p (h v) -> p h v", h=NH), ACT.Copy).then_inc(sem("values"), 1)
                    act.wait_ge(sem("values_ps"), 2 * T + 1)
                    act.activation(vs[:, :, 0:VH], bank[4][0:KEEP, :].rearrange("p (h v) -> p h v", h=NH), ACT.Copy).then_inc(sem("values"), 1)
                    for n, (kind, g, t) in enumerate(PROJ):
                        act.wait_ge(sem("headsT_ps"), n + 1)
                        dst = qT[:, g * HG:(g + 1) * HG] if kind == "q" else kT[:, int(kind == "kw"), g * HG:(g + 1) * HG]
                        act.activation(dst[:, :, t * P:(t + 1) * P], bank[5 + n % 2][0:QK, :].rearrange("p (h k) -> p h k", h=HG), ACT.Copy).then_inc(sem("headsT"), 1)
                    for n in range(G1):
                        act.wait_ge(sem("headsT_ps"), len(PROJ) + n + 1)
                        act.activation(kT2[:, n * HG:(n + 1) * HG, :], bank[5 + n % 2][0:QK, 0:HG * KEEP].rearrange("p (h k) -> p h k", h=HG), ACT.Copy).then_inc(sem("headsT"), 1)
                    for t in range(T):
                        act.wait_ge(sem("shift2"), t + 1)
                        act.activation(p2[:, t], p2[:, t], ACT.Exp, scale=SCALE).then_inc(sem("prob2"), 1)
                    for n in range(T * G1):
                        act.wait_ge(sem("prob2T_ps"), n + 1)
                        t, g = divmod(n, G1)
                        act.activation(p2T[:, g * HG:(g + 1) * HG, t * P:(t + 1) * P], bank[5 + n % 2][0:KEEP, :].rearrange("p (h q) -> p h q", h=HG), ACT.Copy).then_inc(sem("prob2T"), 1)
                    for u, (k, g, t) in enumerate(UNITS):
                        m = u % 2
                        kn = (t + 1) * P
                        act.wait_ge(sem("shift"), u + 1)
                        act.activation(sc_[:, m, :, 0:2 * kn], sc_[:, m, :, 0:2 * kn], ACT.Exp, scale=SCALE).then_inc(sem("prob"), 1)
                        for j in range(t + 1):
                            act.wait_ge(sem("probT_blk"), BLOCKS[u] + j + 1)
                            act.activation(pTT[:, m, j], bank[6][:].rearrange("p (h q) -> p h q", h=HG), ACT.Copy).then_inc(sem("probT"), 1)
                    for t in range(T):
                        act.wait_ge(sem("otT_ps"), t + 1)
                        act.activation(otT[:, :, t * P:(t + 1) * P], bank[2 + t][:].rearrange("p (c q) -> p c q", c=4), ACT.Copy).then_inc(sem("otT"), 1)

                @block.tensor
                def _(pe):
                    norm_pe(pe, psX)
                    pe.wait_ge(sem("xnT"), 1)
                    for t in range(T):
                        mm = pe.matmul(psX[:, t * S:t * S + NS], xnT[:, t * P:(t + 1) * P], small1[:], start=True, stop=True)
                    mm.then_inc(sem("small"), 1)
                    pe.matmul(psP[0:1, 0:S], wimp[:], xnT[:], start=True, stop=True).then_inc(sem("imp_ps"), 1)
                    pe.matmul(bank[4][:, 0:S], win[:].rearrange("p m j -> p (m j)"), xnT[:], start=True, stop=True).then_inc(sem("units_ps"), 1)
                    pe.wait_ge(sem("latents"), T)
                    for t in range(T):
                        mm = pe.transpose(bank[5][:, t * P:(t + 1) * P], cc[:, t, :], ident[:])
                    mm.then_inc(sem("latT_ps"), 1)
                    pe.wait_ge(sem("places"), 1)
                    for t in range(T):
                        mm = pe.matmul(psP[:, t:t + 1], imp[0:1, 3, t * P:(t + 1) * P], ones[0:1, 0:1], start=True, stop=True)
                    mm.then_inc(sem("places_ps"), 1)
                    pe.wait_ge(sem("glog"), 1)
                    pe.wait_ge(sem("selm"), T)
                    for t in range(T):
                        mm = pe.matmul(psP[:, 64:67], ones[:], glog[:, t, :], start=t == 0, stop=t == T - 1)
                    mm.then_inc(sem("gate_ps"), 1)
                    for t in range(T):
                        mm = pe.matmul(bank[6][:, 0:KEEP], xn[:, t, :], selm[:, t, :], start=t == 0, stop=t == T - 1)
                    mm.then_inc(sem("sel_ps"), 1)
                    pe.wait_ge(sem("latT"), 1)
                    pe.wait_ge(sem("inner"), R1)
                    pe.wait_ge(sem("selT"), 1)
                    HV = NH * VH
                    for n in range(2 * T + 1):
                        k, t = divmod(n, T)
                        if n >= 2:
                            pe.wait_ge(sem("values"), n - 1)
                        if k == 0:
                            mm = pe.matmul(bank[4 + n % 2][:], ccT[QL:P, t * P:(t + 1) * P], wdkv[QL:P, HV:], start=True, stop=True)
                        elif k == 1:
                            mm = pe.matmul(bank[4 + n % 2][:], xnT[:, t * P:(t + 1) * P], winv[:], start=True, stop=True)
                        else:
                            mm = pe.matmul(bank[4][0:KEEP, :], selT[:], selv[:], start=True, stop=True)
                        mm.then_inc(sem("values_ps"), 1)

                    def project(n):
                        ps = bank[2 + n % 2]
                        if n >= 2:
                            pe.wait_ge(sem("tok"), n - 1)
                        if n >= len(PROJ):
                            g = n - len(PROJ)
                            mm = pe.matmul(ps[0:KEEP, 0:HG * QK], selT[:], selk[:, g * HG * QK:(g + 1) * HG * QK], start=True, stop=True)
                        else:
                            kind, g, t = PROJ[n]
                            if kind == "q":
                                mm = pe.matmul(ps[:, 0:HG * QK], ccT[0:QL, t * P:(t + 1) * P], wdq[:, g * HG * QK:(g + 1) * HG * QK], start=True, stop=True)
                            elif kind == "k1":
                                mm = pe.matmul(ps[:, 0:HG * NOPE], ccT[QL:P, t * P:(t + 1) * P], wdkv[QL:P, g * HG * NOPE:(g + 1) * HG * NOPE], start=True, stop=True)
                            else:
                                mm = pe.matmul(ps[:, 0:HG * QK], xnT[:, t * P:(t + 1) * P], wink[:, g * HG * QK:(g + 1) * HG * QK], start=True, stop=True)
                        mm.then_inc(sem("heads_ps"), 1)

                    def turn_heads(n):
                        pe.wait_ge(sem("tok"), n + 1)
                        if n >= 2:
                            pe.wait_ge(sem("headsT"), n - 1)
                        else:
                            pe.wait_ge(sem("values"), 2 * T + 1)
                        rows = P if n < len(PROJ) else KEEP
                        for h in range(HG):
                            mm = pe.transpose(bank[5 + n % 2][0:QK, h * rows:(h + 1) * rows], tok[0:rows, n % 2, h, :], ident[0:rows, 0:rows])
                        mm.then_inc(sem("headsT_ps"), 1)

                    NP_ = len(PROJ) + G1
                    project(0)
                    for n in range(NP_):
                        if n + 1 < NP_:
                            project(n + 1)
                        turn_heads(n)
                    pe.wait_ge(sem("headsT"), NP_)
                    for t in range(T):
                        for h in range(NH):
                            mm = pe.matmul(bank[2 + t][:, h * KEEP:(h + 1) * KEEP], qT[:, h, t * P:(t + 1) * P], kT2[:, h, :], start=True, stop=True)
                        mm.then_inc(sem("scores2"), 1)
                    for n in range(T * G1):
                        t, g = divmod(n, G1)
                        pe.wait_ge(sem("prob2"), t + 1)
                        if n >= 2:
                            pe.wait_ge(sem("prob2T"), n - 1)
                        for h in range(HG):
                            mm = pe.transpose(bank[5 + n % 2][0:KEEP, h * P:(h + 1) * P], p2[:, t, g * HG + h, :], ident[:])
                        mm.then_inc(sem("prob2T_ps"), 1)
                    pe.wait_ge(sem("prob2T"), T * G1)
                    pe.wait_ge(sem("v_ones"), 2)

                    def scores(u):
                        k, g, t = UNITS[u]
                        m = u % 2
                        kn = (t + 1) * P
                        if u >= 2:
                            pe.wait_ge(sem("shift"), u - 1)
                        for h in range(HG):
                            ps = bank[2 + 2 * m + h // 2]
                            o = (h % 2) * kn
                            pe.matmul(ps[:, o:o + kn], qT[:, g * HG + h, t * P:(t + 1) * P], kT[:, k, g * HG + h, 0:kn], start=True, stop=False, skip_group_check=True)
                            mm = pe.matmul(ps[:, o + t * P:o + kn], ident[:], cst["negmask"][:], start=False, stop=True, skip_group_check=True)
                        mm.then_inc(sem("scores"), 1)

                    nblk = 0
                    scores(0)
                    for u, (k, g, t) in enumerate(UNITS):
                        m = u % 2
                        kn = (t + 1) * P
                        if u + 1 < len(UNITS):
                            scores(u + 1)
                        pe.wait_ge(sem("prob"), u + 1)
                        for j in range(t + 1):
                            if nblk >= 1:
                                pe.wait_ge(sem("probT"), nblk)
                            nblk += 1
                            for h in range(HG):
                                a = (h % 2) * kn + j * P
                                mm = pe.transpose(bank[6][:, h * P:(h + 1) * P], sc_[:, m, h // 2, a:a + P], ident[:])
                            mm.then_inc(sem("probT_blk"), 1)
                        pe.wait_ge(sem("probT"), nblk)
                        if k == 0 and u >= 2:
                            pe.wait_ge(sem("merged"), u // 2)
                        o = bank[7][:, 0:3 * HG * NV].rearrange("p (a h v) -> p a h v", a=3, h=HG)
                        for h in range(HG):
                            for j in range(t + 1):
                                mm = pe.matmul(o[:, 2 * k, h, :], pTT[:, m, j, h, :], vv[:, k, j, g * HG + h, :], start=j == 0, stop=j == t)
                        if k == 1:
                            for h in range(HG):
                                mm = pe.matmul(o[:, 1, h, :], p2T[:, g * HG + h, t * P:(t + 1) * P], vs[:, g * HG + h, :], start=True, stop=True)
                            mm.then_inc(sem("pv"), 1)
                    pe.wait_ge(sem("merged"), G1 * T)
                    for t in range(T):
                        for c in range(4):
                            mm = pe.transpose(bank[2 + t][:, c * P:(c + 1) * P], ot[:, t, c * HG:(c + 1) * HG, :].rearrange("p h v -> p (h v)"), ident[:])
                        mm.then_inc(sem("otT_ps"), 1)
                    pe.wait_ge(sem("otT"), T)
                    for t in range(T):
                        for c in range(4):
                            pe.matmul(bank[1][:, t * D:(t + 1) * D], otT[:, c, t * P:(t + 1) * P], wpj[:, c, :], start=c == 0, stop=False)
                        for r in range(R1):
                            mm = pe.matmul(bank[1][:, t * D:(t + 1) * D], ri[:, r, t * P:(t + 1) * P], wc1[:, r, :], start=False, stop=r == R1 - 1)
                    mm.then_inc(sem("out_ps"), 1)
            nc.all_engine_barrier()
            sem.clear(nc)
            nc.all_engine_barrier()

        bodies = {0: layer0, 1: layer1, 2: layer2}
        for n in (0, 1):
            if n in layers:
                with nc.Fori(0, B) as b:
                    bodies[n](b)

        wqkvg3 = sb("wqkvg3", [P, 4, NH3 * DK3])
        bg3 = sb("bg3", [P, PAIRS])
        wo3 = sb("wo3", [P, PAIRS, D])
        gate3 = sb("gate3", [P, E3])
        gb3 = sb("gb3", [P, E3])
        w13 = sb("w13", [P, E3, F3])
        b13 = sb("b13", [P, E3, FC3])
        w23 = sb("w23", [P, E3, FC3, D])
        b23 = sb("b23", [E3, D])
        s_load3 = ctx.enter_context(nc.semaphore("loaded3"))
        loads3 = [(wqkvg3[:, n, :], w[name]) for n, name in enumerate(("W_q", "W_k", "W_v", "W_gate"))]
        loads3 += [
            (bg3[:], w["b_gateT"]),
            (wo3[:], w["W_o"].rearrange("(c p) d -> p c d", p=P)),
            (gate3[:], w["gate3T"]),
            (gb3[:], w["gb3_rep"]),
            (w13[:], w["W13"].rearrange("e d f -> d e f")),
            (b13[:], w["b13T"]),
            (w23[:], w["W23"].rearrange("e (c p) d -> p e c d", p=P)),
            (b23[:], w["b23"]),
        ]
        if 3 in layers:
            with nc.Block() as block:
                @block.sync
                def _(sp):
                    for dst, src in loads3:
                        sp.dma_start(dst, src).then_inc(s_load3, 16)
        if 2 in layers:
            with nc.Fori(0, B) as b:
                layer2(b)
        if 3 in layers:
            with nc.Block() as block:
                @block.tensor
                def _(pe):
                    pe.wait_ge(s_load3, 16 * len(loads3))

                @block.vector
                def _(dve):
                    dve.wait_ge(s_load3, 16 * len(loads3))

                @block.scalar
                def _(act):
                    act.wait_ge(s_load3, 16 * len(loads3))
            with nc.Fori(0, B) as b:
                layer3(b, wqkvg3, bg3, wo3, gate3, gb3, w13, b13, w23, b23)

        with nc.Block() as block:
            @block.sync
            def _(sp):
                sp.dma_start(out.rearrange("b (t p) d -> p (b t) d", p=P), x[:]).then_inc(s_out, 16)
                sp.wait_ge(s_out, 16)


def host_layout(i):
    t = lambda a: np.ascontiguousarray(a)
    L = {}
    L["x"] = i["L0_attn_x"]
    L["w_lhs"], L["w_rhs"] = i["L0_attn_w_lhs"], i["L0_attn_w_rhs"]
    L["W_fcT"] = t(i["L0_ffn_W_fc"].T)
    L["W_projT"] = t(i["L0_ffn_W_proj"].T)
    L["ln_wT"], L["ln_bT"] = t(i["L0_ffn_ln_w"].reshape(C0, P).T), t(i["L0_ffn_ln_b"].reshape(C0, P).T)
    for n in ("w_cq", "w_ckv", "w_krope", "w_gate", "g_qnorm", "g_kvnorm", "w_dk_nope", "w_dv", "w_imp", "w_selv", "w_winv", "w_proj"):
        L[n] = i["L1_attn_" + n]
    nope = i["L1_attn_w_dq_nope"].reshape(QL, NH, NOPE)
    rope = i["L1_attn_w_dq_rope"].reshape(QL, NH, ROPE)
    L["w_dq"] = t(np.concatenate([rope, nope], 2).reshape(QL, NH * QK))
    for n in ("w_selk", "w_wink"):
        a = i["L1_attn_" + n].reshape(D, NH, QK)
        L[n] = t(np.concatenate([a[..., NOPE:], a[..., :NOPE]], 2).reshape(D, NH * QK))
    for n in ("W1", "b1", "W2", "b2", "Wout"):
        L[n] = i["L1_ffn_" + n]
    L["bin_rep"] = t(np.repeat(i["L1_ffn_bin_"], J1)[:, None])
    L["Win_rep"] = t(np.repeat(i["L1_ffn_Win"][:, :, None], J1, axis=2))
    L["Wout_rep"] = t(np.repeat(i["L1_ffn_Wout"], J1, axis=0))
    L["bout_rep"] = t(np.broadcast_to(i["L1_ffn_bout"], (P, D)))
    for n in "QKV":
        L[f"W{n}T"] = t(i[f"L2_attn_W{n}"].T)
    L["gate2T"] = t(i["L2_ffn_gate_w"].T)
    L["bias2_rep"] = t(np.broadcast_to(i["L2_ffn_bias_e"], (P, E2)))
    L["up2T"] = t(i["L2_ffn_up_w"].transpose(2, 0, 1).reshape(D, E2 * I2))
    L["down2"] = t(i["L2_ffn_down_w"].transpose(0, 2, 1).reshape(E2 * I2, D))
    L["sup2T"] = t(i["L2_ffn_shared_up"].T)
    L["sdown2T"] = t(i["L2_ffn_shared_down"].T)
    for n in ("W_q", "W_k", "W_v", "W_gate", "W_o"):
        L[n] = i["L3_attn_" + n]
    L["b_gateT"] = t(i["L3_attn_b_gate"].reshape(PAIRS, P).T)
    L["gate3T"] = t(i["L3_ffn_gate_w"].T)
    L["gb3_rep"] = t(np.broadcast_to(i["L3_ffn_gate_b"], (P, E3)))
    L["b13T"] = t(i["L3_ffn_b1"].reshape(E3, FC3, P).transpose(2, 0, 1))
    L["W13"], L["W23"], L["b23"] = i["L3_ffn_W1"], i["L3_ffn_W2"], i["L3_ffn_b2"]
    for n, a in constants().items():
        L["c_" + n] = a
    return L


def kernel(**inputs):
    import concourse.bacc as _bacc
    from concourse.bass_utils import run_bass_kernel_spmd as _run

    arrays = {f"in_{n}": np.ascontiguousarray(a) for n, a in host_layout({k: np.asarray(v) for k, v in inputs.items()}).items()}
    nc = _bacc.Bacc("TRN2", target_bir_lowering=False, num_devices=1)
    w = {n[3:]: nc.dram_tensor(n, a.shape, mybir.dt.from_np(a.dtype), kind="ExternalInput").ap() for n, a in arrays.items()}
    out = nc.dram_tensor("out_x", (B, S, D), F32, kind="ExternalOutput").ap()
    program(nc, w, out)
    r = _run(nc, [arrays], core_ids=[0])
    return r.results[0]["out_x"]
```

```python
from contextlib import ExitStack

import numpy as np

import concourse.bass as bass
from concourse import mybir

F32 = mybir.dt.float32
BF16 = mybir.dt.bfloat16
U32 = mybir.dt.uint32
ALU = mybir.AluOpType
ACT = mybir.ActivationFunctionType
X = mybir.AxisListType.X

P = 128
B, S, D = 8, 256, 128
T = S // P
LN_EPS = 1e-5

H0 = 512
C0 = H0 // P
NH, NOPE, ROPE, VH = 16, 32, 64, 32
QK = NOPE + ROPE
QL, KVL = 96, 32
KEEP = 32
HG = 4
G1 = NH // HG
M1, INNER = 64, 16
J1 = P // M1
R1 = INNER // J1
NEG = -1e30
E2, K2, GR2, I2, SH2 = 16, 4, 4, 64, 256
EP2 = E2 * I2 // P
SP2 = SH2 // P
ROUTED_SCALE = 2.5
NH3, DK3 = 16, 64
PAIRS = NH3 * DK3 // P
LEVELS = [1, 2, 4, 8, 16, 32, 64]
E3, F3 = 8, 512
FC3 = F3 // P
CAP3 = -(-5 * 4 * 256 * 2 // (4 * E3))


def constants():
    i = np.arange(P)
    out = {}
    out["ident"] = np.eye(P, dtype=np.float32)
    out["causal"] = (i[:, None] >= i[None, :]).astype(np.float32)
    out["tri"] = (i[:, None] <= i[None, :]).astype(np.float32)
    out["negmask"] = np.where(i[:, None] >= i[None, :], 0.0, NEG).astype(np.float32)
    out["iota"] = np.broadcast_to(np.arange(KEEP, dtype=np.float32), (P, KEEP)).copy()
    e = np.arange(E2)
    out["before"] = np.broadcast_to((e[None, :] < e[:, None]).astype(np.float32).reshape(-1), (P, E2 * E2)).copy()
    spread = np.zeros((P, EP2, P), np.float32)
    for p in range(EP2):
        for m in range(P):
            spread[(P // I2) * p + m // I2, p, m] = 1
    out["spread"] = spread.reshape(P, -1)
    level = np.zeros((P, len(LEVELS), 2 * T, P // 2), np.uint32)
    for n, h in enumerate(LEVELS):
        right = i[(i // h) % 2 == 1]
        level[:, n, :, :] = (((i[:, None] // h) % 2 == 0) & (i[:, None] // (2 * h) == right[None, :] // (2 * h)))[:, None, :]
    out["level"] = level.reshape(P, -1)
    f = (np.float32(1.0) / np.float32(10000.0) ** (np.arange(0, ROPE, 2, dtype=np.float32) / np.float32(ROPE))).astype(np.float32)
    a = np.outer(np.arange(S, dtype=np.float32), f).astype(np.float32)
    c, s = np.cos(a), np.sin(a)
    out["cos"] = np.concatenate([c, c], 1).reshape(T, P, ROPE).transpose(1, 0, 2).reshape(P, -1).astype(np.float32)
    out["sin"] = np.concatenate([-s, s], 1).reshape(T, P, ROPE).transpose(1, 0, 2).reshape(P, -1).astype(np.float32)
    return out


class Chain:

    def __init__(self, eng, sem):
        self.eng, self.sem, self.n = eng, sem, 0

    def tell(self, ins):
        self.n += 1
        ins.then_inc(self.sem, 1)

    def wait(self):
        self.eng.wait_ge(self.sem, self.n)

    def __call__(self, ins):
        self.tell(ins)
        self.wait()


class Sems:

    def __init__(self, nc, ctx, count):
        self.free = [ctx.enter_context(nc.semaphore(f"s{n}")) for n in range(count)]
        self.named = {}

    def __call__(self, name):
        if name not in self.named:
            self.named[name] = self.free[len(self.named)]
        return self.named[name]

    def clear(self, nc):
        for s in self.named.values():
            nc.sync.sem_clear(s)
        self.named = {}


def program(nc, w, out, layers=(0, 1, 2, 3)):
    ctx = ExitStack()
    with ctx:
        def sb(name, shape, dt=F32):
            return ctx.enter_context(nc.sbuf_tensor(name, shape, dt))

        def pb(name):
            return ctx.enter_context(nc.psum_tensor(name, [P, 512], F32))

        bank = [pb(f"bank{n}") for n in range(8)]
        sem = Sems(nc, ctx, 60)
        s_load = ctx.enter_context(nc.semaphore("loaded"))
        s_out = ctx.enter_context(nc.semaphore("stored"))

        x = sb("x", [P, B * T, D])
        cst = {}
        for name, width, dt in (("ident", P, F32), ("causal", P, F32), ("tri", P, F32), ("negmask", P, F32),
                                ("iota", KEEP, F32), ("before", E2 * E2, F32), ("spread", EP2 * P, F32),
                                ("cos", T * ROPE, F32), ("sin", T * ROPE, F32)):
            cst[name] = sb("c_" + name, [P, width], dt)
        ident = cst["ident"]
        cos = cst["cos"][:].rearrange("p (t r) -> p t r", t=T)
        sin = cst["sin"][:].rearrange("p (t r) -> p t r", t=T)
        ones = sb("ones", [P, P])
        mhalf = sb("mhalf", [P, 8])

        xn = sb("xn", [P, T, D])
        xnT = sb("xnT", [P, S])
        stats = sb("stats", [P, T, 6])
        mv = sb("mv", [P, T, 2])
        ve = sb("ve", [P, T])
        rstd = sb("rstd", [P, T])

        w_lr = sb("w_lr", [P, 2])
        w_lrp = sb("w_lrp", [P, 1])
        fcw = sb("fcw", [P, H0])
        pjw = sb("pjw", [P, C0, D + 1])
        lnw = sb("lnw", [P, C0])
        lnb = sb("lnb", [P, C0])
        wsum = sb("wsum", [P, D])
        bias0 = sb("bias0", [P, D])
        small1 = sb("small1", [P, QL + KVL + ROPE + 3])
        wdq = sb("wdq", [QL, NH * QK])
        gq = sb("gq", [P, 1])
        wdkv = sb("wdkv", [P, 2 * NH * VH])
        wimp = sb("wimp", [P, 1])
        selk = sb("selk", [P, NH * QK])
        selv = sb("selv", [P, NH * VH])
        wink = sb("wink", [P, NH * QK])
        winv = sb("winv", [P, NH * VH])
        wpj = sb("wpj", [P, 4, D])
        win = sb("win", [P, M1, J1])
        f1 = sb("f1", [P, 4, R1])
        wo1 = sb("wo1", [P, D])
        wc1 = sb("wc1", [P, R1, D])
        b2o = sb("b2o", [M1, 1])
        b2b = sb("b2b", [M1, P])
        wout1 = sb("wout1", [M1, D])
        bias1 = sb("bias1", [P, D])
        wqkv2 = sb("wqkv2", [P, 3, D])
        gate2 = sb("gate2", [P, E2])
        bias2 = sb("bias2", [P, E2])
        up2 = sb("up2", [P, E2 * I2])
        down2 = sb("down2", [P, EP2, D])
        sup2 = sb("sup2", [P, SH2])
        sdown2 = sb("sdown2", [P, SP2, D])
        carry = sb("carry", [P, 2, E3])

        loads = []

        def load(dst, src):
            loads.append((dst, src))

        load(x[:], w["x"].rearrange("b (t p) d -> p (b t) d", p=P))
        for name in cst:
            load(cst[name][:], w["c_" + name])
        load(w_lr[:, 0:1], w["w_lhs"].rearrange("a b d -> d (a b)"))
        load(w_lr[:, 1:2], w["w_rhs"].rearrange("a b d -> d (a b)"))
        load(fcw[:], w["W_fcT"])
        load(pjw[:, :, 0:D], w["W_projT"].rearrange("(c p) d -> p c d", p=P))
        load(lnw[:], w["ln_wT"])
        load(lnb[:], w["ln_bT"])
        if 1 in layers:
            for a, n, name in ((0, QL, "w_cq"), (QL, KVL, "w_ckv"), (QL + KVL, ROPE, "w_krope"), (QL + KVL + ROPE, 3, "w_gate")):
                load(small1[:, a:a + n], w[name])
            load(wdq[:], w["w_dq"])
            load(gq[0:QL, :], w["g_qnorm"].rearrange("(p a) -> p a", a=1))
            load(gq[QL:P, :], w["g_kvnorm"].rearrange("(p a) -> p a", a=1))
            load(wdkv[QL:P, 0:NH * VH], w["w_dk_nope"])
            load(wdkv[QL:P, NH * VH:], w["w_dv"])
            load(wimp[:], w["w_imp"])
            load(selk[:], w["w_selk"])
            load(selv[:], w["w_selv"])
            load(wink[:], w["w_wink"])
            load(winv[:], w["w_winv"])
            load(wpj[:], w["w_proj"].rearrange("(c p) d -> p c d", p=P))
            load(win[:], w["Win_rep"])
            load(f1[:, 0, :], w["W1"].rearrange("m (j r) -> (m j) r", j=J1))
            load(f1[:, 1, :], w["b1"].rearrange("m (j r) -> (m j) r", j=J1))
            load(f1[:, 2, :], w["W2"].rearrange("m (j r) -> (m j) r", j=J1))
            load(f1[:, 3, 0:1], w["bin_rep"])
            load(wo1[:], w["Wout_rep"])
            load(b2o[:], w["b2"].rearrange("(p a) -> p a", a=1))
            load(wout1[:], w["Wout"])
            load(bias1[:], w["bout_rep"])
        if 2 in layers:
            for n, name in enumerate(("WQT", "WKT", "WVT")):
                load(wqkv2[:, n, :], w[name])
            load(gate2[:], w["gate2T"])
            load(bias2[:], w["bias2_rep"])
            load(up2[:], w["up2T"])
            load(down2[:], w["down2"].rearrange("(c p) d -> p c d", p=P))
            load(sup2[:], w["sup2T"])
            load(sdown2[:], w["sdown2T"].rearrange("(c p) d -> p c d", p=P))
        with ExitStack() as sx:
            absum = sx.enter_context(nc.sbuf_tensor("absum", [P, 2], F32))
            gamma = sx.enter_context(nc.sbuf_tensor("gamma", [P, 4], F32))
            tern = sx.enter_context(nc.sbuf_tensor("tern", [P, 3, H0], F32))
            lnb_b = sx.enter_context(nc.sbuf_tensor("lnb_b", [P, C0, P], F32))
            block = sx.enter_context(nc.Block())

            @block.sync
            def _(sp):
                for n, (dst, src) in enumerate(loads):
                    if n % 2 == 0:
                        sp.dma_start(dst, src).then_inc(s_load, 16)

            @block.scalar
            def _(act):
                for n, (dst, src) in enumerate(loads):
                    if n % 2 == 1:
                        act.dma_start(dst, src).then_inc(s_load, 16)

            @block.gpsimd
            def _(pool):
                pool.memset(ones[:], 1.0).then_inc(sem("ones"), 1)
                pool.memset(mhalf[:], -0.5)
                pool.memset(carry[:], 0.0)

            @block.vector
            def _(dve):
                link = Chain(dve, sem("dve_chain"))
                dve.wait_ge(s_load, 16 * len(loads))
                dve.tensor_reduce(absum[:, 0:1], fcw[:], X, ALU.add, apply_absolute_value=True)
                dve.tensor_reduce(absum[:, 1:2], pjw[:, :, 0:D], mybir.AxisListType.XY, ALU.add,
                                  apply_absolute_value=True).then_inc(sem("absum"), 1)
                link(dve.tensor_tensor(w_lrp[:], w_lr[:, 0:1], w_lr[:, 1:2], ALU.mult))
                dve.wait_ge(sem("abs_all"), 1)
                link(dve.tensor_scalar(gamma[:, 0:2], bank[0][:, 0:2], 1.0 / (H0 * D), 1e-6, ALU.mult, ALU.add))
                link(dve.reciprocal(gamma[:, 2:4], gamma[:, 0:2]))
                for n, (wt, view) in enumerate(((fcw[:], tern[:, 0, :]), (pjw[:, :, 0:D], tern[:, 0, :].rearrange("p (c d) -> p c d", c=C0)))):
                    up = tern[:, 1, :] if n == 0 else tern[:, 1, :].rearrange("p (c d) -> p c d", c=C0)
                    link(dve.tensor_scalar(view, wt, gamma[:, 2 + n:3 + n], None, ALU.mult))
                    link(dve.tensor_scalar(up, view, 0.5, None, ALU.is_gt))
                    link(dve.tensor_scalar(view, view, -0.5, None, ALU.is_lt))
                    link(dve.tensor_tensor(wt, up, view, ALU.subtract))
                for c in range(C0):
                    link(dve.tensor_scalar(lnb_b[:, c, :], ident[:], 0.0, lnb[:, c:c + 1], ALU.mult, ALU.add))
                dve.sem_inc(sem("lnb_ready"), 1)
                dve.wait_ge(sem("bias0"), 1)
                dve.tensor_copy(bias0[:], bank[1][:, 0:D])
                for c in range(C0):
                    link(dve.tensor_scalar(pjw[:, c, 0:D], pjw[:, c, 0:D], lnw[:, c:c + 1], None, ALU.mult))
                link(dve.memset(pjw[:, :, D:D + 1], 1.0))
                dve.sem_inc(sem("pjw_ready"), 1)
                dve.wait_ge(sem("wsum"), 1)
                dve.tensor_copy(wsum[:], bank[2][:, 0:D])
                if 1 in layers:
                    dve.tensor_scalar(wdq[:], wdq[:], gq[0:QL, :], None, ALU.mult)
                    dve.tensor_scalar(wdkv[QL:P, :], wdkv[QL:P, :], gq[QL:P, :], None, ALU.mult)
                    link(dve.scalar_tensor_tensor(f1[:, 1, :], f1[:, 0, :], f1[:, 3, 0:1], f1[:, 1, :], ALU.mult, ALU.add))
                    for r in range(R1):
                        dve.tensor_scalar(wc1[:, r, :], wo1[:], f1[:, 2, r:r + 1], None, ALU.mult)
                    link(dve.tensor_scalar(b2b[:], ident[0:M1, :], 0.0, b2o[:], ALU.mult, ALU.add))
                    dve.sem_inc(sem("b2_ready"), 1)
                    dve.wait_ge(sem("bias1"), 1)
                    dve.tensor_tensor(bias1[:], bias1[:], bank[3][:, 0:D], ALU.add)

            @block.tensor
            def _(pe):
                pe.wait_ge(sem("ones"), 1)
                pe.wait_ge(sem("absum"), 1)
                pe.matmul(bank[0][:, 0:2], ones[:], absum[:], start=True, stop=True).then_inc(sem("abs_all"), 1)
                pe.wait_ge(sem("lnb_ready"), 1)
                for c in range(C0):
                    mm = pe.matmul(bank[1][:, 0:D], lnb_b[:, c, :], pjw[:, c, 0:D], start=c == 0, stop=c == C0 - 1)
                mm.then_inc(sem("bias0"), 1)
                pe.wait_ge(sem("pjw_ready"), 1)
                for c in range(C0):
                    mm = pe.matmul(bank[2][:, 0:D], ones[:], pjw[:, c, 0:D], start=c == 0, stop=c == C0 - 1)
                mm.then_inc(sem("wsum"), 1)
                if 1 in layers:
                    pe.wait_ge(sem("b2_ready"), 1)
                    pe.matmul(bank[3][:, 0:D], b2b[:], wout1[:], start=True, stop=True).then_inc(sem("bias1"), 1)

        nc.all_engine_barrier()
        sem.clear(nc)
        nc.all_engine_barrier()

        def norm_dve(dve, link, xb):
            for t in range(T):
                link.tell(dve.bn_stats(stats[:, t, :], xb[:, t, :]))
            link.wait()
            for t in range(T):
                link.tell(dve.bn_aggr(mv[:, t, :], stats[:, t, :]))
            link.wait()
            dve.tensor_scalar(ve[:], mv[:, :, 1], LN_EPS, None, ALU.add).then_inc(sem("var"), 1)
            dve.wait_ge(sem("rstd"), 1)
            for t in range(T):
                dve.tensor_scalar(xn[:, t, :], xb[:, t, :], mv[:, t, 0:1], rstd[:, t:t + 1],
                                  ALU.subtract, ALU.mult).then_inc(sem("xn"), 1)

        def norm_pool(pool):
            pool.wait_ge(sem("var"), 1)
            pool.tensor_tensor(rstd[:], ve[:], mhalf[:, 0:T], ALU.pow).then_inc(sem("rstd"), 1)

        def norm_pe(pe, ps):
            for t in range(T):
                pe.wait_ge(sem("xn"), t + 1)
                pe.transpose(ps[:, t * P:(t + 1) * P], xn[:, t, :], ident[:]).then_inc(sem("xnT_ps"), 1)

        def norm_act(act, ps):
            act.wait_ge(sem("xnT_ps"), T)
            act.activation(xnT[:], ps[:, 0:S], ACT.Copy).then_inc(sem("xnT"), 1)

        def layer0(b):
            with ExitStack() as lx:
                def lsb(name, shape, dt=F32):
                    return lx.enter_context(nc.sbuf_tensor(name, shape, dt))
                xwT = lsb("xwT", [P, S])
                nmax = lsb("nmax", [P, T])
                rsum = lsb("rsum", [P, T])
                rinv = lsb("rinv", [P, T])
                prob = lsb("prob", [P, T, S])
                probT = lsb("probT", [P, T, S])
                g = lsb("g", [P, C0, S])
                g2 = lsb("g2", [P, C0, S])
                x1 = lsb("x1", [P, T, D])
                y0 = lsb("y0", [P, T, D])
                s0 = lsb("s0", [P, T, 6])
                block = lx.enter_context(nc.Block())
                psX, psS, psT, psO, psH, psY = bank[0], bank[1], bank[2], bank[3], bank[4:6], bank[6:8]
                xb = x[:, bass.ds(b * T, T), :]

                @block.vector
                def _(dve):
                    link = Chain(dve, sem("dve_chain"))
                    norm_dve(dve, link, xb)
                    dve.wait_ge(sem("xnT"), 1)
                    dve.tensor_scalar(xwT[:], xnT[:], w_lrp[:], None, ALU.mult).then_inc(sem("xwT"), 1)
                    dve.wait_ge(sem("scores"), 1)
                    dve.tensor_reduce(nmax[:], psS[:].rearrange("p (t k) -> p t k", t=T), X, ALU.max, negate=True).then_inc(sem("nmax"), 1)
                    dve.wait_ge(sem("gelu"), C0)
                    dve.tensor_tensor(g2[:], g[:], g[:], ALU.mult).then_inc(sem("g2"), 1)
                    dve.wait_ge(sem("probT_ps"), 1)
                    dve.tensor_copy(probT[:], psT[:].rearrange("p (t k) -> p t k", t=T)).then_inc(sem("probT"), 1)
                    link(dve.reciprocal(rinv[:], rsum[:]))
                    dve.wait_ge(sem("pv"), T)
                    for t in range(T):
                        link(dve.scalar_tensor_tensor(x1[:, t, :], psO[:, t * D:(t + 1) * D], rinv[:, t:t + 1], xb[:, t, :], ALU.mult, ALU.add))
                    dve.wait_ge(sem("ffn"), T)
                    for t in range(T):
                        link(dve.tensor_scalar(s0[:, t, 0:2], psY[t][:, D:D + 2], 1.0 / H0, None, ALU.mult))
                    link(dve.tensor_tensor(s0[:, :, 2:3], s0[:, :, 0:1], s0[:, :, 0:1], ALU.mult))
                    link(dve.scalar_tensor_tensor(s0[:, :, 3:4], s0[:, :, 1:2], LN_EPS, s0[:, :, 2:3], ALU.add, ALU.subtract))
                    link(dve.tensor_scalar(s0[:, :, 4:5], s0[:, :, 0:1], -1.0, None, ALU.mult))
                    dve.sem_inc(sem("var2"), 1)
                    for t in range(T):
                        link(dve.scalar_tensor_tensor(y0[:, t, :], wsum[:], s0[:, t, 4:5], psY[t][:, 0:D], ALU.mult, ALU.add))
                    dve.wait_ge(sem("rstd2"), 1)
                    for t in range(T):
                        link(dve.scalar_tensor_tensor(y0[:, t, :], y0[:, t, :], s0[:, t, 5:6], x1[:, t, :], ALU.mult, ALU.add))
                        link(dve.tensor_tensor(xb[:, t, :], y0[:, t, :], bias0[:], ALU.add))

                @block.gpsimd
                def _(pool):
                    norm_pool(pool)
                    pool.wait_ge(sem("var2"), 1)
                    pool.tensor_tensor(s0[:, :, 5], s0[:, :, 3], mhalf[:, 0:T], ALU.pow).then_inc(sem("rstd2"), 1)

                @block.scalar
                def _(act):
                    norm_act(act, psX)
                    act.wait_ge(sem("nmax"), 1)
                    for t in range(T):
                        act.activation(prob[:, t, :], psS[:, t * S:(t + 1) * S], ACT.Exp, bias=nmax[:, t:t + 1],
                                       accum_out=rsum[:, t:t + 1]).then_inc(sem("prob"), 1)
                    for c in range(0, C0, 2):
                        act.wait_ge(sem("hidden"), c + 2)
                        act.activation(g[:, c:c + 2, :], psH[c // 2][:].rearrange("p (c k) -> p c k", c=2), ACT.Gelu).then_inc(sem("gelu"), 2)

                @block.tensor
                def _(pe):
                    norm_pe(pe, psX)
                    pe.wait_ge(sem("xnT"), 1)
                    pe.wait_ge(sem("xwT"), 1)
                    for t in range(T):
                        mm = pe.matmul(psS[:, t * S:(t + 1) * S], xwT[:, t * P:(t + 1) * P], xnT[:], start=True, stop=True)
                    mm.then_inc(sem("scores"), 1)
                    for c in range(C0):
                        pe.matmul(psH[c // 2][:, (c % 2) * S:(c % 2 + 1) * S], fcw[:, c * P:(c + 1) * P], xnT[:],
                                  start=True, stop=True).then_inc(sem("hidden"), 1)
                    pe.wait_ge(sem("prob"), T)
                    for t in range(T):
                        for k in range(T):
                            mm = pe.transpose(psT[:, k * S + t * P:k * S + (t + 1) * P], prob[:, t, k * P:(k + 1) * P], ident[:])
                    mm.then_inc(sem("probT_ps"), 1)
                    pe.wait_ge(sem("probT"), 1)
                    for t in range(T):
                        for k in range(T):
                            mm = pe.matmul(psO[:, t * D:(t + 1) * D], probT[:, k, t * P:(t + 1) * P], xn[:, k, :], start=k == 0, stop=k == T - 1)
                        mm.then_inc(sem("pv"), 1)
                    for t in range(T):
                        for c in range(C0):
                            pe.matmul(psY[t][:, 0:D + 1], g[:, c, t * P:(t + 1) * P], pjw[:, c, :], start=c == 0, stop=c == C0 - 1)
                        if t == 0:
                            pe.wait_ge(sem("g2"), 1)
                        for c in range(C0):
                            mm = pe.matmul(psY[t][:, D + 1:D + 2], g2[:, c, t * P:(t + 1) * P], ones[:, 0:1], start=c == 0, stop=c == C0 - 1)
                        mm.then_inc(sem("ffn"), 1)
            nc.all_engine_barrier()
            sem.clear(nc)
            nc.all_engine_barrier()

        def rank_dve(dve, link, v, n, gt, eq, rank):
            other = v.unsqueeze(2).broadcast_to([P, T, n, n])
            own = v.unsqueeze(3).broadcast_to([P, T, n, n])
            before = cst["before"][:].rearrange("p (a b) -> p a b", a=E2)[:, 0:n, 0:n]
            for t in range(T):
                link.tell(dve.tensor_tensor(gt[:, t], other[:, t], own[:, t], ALU.is_gt))
                link(dve.tensor_tensor(eq[:, t], other[:, t], own[:, t], ALU.is_equal))
                link(dve.tensor_tensor(eq[:, t], eq[:, t], before, ALU.mult))
                link(dve.tensor_tensor(gt[:, t], gt[:, t], eq[:, t], ALU.add))
                link(dve.tensor_reduce(rank[:, t, :], gt[:, t], X, ALU.add))

        def layer2(b):
            with ExitStack() as lx:
                def lsb(name, shape, dt=F32):
                    return lx.enter_context(nc.sbuf_tensor(name, shape, dt))
                SCALE = float(D) ** -0.5
                W = P + S
                qk = lsb("qk", [P, 2, S])
                v2 = lsb("v2", [P, T, D])
                sm = lsb("sm", [P, W])
                zero = lsb("zero", [P, W])
                nmax = lsb("nmax2", [P, T])
                rsum = lsb("rsum2", [P, T])
                rinv = lsb("rinv2", [P, T])
                alive = lsb("alive", [P, T])
                prob = lsb("prob2", [P, W])
                probT = lsb("probT2", [P, W])
                x1 = lsb("x12", [P, T, D])
                r = {n: lsb("r_" + n, [P, T, E2]) for n in ("e", "s", "sc", "rank", "m", "c")}
                pair = lsb("pair", [P, T, GR2, 6])
                gs = lsb("gs", [P, T, GR2])
                grank = lsb("grank", [P, T, GR2])
                gt = lsb("gt", [P, T, E2, E2])
                eq = lsb("eq", [P, T, E2, E2])
                ggt = lsb("ggt", [P, T, GR2, GR2])
                geq = lsb("geq", [P, T, GR2, GR2])
                csum = lsb("csum", [P, T])
                cT = lsb("cT", [E2, S])
                hr = lsb("hr", [P, EP2 + SP2, S])
                hc = lsb("hc", [P, EP2 + SP2, S])
                h2 = lsb("h2", [P, EP2 + SP2, S])
                block = lx.enter_context(nc.Block())
                psX, psQ, psV, psS = bank[0], bank[1], bank[2], bank[3]
                psT, psO = bank[1], bank[2]
                psG = bank[0]
                psU, psC, psD = bank[4:6], bank[6], bank[7]
                xb = x[:, bass.ds(b * T, T), :]
                NT2 = EP2 + SP2

                @block.vector
                def _(dve):
                    link = Chain(dve, sem("dve_chain"))
                    norm_dve(dve, link, xb)
                    dve.wait_ge(sem("values_ps"), 1)
                    dve.tensor_copy(v2[:], psV[:, 0:T * D].rearrange("p (t d) -> p t d", t=T)).then_inc(sem("values"), 1)
                    dve.wait_ge(sem("sig_e"), 1)
                    link(dve.tensor_scalar(r["e"][:], r["e"][:], 1.0, None, ALU.add))
                    link(dve.reciprocal(r["s"][:], r["e"][:]))
                    link(dve.tensor_tensor(r["sc"][:], r["s"][:], bias2[:].unsqueeze(1).broadcast_to([P, T, E2]), ALU.add))
                    sg = r["sc"][:].rearrange("p t (g k) -> p t g k", g=GR2)
                    link.tell(dve.tensor_tensor(pair[:, :, :, 0:3], sg[:, :, :, 0:3], sg[:, :, :, 1:4], ALU.add))
                    link.tell(dve.tensor_tensor(pair[:, :, :, 3:5], sg[:, :, :, 0:2], sg[:, :, :, 2:4], ALU.add))
                    link(dve.tensor_tensor(pair[:, :, :, 5:6], sg[:, :, :, 0:1], sg[:, :, :, 3:4], ALU.add))
                    link(dve.tensor_reduce(gs[:], pair[:], X, ALU.max))
                    rank_dve(dve, link, gs[:], GR2, ggt, geq, grank)
                    link(dve.tensor_scalar(grank[:], grank[:], 2.0, None, ALU.is_lt))
                    link(dve.tensor_tensor(r["m"][:].rearrange("p t (g k) -> p t g k", g=GR2), sg,
                                           grank[:].unsqueeze(3).broadcast_to([P, T, GR2, E2 // GR2]), ALU.mult))
                    dve.wait_ge(sem("scores"), 1)
                    for a, n in ((0, P), (2 * P, P)):
                        link.tell(dve.tensor_tensor(sm[:, a:a + n], psS[:, a:a + n], cst["causal"][:], ALU.mult))
                    link(dve.tensor_copy(sm[:, P:2 * P], psS[:, P:2 * P]))
                    link(dve.tensor_scalar(zero[:], sm[:], 0.0, -3e38, ALU.is_equal, ALU.mult))
                    link(dve.tensor_tensor(sm[:], zero[:], sm[:], ALU.add))
                    link.tell(dve.tensor_reduce(nmax[:, 0:1], sm[:, 0:P], X, ALU.max, negate=True))
                    link(dve.tensor_reduce(nmax[:, 1:2], sm[:, P:W], X, ALU.max, negate=True))
                    link(dve.tensor_scalar(alive[:], nmax[:], 1e38, None, ALU.is_lt))
                    dve.tensor_scalar(nmax[:], nmax[:], SCALE, None, ALU.mult).then_inc(sem("nmax"), 1)
                    rank_dve(dve, link, r["m"][:], E2, gt, eq, r["rank"])
                    link(dve.tensor_scalar(r["rank"][:], r["rank"][:], float(K2), None, ALU.is_lt))
                    link(dve.tensor_tensor(r["c"][:], r["rank"][:], r["s"][:], ALU.mult))
                    link(dve.tensor_reduce(csum[:], r["c"][:], X, ALU.add))
                    link(dve.tensor_scalar(csum[:], csum[:], 1e-20, None, ALU.add))
                    link(dve.reciprocal(csum[:], csum[:]))
                    for t in range(T):
                        dve.tensor_scalar(r["c"][:, t, :], r["c"][:, t, :], csum[:, t:t + 1], ROUTED_SCALE, ALU.mult, ALU.mult).then_inc(sem("combine"), 1)
                    dve.wait_ge(sem("cT_ps"), 1)
                    dve.tensor_copy(cT[:], psG[0:E2, 0:S]).then_inc(sem("cT"), 1)
                    dve.wait_ge(sem("probT_ps"), 1)
                    dve.tensor_copy(probT[:], psT[:, 0:W]).then_inc(sem("probT"), 1)
                    for c in range(EP2):
                        dve.wait_ge(sem("relu"), c + 1)
                        dve.wait_ge(sem("spread"), c + 1)
                        dve.tensor_tensor(hc[:, c, :], hr[:, c, :], psC[:, 0:S], ALU.mult).then_inc(sem("weighted"), 1)
                    link(dve.tensor_tensor(rinv[:], rsum[:], alive[:], ALU.mult))
                    link(dve.reciprocal(rinv[:], rinv[:]))
                    link(dve.tensor_tensor(rinv[:], rinv[:], alive[:], ALU.mult))
                    dve.wait_ge(sem("pv"), 1)
                    for t in range(T):
                        link(dve.scalar_tensor_tensor(x1[:, t, :], psO[:, t * D:(t + 1) * D], rinv[:, t:t + 1], xb[:, t, :], ALU.mult, ALU.add))
                    dve.wait_ge(sem("ffn"), 1)
                    dve.tensor_tensor(xb, x1[:], psD[:, 0:T * D].rearrange("p (t d) -> p t d", t=T), ALU.add)

                @block.gpsimd
                def _(pool):
                    norm_pool(pool)
                    for c in list(range(EP2, NT2)) + list(range(EP2)):
                        if c < EP2:
                            pool.wait_ge(sem("weighted"), c + 1)
                            pool.tensor_tensor(h2[:, c, :], hr[:, c, :], hc[:, c, :], ALU.mult).then_inc(sem("squared"), 1)
                        else:
                            pool.wait_ge(sem("relu_shared"), c - EP2 + 1)
                            pool.tensor_tensor(h2[:, c, :], hr[:, c, :], hr[:, c, :], ALU.mult).then_inc(sem("squared"), 1)

                @block.scalar
                def _(act):
                    norm_act(act, psX)
                    act.wait_ge(sem("qk_ps"), 1)
                    act.activation(qk[:], psQ[:].rearrange("p (a k) -> p a k", a=2), ACT.Copy).then_inc(sem("qk"), 1)
                    act.wait_ge(sem("logits"), 1)
                    act.activation(r["e"][:], psG[:, 0:T * E2].rearrange("p (t e) -> p t e", t=T), ACT.Exp, scale=-1.0).then_inc(sem("sig_e"), 1)
                    for c in list(range(EP2, NT2)) + list(range(EP2)):
                        n = (c - EP2) % NT2
                        act.wait_ge(sem("up"), n + 1)
                        act.activation(hr[:, c, :], psU[n % 2][:, 0:S], ACT.Relu).then_inc(sem("relu" if c < EP2 else "relu_shared"), 1)
                        if n == 2:
                            act.wait_ge(sem("nmax"), 1)
                            for t, (a, e) in enumerate(((0, P), (P, W))):
                                act.activation(prob[:, a:e], sm[:, a:e], ACT.Exp, bias=nmax[:, t:t + 1], scale=SCALE,
                                               accum_out=rsum[:, t:t + 1]).then_inc(sem("prob"), 1)

                @block.tensor
                def _(pe):
                    norm_pe(pe, psX)
                    pe.wait_ge(sem("xnT"), 1)
                    for n in range(2):
                        mm = pe.matmul(psQ[:, n * S:(n + 1) * S], wqkv2[:, n, :], xnT[:], start=True, stop=True)
                    mm.then_inc(sem("qk_ps"), 1)
                    for t in range(T):
                        mm = pe.matmul(psG[:, t * E2:(t + 1) * E2], xnT[:, t * P:(t + 1) * P], gate2[:], start=True, stop=True)
                    mm.then_inc(sem("logits"), 1)
                    for t in range(T):
                        mm = pe.matmul(psV[:, t * D:(t + 1) * D], xnT[:, t * P:(t + 1) * P], wqkv2[:, 2, :], start=True, stop=True)
                    mm.then_inc(sem("values_ps"), 1)
                    pe.wait_ge(sem("qk"), 1)
                    pe.matmul(psS[:, 0:P], qk[:, 0, 0:P], qk[:, 1, 0:P], start=True, stop=True)
                    pe.matmul(psS[:, P:W], qk[:, 0, P:S], qk[:, 1, :], start=True, stop=True).then_inc(sem("scores"), 1)

                    def up(c):
                        n = (c - EP2) % NT2
                        if n >= 2:
                            pe.wait_ge(sem("relu_shared"), min(n - 1, SP2))
                            if n - 1 > SP2:
                                pe.wait_ge(sem("relu"), n - 1 - SP2)
                        wt = up2[:, c * P:(c + 1) * P] if c < EP2 else sup2[:, (c - EP2) * P:(c - EP2 + 1) * P]
                        pe.matmul(psU[n % 2][:, 0:S], wt, xnT[:], start=True, stop=True).then_inc(sem("up"), 1)
                    for c in range(EP2, NT2):
                        up(c)
                    for c in range(2):
                        up(c)
                    pe.wait_ge(sem("prob"), T)
                    pe.wait_ge(sem("values"), 1)
                    for n in range(W // P):
                        mm = pe.transpose(psT[:, n * P:(n + 1) * P], prob[:, n * P:(n + 1) * P], ident[:])
                    mm.then_inc(sem("probT_ps"), 1)
                    pe.wait_ge(sem("combine"), T)
                    for t in range(T):
                        mm = pe.transpose(psG[0:E2, t * P:(t + 1) * P], r["c"][:, t, :], ident[:])
                    mm.then_inc(sem("cT_ps"), 1)
                    pe.wait_ge(sem("probT"), 1)
                    pe.matmul(psO[:, 0:D], probT[:, 0:P], v2[:, 0, :], start=True, stop=True)
                    pe.matmul(psO[:, D:2 * D], probT[:, P:2 * P], v2[:, 0, :], start=True, stop=False)
                    pe.matmul(psO[:, D:2 * D], probT[:, 2 * P:W], v2[:, 1, :], start=False, stop=True).then_inc(sem("pv"), 1)
                    pe.wait_ge(sem("cT"), 1)
                    for c in range(EP2):
                        if c + 2 < EP2:
                            up(c + 2)
                        if c >= 1:
                            pe.wait_ge(sem("weighted"), c)
                        pe.matmul(psC[:, 0:S], spread(c), cT[:], start=True, stop=True).then_inc(sem("spread"), 1)
                    pe.wait_ge(sem("squared"), NT2)
                    for t in range(T):
                        for c in range(NT2):
                            wt = down2[:, c, :] if c < EP2 else sdown2[:, c - EP2, :]
                            mm = pe.matmul(psD[:, t * D:(t + 1) * D], h2[:, c, t * P:(t + 1) * P], wt, start=c == 0, stop=c == NT2 - 1)
                    mm.then_inc(sem("ffn"), 1)
            nc.all_engine_barrier()
            sem.clear(nc)
            nc.all_engine_barrier()

        def spread(c):
            return cst["spread"][0:E2, c * P:(c + 1) * P]

        def layer3(b, wqkvg3, bg3, wo3, gate3, gb3, w13, b13, w23, b23, level3):
            with ExitStack() as lx:
                def lsb(name, shape, dt=F32):
                    return lx.enter_context(nc.sbuf_tensor(name, shape, dt))
                r = {n: lsb("t_" + n, [P, T, E3]) for n in ("l", "e", "p", "rank", "w")}
                oh = lsb("oh", [P, 2, T, E3])
                pos = lsb("pos", [P, 2, T, E3])
                tmx = lsb("tmx", [P, T])
                tsum = lsb("tsum", [P, T])
                gt = lsb("gt3", [P, T, E3, E3])
                eq = lsb("eq3", [P, T, E3, E3])
                wT = lsb("wT", [E3, S])
                hm = lsb("hm", [P, 2, FC3, S])
                acc = lsb("acc", [P, T, D])
                v3 = lsb("v3", [P, T, NH3 * DK3])
                edge = [lsb(f"edge{h}", [P, PAIRS, S // h]) for h in LEVELS + [P]]
                NB = 4
                qp = lsb("qp", [P, NB, 2, S])
                kk = lsb("kk", [P, NB, S])
                pT = lsb("pT", [P, NB, T, 2, P])
                pX = lsb("pX", [P, NB, 2, P])
                oT = lsb("oT", [P, 2, S])
                block = lx.enter_context(nc.Block())
                psX, psA, psL, psV, psO, psH, psY = bank[0], bank[1], bank[2:4], bank[4], bank[5], (bank[6], bank[0]), bank[7]
                xb = x[:, bass.ds(b * T, T), :]
                level = level3[:].rearrange("p (l c) -> p l c", l=len(LEVELS))
                STEPS = [0] + LEVELS + [P]
                NL, NSTEP = len(LEVELS), len(LEVELS) + 2
                COUPLES = PAIRS // 2
                ORDER = [(jj, n, m) for jj in range(COUPLES) for n in range(NSTEP) for m in range(2)]
                STEP_AT = {o: i for i, o in enumerate(ORDER)}
                KEYED = [o for o in ORDER if 1 <= o[1] <= NL]
                KEYED_AT = {o: i for i, o in enumerate(KEYED)}
                PIECES = [(e, c) for e in range(E3) for c in range(FC3 + 1)]
                FIRST = 2 * NSTEP
                piece_at = {}
                for n, p in enumerate(PIECES):
                    piece_at.setdefault(FIRST + n * (len(ORDER) - FIRST) // len(PIECES), []).append(p)
                PAIR_OF = lambda jj, m: 2 * jj + m

                def halves(a, h):
                    return a.rearrange("p (n two h) -> p n two h", two=2, h=h)

                @block.vector
                def _(dve):
                    link = Chain(dve, sem("dve_chain"))
                    norm_dve(dve, link, xb)

                    def route_logits():
                        dve.wait_ge(sem("logits"), 1)
                        link(dve.tensor_tensor(r["l"][:], psX[:, 0:T * E3].rearrange("p (t e) -> p t e", t=T),
                                               gb3[:].unsqueeze(1).broadcast_to([P, T, E3]), ALU.add))
                        link(dve.tensor_reduce(tmx[:], r["l"][:], X, ALU.max))
                        dve.tensor_tensor(r["l"][:], r["l"][:], tmx[:].unsqueeze(2).broadcast_to([P, T, E3]), ALU.subtract).then_inc(sem("shifted"), 1)

                    def route_rank():
                        dve.wait_ge(sem("exps"), 1)
                        link(dve.tensor_reduce(tsum[:], r["e"][:], X, ALU.add))
                        link(dve.reciprocal(tsum[:], tsum[:]))
                        link(dve.tensor_tensor(r["p"][:], r["e"][:], tsum[:].unsqueeze(2).broadcast_to([P, T, E3]), ALU.mult))
                        rank_dve(dve, link, r["p"][:], E3, gt, eq, r["rank"])
                        for c in range(2):
                            dve.tensor_scalar(oh[:, c], r["rank"][:], float(c), None, ALU.is_equal).then_inc(sem("onehot"), 1)

                    def route_keep():
                        dve.wait_ge(sem("places"), 1)
                        places = psX[:, 64:64 + 2 * T * E3].rearrange("p (c t e) -> p c t e", c=2, t=T)
                        link(dve.tensor_tensor(pos[:], places, carry[:].unsqueeze(2).broadcast_to([P, 2, T, E3]), ALU.add))
                        counts = psX[:, 128:128 + 2 * E3].rearrange("p (c e) -> p c e", c=2)
                        link.tell(dve.tensor_tensor(carry[:], carry[:], counts, ALU.add))
                        link(dve.tensor_scalar(pos[:], pos[:], float(CAP3), None, ALU.is_le))
                        link(dve.tensor_tensor(pos[:], pos[:], oh[:], ALU.mult))
                        link(dve.tensor_tensor(pos[:, 0], pos[:, 0], pos[:, 1], ALU.add))
                        dve.tensor_tensor(r["w"][:], pos[:, 0], r["p"][:], ALU.mult).then_inc(sem("weights"), 1)

                    def route_bias():
                        dve.wait_ge(sem("wT_ps"), 1)
                        dve.tensor_copy(wT[:], psX[0:E3, 256:256 + S]).then_inc(sem("wT"), 1)
                        dve.wait_ge(sem("bias_ps"), 1)
                        dve.tensor_tensor(acc[:], psY[:, 0:T * D].rearrange("p (t d) -> p t d", t=T), xb, ALU.add).then_inc(sem("expert_added"), 1)

                    def expert(e):
                        dve.wait_ge(sem("expert_ps"), e + 1)
                        dve.wait_ge(sem("expert_added"), e + 1)
                        for t in range(T):
                            ins = dve.scalar_tensor_tensor(acc[:, t, :], psY[:, t * D:(t + 1) * D], r["w"][:, t, e:e + 1], acc[:, t, :], ALU.mult, ALU.add)
                        ins.then_inc(sem("expert_added"), 1)

                    route_logits()
                    dve.wait_ge(sem("gates"), PAIRS)
                    for n in range(NL):
                        two = edge[n][:].rearrange("p j (n two) -> p j n two", two=2)
                        dve.tensor_tensor(edge[n + 1][:], two[:, :, :, 0], two[:, :, :, 1], ALU.mult).then_inc(sem("edges"), 1)
                        dve.wait_ge(sem("edges"), n + 1)

                    def step(i):
                        jj, n, m = ORDER[i]
                        j = PAIR_OF(jj, m)
                        s = j % NB
                        h = STEPS[n]
                        ps = psL[m]
                        dve.wait_ge(sem("scored"), i + 1)
                        if n == 0:
                            if j >= NB:
                                dve.wait_ge(sem("pv"), j - NB + 1)
                            dve.tensor_tensor(pT[:, s].rearrange("p t a q -> p (t a) q"), ps[:].rearrange("p (n q) -> p n q", n=4),
                                              ident[:].unsqueeze(1).broadcast_to([P, 4, P]), ALU.mult)
                            for a in range(2):
                                rows = slice(64 * a, 64 * a + 64)
                                ins = dve.tensor_tensor(qp[rows, s, a, :], qp[rows, s, a, :], edge[0][rows, j, :], ALU.mult)
                            ins.then_inc(sem("levelled"), 1)
                        elif h < P:
                            dve.wait_ge(sem("levelled"), STEP_AT[jj, n - 1, m] + 1)
                            right = halves(pT[:, s].rearrange("p t a q -> p (t a q)"), h)[:, :, 1, :]
                            dve.copy_predicated(right, level[:, n - 1, :].rearrange("p (c h) -> p c h", h=h),
                                                ps[:, 0:S].rearrange("p (c h) -> p c h", h=h))
                            two = edge[n - 1][:, j, :].rearrange("p (n two) -> p n two", two=2)
                            for a in range(2):
                                rows = slice(64 * a, 64 * a + 64)
                                q = halves(qp[rows, s, a, :], h)[:, :, 1, :]
                                ins = dve.tensor_tensor(q, q, two[rows, :, 0:1].broadcast_to([64, S // (2 * h), h]), ALU.mult)
                            ins.then_inc(sem("levelled"), 1)
                        else:
                            dve.tensor_copy(pX[:, s], ps[:, 0:2 * P].rearrange("p (a q) -> p a q", a=2)).then_inc(sem("levelled"), 1)

                    for i in range(len(ORDER)):
                        step(i)
                        if i == 3:
                            route_rank()
                        if i == 9:
                            route_keep()
                        if i == 13:
                            route_bias()
                        for e, c in piece_at.get(i - 2, []):
                            if c == FC3:
                                expert(e)
                    for i in range(len(ORDER) - 2, len(ORDER)):
                        for e, c in piece_at.get(i, []):
                            if c == FC3:
                                expert(e)
                    dve.wait_ge(sem("projected"), PAIRS)
                    dve.wait_ge(sem("expert_added"), E3 + 1)
                    dve.tensor_tensor(xb, acc[:], psV[:, 0:T * D].rearrange("p (t d) -> p t d", t=T), ALU.add)

                @block.gpsimd
                def _(pool):
                    for a in range(2):
                        pool.memset(qp[64 * (1 - a):64 * (1 - a) + 64, :, a, :], 0.0).then_inc(sem("zeros"), 1)
                        pool.wait_ge(sem("zeros"), a + 1)
                    norm_pool(pool)
                    for jj, n, m in KEYED:
                        j = PAIR_OF(jj, m)
                        h = STEPS[n]
                        pool.wait_ge(sem("scored"), STEP_AT[jj, n, m] + 1)
                        pool.wait_ge(sem("edges"), NL)
                        k = halves(kk[:, j % NB, :], h)[:, :, 0, :]
                        two = edge[n - 1][:, j, :].rearrange("p (n two) -> p n two", two=2)
                        if n >= 2:
                            pool.wait_ge(sem("keyed"), KEYED_AT[jj, n - 1, m] + 1)
                        pool.tensor_tensor(k, k, two[:, :, 1:2].broadcast_to([P, S // (2 * h), h]), ALU.mult).then_inc(sem("keyed"), 1)

                @block.scalar
                def _(act):
                    norm_act(act, psX)
                    act.wait_ge(sem("shifted"), 1)
                    act.activation(r["e"][:], r["l"][:], ACT.Exp).then_inc(sem("exps"), 1)
                    for j in range(PAIRS):
                        act.wait_ge(sem("gate_ps"), j + 1)
                        act.activation(edge[0][:, j, :], bank[2 + j % 2][:, 0:S], ACT.Sigmoid, bias=bg3[:, j:j + 1]).then_inc(sem("gates"), 1)

                    def queries_keys(j):
                        s = j % NB
                        act.wait_ge(sem("qk_ps"), j + 1)
                        if j == 0:
                            act.wait_ge(sem("zeros"), 2)
                        act.activation(kk[:, s, :], psA[:, S:2 * S], ACT.Copy)
                        for a in range(2):
                            rows = slice(64 * a, 64 * a + 64)
                            ins = act.activation(qp[rows, s, a, :], psA[rows, 0:S], ACT.Copy)
                        ins.then_inc(sem("qk"), 1)

                    def outputs(j):
                        act.wait_ge(sem("pv"), j + 1)
                        if j >= 2:
                            act.wait_ge(sem("projected"), j - 1)
                        act.activation(oT[:, j % 2, :], psO[:, 0:S], ACT.Copy).then_inc(sem("oT"), 1)

                    queries_keys(0)
                    queries_keys(1)
                    for n in range(4):
                        act.wait_ge(sem("values_ps"), n + 1)
                        act.activation(v3[:, n // 2, (n % 2) * 512:(n % 2 + 1) * 512], bank[4 + n][:], ACT.Copy).then_inc(sem("values"), 1)
                    for i, (jj, n, m) in enumerate(ORDER):
                        for e, c in piece_at.get(i, []):
                            if c < FC3:
                                if c == 0 and e >= 2:
                                    act.wait_ge(sem("expert_ps"), e - 1)
                                act.wait_ge(sem("hidden_ps"), e * FC3 + c + 1)
                                act.activation(hm[:, e % 2, c, :], psH[(e * FC3 + c) % 2][:, 0:S], ACT.Relu, bias=b13[:, e, c:c + 1]).then_inc(sem("hidden"), 1)
                        if n == NSTEP - 3 and jj + 1 < COUPLES:
                            queries_keys(PAIR_OF(jj + 1, m))
                        if n == 1 and jj >= 1:
                            outputs(PAIR_OF(jj - 1, m))
                    for m in range(2):
                        outputs(PAIR_OF(COUPLES - 1, m))

                @block.tensor
                def _(pe):
                    norm_pe(pe, psX)
                    pe.wait_ge(sem("xnT"), 1)
                    for t in range(T):
                        mm = pe.matmul(psX[:, t * E3:(t + 1) * E3], xnT[:, t * P:(t + 1) * P], gate3[:], start=True, stop=True)
                    mm.then_inc(sem("logits"), 1)
                    for j in range(PAIRS):
                        if j >= 2:
                            pe.wait_ge(sem("gates"), j - 1)
                        pe.matmul(bank[2 + j % 2][:, 0:S], wqkvg3[:, 3, j * P:(j + 1) * P], xnT[:], start=True, stop=True).then_inc(sem("gate_ps"), 1)

                    def queries_keys(j):
                        if j >= 1:
                            pe.wait_ge(sem("qk"), j)
                        for n in range(2):
                            mm = pe.matmul(psA[:, n * S:(n + 1) * S], wqkvg3[:, n, j * P:(j + 1) * P], xnT[:], start=True, stop=True)
                        mm.then_inc(sem("qk_ps"), 1)

                    queries_keys(0)
                    for n in range(2):
                        pe.matmul(bank[4 + n][:], xnT[:, 0:P], wqkvg3[:, 2, n * 512:(n + 1) * 512], start=True, stop=True).then_inc(sem("values_ps"), 1)
                    queries_keys(1)
                    for n in range(2, 4):
                        pe.matmul(bank[4 + n][:], xnT[:, P:S], wqkvg3[:, 2, (n % 2) * 512:(n % 2 + 1) * 512], start=True, stop=True).then_inc(sem("values_ps"), 1)

                    def places():
                        pe.wait_ge(sem("onehot"), 2)
                        for c in range(2):
                            a = 64 + c * T * E3
                            for t in range(T):
                                pe.matmul(psX[:, a + t * E3:a + (t + 1) * E3], cst["tri"][:], oh[:, c, t, :], start=True, stop=t == 0)
                                if t:
                                    pe.matmul(psX[:, a + t * E3:a + (t + 1) * E3], ones[:], oh[:, c, 0, :], start=False, stop=True)
                            for t in range(T):
                                mm = pe.matmul(psX[:, 128 + c * E3:128 + (c + 1) * E3], ones[:], oh[:, c, t, :], start=t == 0, stop=t == T - 1)
                        mm.then_inc(sem("places"), 1)

                    def weights_T():
                        pe.wait_ge(sem("weights"), 1)
                        for t in range(T):
                            mm = pe.transpose(psX[0:E3, 256 + t * P:256 + (t + 1) * P], r["w"][:, t, :], ident[:])
                        mm.then_inc(sem("wT_ps"), 1)

                    def bias():
                        pe.wait_ge(sem("wT"), 1)
                        pe.wait_ge(sem("values"), 4)
                        for t in range(T):
                            mm = pe.matmul(psY[:, t * D:(t + 1) * D], wT[:, t * P:(t + 1) * P], b23[:], start=True, stop=True)
                        mm.then_inc(sem("bias_ps"), 1)

                    def piece(e, c):
                        n = e * FC3 + c
                        if c < FC3:
                            if n >= 2:
                                pe.wait_ge(sem("hidden"), n - 1)
                            pe.matmul(psH[n % 2][:, 0:S], w13[:, e, c * P:(c + 1) * P], xnT[:], start=True, stop=True).then_inc(sem("hidden_ps"), 1)
                        else:
                            pe.wait_ge(sem("hidden"), (e + 1) * FC3)
                            pe.wait_ge(sem("expert_added"), e + 1)
                            for t in range(T):
                                for c4 in range(FC3):
                                    mm = pe.matmul(psY[:, t * D:(t + 1) * D], hm[:, e % 2, c4, t * P:(t + 1) * P], w23[:, e, c4, :], start=c4 == 0, stop=c4 == FC3 - 1)
                            mm.then_inc(sem("expert_ps"), 1)

                    def step(i):
                        jj, n, m = ORDER[i]
                        j = PAIR_OF(jj, m)
                        s = j % NB
                        h = STEPS[n]
                        ps = psL[m]
                        if n == 0:
                            pe.wait_ge(sem("qk"), j + 1)
                            if jj:
                                pe.wait_ge(sem("levelled"), STEP_AT[jj - 1, NSTEP - 1, m] + 1)
                            else:
                                pe.wait_ge(sem("gates"), PAIRS)
                            for t in range(T):
                                mm = pe.matmul(ps[:, t * S:(t + 1) * S], kk[:, s, t * P:(t + 1) * P], qp[:, s, :, t * P:(t + 1) * P], start=True, stop=True)
                        else:
                            pe.wait_ge(sem("levelled"), STEP_AT[jj, n - 1, m] + 1)
                            if n >= 2:
                                pe.wait_ge(sem("keyed"), KEYED_AT[jj, n - 1, m] + 1)
                            if h < P:
                                for t in range(T):
                                    q = qp[:, s, :, t * P:(t + 1) * P].rearrange("p a (c two h) -> p a c two h", two=2, h=h)[:, :, :, 1, :]
                                    mm = pe.matmul(ps[:, t * P:(t + 1) * P], kk[:, s, t * P:(t + 1) * P], q, start=True, stop=True)
                            else:
                                mm = pe.matmul(ps[:, 0:2 * P], kk[:, s, 0:P], qp[:, s, :, P:S], start=True, stop=True)
                        mm.then_inc(sem("scored"), 1)

                    def values(j):
                        s = j % NB
                        if j == 0:
                            pe.wait_ge(sem("values"), 4)
                        else:
                            pe.wait_ge(sem("oT"), j)
                        pe.wait_ge(sem("levelled"), STEP_AT[j // 2, NSTEP - 1, j % 2] + 1)
                        for a in range(2):
                            ch = slice(j * P + 64 * a, j * P + 64 * a + 64)
                            o = psO[64 * a:64 * a + 64, :]
                            pe.matmul(o[:, 0:P], v3[:, 0, ch], pT[:, s, 0, a, :], start=True, stop=True)
                            pe.matmul(o[:, P:S], v3[:, 1, ch], pT[:, s, 1, a, :], start=True, stop=False)
                            mm = pe.matmul(o[:, P:S], v3[:, 0, ch], pX[:, s, a, :], start=False, stop=True)
                        mm.then_inc(sem("pv"), 1)

                    def project(j):
                        pe.wait_ge(sem("oT"), j + 1)
                        for t in range(T):
                            mm = pe.matmul(psV[:, t * D:(t + 1) * D], oT[:, j % 2, t * P:(t + 1) * P], wo3[:, j, :],
                                           start=j == 0 and t == 0, stop=j == PAIRS - 1, skip_group_check=True)
                        mm.then_inc(sem("projected"), 1)

                    for i, (jj, n, m) in enumerate(ORDER):
                        step(i)
                        if i == 7:
                            places()
                        if i == 11:
                            weights_T()
                        if i == 13:
                            bias()
                        for e, c in piece_at.get(i, []):
                            piece(e, c)
                        if n == NSTEP - 3 and jj + 1 < COUPLES:
                            queries_keys(PAIR_OF(jj + 1, m))
                        if n == 1 and jj >= 1:
                            values(PAIR_OF(jj - 1, m))
                        if n == 2 and jj >= 1:
                            project(PAIR_OF(jj - 1, m))
                    for m in range(2):
                        values(PAIR_OF(COUPLES - 1, m))
                        project(PAIR_OF(COUPLES - 1, m))
            nc.all_engine_barrier()
            sem.clear(nc)
            nc.all_engine_barrier()

        def layer1(b):
            with ExitStack() as lx:
                def lsb(name, shape, dt=F32):
                    return lx.enter_context(nc.sbuf_tensor(name, shape, dt))
                SCALE = float(QK) ** -0.5
                NV = VH + 1
                cc = lsb("cc", [P, T, P])
                ss = lsb("ss", [P, T, 4])
                junk = lsb("junk", [P, T, P])
                ccT = lsb("ccT", [P, S])
                krs = lsb("krs", [P, T, ROPE])
                krt = lsb("krt", [P, T, ROPE])
                kr = lsb("kr", [P, T, ROPE])
                glog = lsb("glog", [P, T, 3])
                gate = lsb("gate", [P, 4, 3])
                imp = lsb("imp", [1, 5, S])
                top8 = lsb("top8", [1, 4, 8])
                selc = lsb("selc", [P, T])
                selm = lsb("selm", [P, T, KEEP])
                selT = lsb("selT", [P, KEEP])
                tok = lsb("tok", [P, 2, HG, QK])
                tb = lsb("tb", [P, 2, HG, ROPE])
                qT = lsb("qT", [QK, NH, S])
                kT = lsb("kT", [QK, 2, NH, S])
                kT2 = lsb("kT2", [QK, NH, KEEP])
                vv = lsb("vv", [P, 2, T, NH, NV])
                vs = lsb("vs", [KEEP, NH, NV])
                sc_ = lsb("sc_", [P, 2, 2, HG * S // 2])
                p2 = lsb("p2", [P, T, NH, KEEP])
                p2T = lsb("p2T", [KEEP, NH, S])
                mx = lsb("mx", [P, 2, HG])
                mx2 = lsb("mx2", [P, T, NH])
                pTT = lsb("pTT", [P, 2, T, HG, P])
                rr = lsb("rr", [P, 3, HG])
                oo = lsb("oo", [P, 3, HG, VH])
                ot = lsb("ot", [P, T, NH, VH])
                otT = lsb("otT", [P, 4, S])
                ri = lsb("ri", [P, R1, S])
                xr = lsb("xr", [P, T, D])
                block = lx.enter_context(nc.Block())
                xb = x[:, bass.ds(b * T, T), :]
                NS = QL + KVL + ROPE + 3
                psX, psP = bank[0], bank[1]
                PROJ = [(k, g, t) for k in ("q", "k1", "kw") for g in range(G1) for t in range(T)]
                UNITS = [(k, g, t) for g in range(G1) for t in range(T) for k in (0, 1)]
                BLOCKS = [sum(t + 1 for _, _, t in UNITS[:u]) for u in range(len(UNITS))]

                def turn(dve, link, to, tmp, ps, sn, cs, n, hg):
                    H2 = ROPE // 2
                    bc = lambda a: a.unsqueeze(1).broadcast_to([n, hg, a.shape[-1]])
                    link.tell(dve.tensor_tensor(tmp[:, :, 0:H2], ps[:, :, H2:ROPE], bc(sn[:, 0:H2]), ALU.mult))
                    link.tell(dve.tensor_tensor(tmp[:, :, H2:], ps[:, :, 0:H2], bc(sn[:, H2:]), ALU.mult))
                    link.tell(dve.tensor_copy(to[:, :, ROPE:], ps[:, :, ROPE:]))
                    link(dve.tensor_tensor(to[:, :, 0:ROPE], ps[:, :, 0:ROPE], bc(cs), ALU.mult))
                    dve.tensor_tensor(to[:, :, 0:ROPE], to[:, :, 0:ROPE], tmp, ALU.add).then_inc(sem("tok"), 1)

                def merge(dve, link, n):
                    g, t = divmod(n, T)
                    dve.wait_ge(sem("pv"), n + 1)
                    o = bank[7][:, 0:3 * HG * NV].rearrange("p (a h v) -> p a h v", a=3, h=HG)
                    link(dve.reciprocal(rr[:], o[:, :, :, VH]))
                    link(dve.tensor_tensor(rr[:], rr[:], gate[:, 3, :].unsqueeze(2).broadcast_to([P, 3, HG]), ALU.mult))
                    for a in range(3):
                        link.tell(dve.tensor_tensor(oo[:, a], o[:, a, :, 0:VH], rr[:, a].unsqueeze(2).broadcast_to([P, HG, VH]), ALU.mult))
                    link.wait()
                    link(dve.tensor_tensor(oo[:, 0], oo[:, 0], oo[:, 1], ALU.add))
                    dve.tensor_tensor(ot[:, t, g * HG:(g + 1) * HG, :], oo[:, 0], oo[:, 2], ALU.add).then_inc(sem("merged"), 1)

                @block.vector
                def _(dve):
                    link = Chain(dve, sem("dve_chain"))
                    norm_dve(dve, link, xb)
                    dve.wait_ge(sem("squares"), 2 * T)
                    link.tell(dve.tensor_scalar(ss[:, :, 2:3], ss[:, :, 0:1], 1.0 / QL, 1e-6, ALU.mult, ALU.add))
                    link(dve.tensor_scalar(ss[:, :, 3:4], ss[:, :, 1:2], 1.0 / KVL, 1e-6, ALU.mult, ALU.add))
                    dve.sem_inc(sem("ms"), 1)
                    dve.tensor_copy(glog[:], psX[:].rearrange("p (t c) -> p t c", t=T)[:, :, QL + KVL + ROPE:NS]).then_inc(sem("glog"), 1)
                    link.tell(dve.tensor_copy(krs[:], psX[:].rearrange("p (t c) -> p t c", t=T)[:, :, QL + KVL:QL + KVL + ROPE]))
                    dve.wait_ge(sem("rms"), 1)
                    for t in range(T):
                        dve.tensor_scalar(cc[:, t, 0:QL], psX[:, t * S:t * S + QL], ss[:, t, 0:1], None, ALU.mult)
                        dve.tensor_scalar(cc[:, t, QL:P], psX[:, t * S + QL:t * S + P], ss[:, t, 1:2], None, ALU.mult).then_inc(sem("latents"), 1)
                    link.wait()
                    link(dve.tensor_scalar(krs[:], krs[:], 1.0 / NH, None, ALU.mult))
                    H2 = ROPE // 2
                    link.tell(dve.tensor_tensor(krt[:, :, 0:H2], krs[:, :, H2:], sin[:, :, 0:H2], ALU.mult))
                    link.tell(dve.tensor_tensor(krt[:, :, H2:], krs[:, :, 0:H2], sin[:, :, H2:], ALU.mult))
                    link(dve.tensor_tensor(kr[:], krs[:], cos, ALU.mult))
                    link(dve.tensor_tensor(kr[:], kr[:], krt[:], ALU.add))
                    dve.wait_ge(sem("imp_ps"), 1)
                    link(dve.tensor_copy(imp[:, 0, :], psP[0:1, 0:S]))
                    for n in range(KEEP // 8):
                        link(dve.max(top8[:, n, :], imp[:, n, :]))
                        link(dve.match_replace(imp[:, n + 1, :], top8[:, n, :], imp[:, n, :], -3e38))
                    link(dve.tensor_scalar(imp[:, 0, :], imp[:, 4, :], -2.9e38, None, ALU.is_lt))
                    link(dve.memset(imp[:, 1, :], 0.0))
                    link(dve.tensor_tensor_scan(imp[:, 2, :], imp[:, 0, :], imp[:, 1, :], 0.0, ALU.add, ALU.add))
                    link(dve.tensor_tensor(imp[:, 3, :], imp[:, 2, :], imp[:, 0, :], ALU.mult))
                    dve.tensor_scalar(imp[:, 3, :], imp[:, 3, :], -1.0, None, ALU.add).then_inc(sem("places"), 1)
                    dve.wait_ge(sem("places_ps"), 1)
                    link(dve.tensor_copy(selc[:], psP[:, 0:T]))
                    for t in range(T):
                        dve.tensor_scalar(selm[:, t, :], cst["iota"][:], selc[:, t:t + 1], None, ALU.is_equal).then_inc(sem("selm"), 1)
                    dve.wait_ge(sem("gate_ps"), 1)
                    link(dve.tensor_scalar(gate[:, 0, :], psP[:, 64:67], 1.0 / S, None, ALU.mult))
                    link(dve.tensor_reduce(mx[:, 0, 0:1], gate[:, 0, :], X, ALU.max, negate=True))
                    dve.tensor_scalar(gate[:, 1, :], gate[:, 0, :], mx[:, 0, 0:1], None, ALU.add).then_inc(sem("gate_in"), 1)
                    dve.wait_ge(sem("gate_exp"), 1)
                    link(dve.tensor_reduce(mx[:, 0, 0:1], gate[:, 2, :], X, ALU.add))
                    link(dve.reciprocal(mx[:, 0, 0:1], mx[:, 0, 0:1]))
                    link(dve.tensor_scalar(gate[:, 3, :], gate[:, 2, :], mx[:, 0, 0:1], None, ALU.mult))
                    for n, (kind, g, t) in enumerate(PROJ):
                        m = n % 2
                        ps = bank[2 + m]
                        if n >= 2:
                            dve.wait_ge(sem("headsT_ps"), n - 1)
                        dve.wait_ge(sem("heads_ps"), n + 1)
                        if kind == "k1":
                            dve.tensor_copy(tok[:, m, :, 0:ROPE], kr[:, t, :].unsqueeze(1).broadcast_to([P, HG, ROPE]))
                            dve.tensor_copy(tok[:, m, :, ROPE:], ps[:, 0:HG * NOPE].rearrange("p (h c) -> p h c", h=HG)).then_inc(sem("tok"), 1)
                        else:
                            turn(dve, link, tok[:, m], tb[:, m], ps[:, 0:HG * QK].rearrange("p (h c) -> p h c", h=HG),
                                 sin[:, t, :], cos[:, t, :], P, HG)
                    for n in range(G1):
                        m = n % 2
                        dve.wait_ge(sem("heads_ps"), len(PROJ) + n + 1)
                        dve.wait_ge(sem("headsT_ps"), len(PROJ) + n - 1)
                        turn(dve, link, tok[0:KEEP, m], tb[0:KEEP, m], bank[2 + m][0:KEEP, 0:HG * QK].rearrange("p (h c) -> p h c", h=HG),
                             sin[0:KEEP, 0, :], cos[0:KEEP, 0, :], KEEP, HG)
                    for t in range(T):
                        dve.wait_ge(sem("scores2"), t + 1)
                        s2 = bank[2 + t][:].rearrange("p (h k) -> p h k", h=NH)
                        link(dve.tensor_reduce(mx2[:, t, :], s2, X, ALU.max))
                        dve.tensor_tensor(p2[:, t], s2, mx2[:, t, :].unsqueeze(2).broadcast_to([P, NH, KEEP]), ALU.subtract).then_inc(sem("shift2"), 1)
                    for u, (k, g, t) in enumerate(UNITS):
                        m = u % 2
                        kn = (t + 1) * P
                        dve.wait_ge(sem("scores"), u + 1)
                        if u >= 2:
                            dve.wait_ge(sem("probT_blk"), BLOCKS[u - 1])
                        for h2 in range(2):
                            sview = bank[2 + 2 * m + h2][:, 0:2 * kn].rearrange("p (h k) -> p h k", h=2)
                            hs = slice(2 * h2, 2 * h2 + 2)
                            link(dve.tensor_reduce(mx[:, m, hs], sview, X, ALU.max))
                            ins = dve.tensor_tensor(sc_[:, m, h2, 0:2 * kn].rearrange("p (h k) -> p h k", h=2), sview,
                                                    mx[:, m, hs].unsqueeze(2).broadcast_to([P, 2, kn]), ALU.subtract)
                        ins.then_inc(sem("shift"), 1)
                        if u >= 2 and u % 2 == 1:
                            merge(dve, link, u // 2 - 1)
                    merge(dve, link, len(UNITS) // 2 - 1)
                    dve.wait_ge(sem("out_ps"), 1)
                    link(dve.tensor_tensor(xr[:], bank[1][:, 0:T * D].rearrange("p (t d) -> p t d", t=T), xb, ALU.add))
                    dve.tensor_tensor(xb, xr[:], bias1[:].unsqueeze(1).broadcast_to([P, T, D]), ALU.add)

                @block.gpsimd
                def _(pool):
                    norm_pool(pool)
                    pool.memset(vv[:, :, :, :, VH:NV], 1.0).then_inc(sem("v_ones"), 1)
                    pool.memset(vs[:, :, VH:NV], 1.0).then_inc(sem("v_ones"), 1)
                    pool.wait_ge(sem("ms"), 1)
                    pool.tensor_tensor(ss[:, :, 0:2], ss[:, :, 2:4], mhalf[:, 0:4].rearrange("p (t a) -> p t a", t=T), ALU.pow).then_inc(sem("rms"), 1)

                @block.scalar
                def _(act):
                    norm_act(act, psX)
                    act.wait_ge(sem("small"), 1)
                    for t in range(T):
                        act.activation(junk[:, t, 0:QL], psX[:, t * S:t * S + QL], ACT.Square, accum_out=ss[:, t, 0:1]).then_inc(sem("squares"), 1)
                        act.activation(junk[:, t, QL:P], psX[:, t * S + QL:t * S + P], ACT.Square, accum_out=ss[:, t, 1:2]).then_inc(sem("squares"), 1)
                    act.wait_ge(sem("units_ps"), 1)
                    for r in range(R1):
                        act.activation(ri[:, r, :], bank[4][:, 0:S], ACT.Relu, scale=f1[:, 0, r:r + 1], bias=f1[:, 1, r:r + 1]).then_inc(sem("inner"), 1)
                    act.wait_ge(sem("latT_ps"), 1)
                    act.activation(ccT[:], bank[5][:, 0:S], ACT.Copy).then_inc(sem("latT"), 1)
                    act.wait_ge(sem("gate_in"), 1)
                    act.activation(gate[:, 2, :], gate[:, 1, :], ACT.Exp).then_inc(sem("gate_exp"), 1)
                    act.wait_ge(sem("sel_ps"), 1)
                    act.activation(selT[:], bank[6][:, 0:KEEP], ACT.Copy).then_inc(sem("selT"), 1)
                    for n in range(2 * T):
                        act.wait_ge(sem("values_ps"), n + 1)
                        act.activation(vv[:, n // T, n % T, :, 0:VH], bank[4 + n % 2][:].rearrange("p (h v) -> p h v", h=NH), ACT.Copy).then_inc(sem("values"), 1)
                    act.wait_ge(sem("values_ps"), 2 * T + 1)
                    act.activation(vs[:, :, 0:VH], bank[4][0:KEEP, :].rearrange("p (h v) -> p h v", h=NH), ACT.Copy).then_inc(sem("values"), 1)
                    for n, (kind, g, t) in enumerate(PROJ):
                        act.wait_ge(sem("headsT_ps"), n + 1)
                        dst = qT[:, g * HG:(g + 1) * HG] if kind == "q" else kT[:, int(kind == "kw"), g * HG:(g + 1) * HG]
                        act.activation(dst[:, :, t * P:(t + 1) * P], bank[5 + n % 2][0:QK, :].rearrange("p (h k) -> p h k", h=HG), ACT.Copy).then_inc(sem("headsT"), 1)
                    for n in range(G1):
                        act.wait_ge(sem("headsT_ps"), len(PROJ) + n + 1)
                        act.activation(kT2[:, n * HG:(n + 1) * HG, :], bank[5 + n % 2][0:QK, 0:HG * KEEP].rearrange("p (h k) -> p h k", h=HG), ACT.Copy).then_inc(sem("headsT"), 1)
                    for t in range(T):
                        act.wait_ge(sem("shift2"), t + 1)
                        act.activation(p2[:, t], p2[:, t], ACT.Exp, scale=SCALE).then_inc(sem("prob2"), 1)
                    for n in range(T * G1):
                        act.wait_ge(sem("prob2T_ps"), n + 1)
                        t, g = divmod(n, G1)
                        act.activation(p2T[:, g * HG:(g + 1) * HG, t * P:(t + 1) * P], bank[5 + n % 2][0:KEEP, :].rearrange("p (h q) -> p h q", h=HG), ACT.Copy).then_inc(sem("prob2T"), 1)
                    for u, (k, g, t) in enumerate(UNITS):
                        m = u % 2
                        kn = (t + 1) * P
                        act.wait_ge(sem("shift"), u + 1)
                        act.activation(sc_[:, m, :, 0:2 * kn], sc_[:, m, :, 0:2 * kn], ACT.Exp, scale=SCALE).then_inc(sem("prob"), 1)
                        for j in range(t + 1):
                            act.wait_ge(sem("probT_blk"), BLOCKS[u] + j + 1)
                            act.activation(pTT[:, m, j], bank[6][:].rearrange("p (h q) -> p h q", h=HG), ACT.Copy).then_inc(sem("probT"), 1)
                    for t in range(T):
                        act.wait_ge(sem("otT_ps"), t + 1)
                        act.activation(otT[:, :, t * P:(t + 1) * P], bank[2 + t][:].rearrange("p (c q) -> p c q", c=4), ACT.Copy).then_inc(sem("otT"), 1)

                @block.tensor
                def _(pe):
                    norm_pe(pe, psX)
                    pe.wait_ge(sem("xnT"), 1)
                    for t in range(T):
                        mm = pe.matmul(psX[:, t * S:t * S + NS], xnT[:, t * P:(t + 1) * P], small1[:], start=True, stop=True)
                    mm.then_inc(sem("small"), 1)
                    pe.matmul(psP[0:1, 0:S], wimp[:], xnT[:], start=True, stop=True).then_inc(sem("imp_ps"), 1)
                    pe.matmul(bank[4][:, 0:S], win[:].rearrange("p m j -> p (m j)"), xnT[:], start=True, stop=True).then_inc(sem("units_ps"), 1)
                    pe.wait_ge(sem("latents"), T)
                    for t in range(T):
                        mm = pe.transpose(bank[5][:, t * P:(t + 1) * P], cc[:, t, :], ident[:])
                    mm.then_inc(sem("latT_ps"), 1)
                    pe.wait_ge(sem("places"), 1)
                    for t in range(T):
                        mm = pe.matmul(psP[:, t:t + 1], imp[0:1, 3, t * P:(t + 1) * P], ones[0:1, 0:1], start=True, stop=True)
                    mm.then_inc(sem("places_ps"), 1)
                    pe.wait_ge(sem("glog"), 1)
                    pe.wait_ge(sem("selm"), T)
                    for t in range(T):
                        mm = pe.matmul(psP[:, 64:67], ones[:], glog[:, t, :], start=t == 0, stop=t == T - 1)
                    mm.then_inc(sem("gate_ps"), 1)
                    for t in range(T):
                        mm = pe.matmul(bank[6][:, 0:KEEP], xn[:, t, :], selm[:, t, :], start=t == 0, stop=t == T - 1)
                    mm.then_inc(sem("sel_ps"), 1)
                    pe.wait_ge(sem("latT"), 1)
                    pe.wait_ge(sem("inner"), R1)
                    pe.wait_ge(sem("selT"), 1)
                    HV = NH * VH
                    for n in range(2 * T + 1):
                        k, t = divmod(n, T)
                        if n >= 2:
                            pe.wait_ge(sem("values"), n - 1)
                        if k == 0:
                            mm = pe.matmul(bank[4 + n % 2][:], ccT[QL:P, t * P:(t + 1) * P], wdkv[QL:P, HV:], start=True, stop=True)
                        elif k == 1:
                            mm = pe.matmul(bank[4 + n % 2][:], xnT[:, t * P:(t + 1) * P], winv[:], start=True, stop=True)
                        else:
                            mm = pe.matmul(bank[4][0:KEEP, :], selT[:], selv[:], start=True, stop=True)
                        mm.then_inc(sem("values_ps"), 1)

                    def project(n):
                        ps = bank[2 + n % 2]
                        if n >= 2:
                            pe.wait_ge(sem("tok"), n - 1)
                        if n >= len(PROJ):
                            g = n - len(PROJ)
                            mm = pe.matmul(ps[0:KEEP, 0:HG * QK], selT[:], selk[:, g * HG * QK:(g + 1) * HG * QK], start=True, stop=True)
                        else:
                            kind, g, t = PROJ[n]
                            if kind == "q":
                                mm = pe.matmul(ps[:, 0:HG * QK], ccT[0:QL, t * P:(t + 1) * P], wdq[:, g * HG * QK:(g + 1) * HG * QK], start=True, stop=True)
                            elif kind == "k1":
                                mm = pe.matmul(ps[:, 0:HG * NOPE], ccT[QL:P, t * P:(t + 1) * P], wdkv[QL:P, g * HG * NOPE:(g + 1) * HG * NOPE], start=True, stop=True)
                            else:
                                mm = pe.matmul(ps[:, 0:HG * QK], xnT[:, t * P:(t + 1) * P], wink[:, g * HG * QK:(g + 1) * HG * QK], start=True, stop=True)
                        mm.then_inc(sem("heads_ps"), 1)

                    def turn_heads(n):
                        pe.wait_ge(sem("tok"), n + 1)
                        if n >= 2:
                            pe.wait_ge(sem("headsT"), n - 1)
                        else:
                            pe.wait_ge(sem("values"), 2 * T + 1)
                        rows = P if n < len(PROJ) else KEEP
                        for h in range(HG):
                            mm = pe.transpose(bank[5 + n % 2][0:QK, h * rows:(h + 1) * rows], tok[0:rows, n % 2, h, :], ident[0:rows, 0:rows])
                        mm.then_inc(sem("headsT_ps"), 1)

                    NP_ = len(PROJ) + G1
                    project(0)
                    for n in range(NP_):
                        if n + 1 < NP_:
                            project(n + 1)
                        turn_heads(n)
                    pe.wait_ge(sem("headsT"), NP_)
                    for t in range(T):
                        for h in range(NH):
                            mm = pe.matmul(bank[2 + t][:, h * KEEP:(h + 1) * KEEP], qT[:, h, t * P:(t + 1) * P], kT2[:, h, :], start=True, stop=True)
                        mm.then_inc(sem("scores2"), 1)
                    for n in range(T * G1):
                        t, g = divmod(n, G1)
                        pe.wait_ge(sem("prob2"), t + 1)
                        if n >= 2:
                            pe.wait_ge(sem("prob2T"), n - 1)
                        for h in range(HG):
                            mm = pe.transpose(bank[5 + n % 2][0:KEEP, h * P:(h + 1) * P], p2[:, t, g * HG + h, :], ident[:])
                        mm.then_inc(sem("prob2T_ps"), 1)
                    pe.wait_ge(sem("prob2T"), T * G1)
                    pe.wait_ge(sem("v_ones"), 2)

                    def scores(u):
                        k, g, t = UNITS[u]
                        m = u % 2
                        kn = (t + 1) * P
                        if u >= 2:
                            pe.wait_ge(sem("shift"), u - 1)
                        for h in range(HG):
                            ps = bank[2 + 2 * m + h // 2]
                            o = (h % 2) * kn
                            pe.matmul(ps[:, o:o + kn], qT[:, g * HG + h, t * P:(t + 1) * P], kT[:, k, g * HG + h, 0:kn], start=True, stop=False, skip_group_check=True)
                            mm = pe.matmul(ps[:, o + t * P:o + kn], ident[:], cst["negmask"][:], start=False, stop=True, skip_group_check=True)
                        mm.then_inc(sem("scores"), 1)

                    nblk = 0
                    scores(0)
                    for u, (k, g, t) in enumerate(UNITS):
                        m = u % 2
                        kn = (t + 1) * P
                        if u + 1 < len(UNITS):
                            scores(u + 1)
                        pe.wait_ge(sem("prob"), u + 1)
                        for j in range(t + 1):
                            if nblk >= 1:
                                pe.wait_ge(sem("probT"), nblk)
                            nblk += 1
                            for h in range(HG):
                                a = (h % 2) * kn + j * P
                                mm = pe.transpose(bank[6][:, h * P:(h + 1) * P], sc_[:, m, h // 2, a:a + P], ident[:])
                            mm.then_inc(sem("probT_blk"), 1)
                        pe.wait_ge(sem("probT"), nblk)
                        if k == 0 and u >= 2:
                            pe.wait_ge(sem("merged"), u // 2)
                        o = bank[7][:, 0:3 * HG * NV].rearrange("p (a h v) -> p a h v", a=3, h=HG)
                        for h in range(HG):
                            for j in range(t + 1):
                                mm = pe.matmul(o[:, 2 * k, h, :], pTT[:, m, j, h, :], vv[:, k, j, g * HG + h, :], start=j == 0, stop=j == t)
                        if k == 1:
                            for h in range(HG):
                                mm = pe.matmul(o[:, 1, h, :], p2T[:, g * HG + h, t * P:(t + 1) * P], vs[:, g * HG + h, :], start=True, stop=True)
                            mm.then_inc(sem("pv"), 1)
                    pe.wait_ge(sem("merged"), G1 * T)
                    for t in range(T):
                        for c in range(4):
                            mm = pe.transpose(bank[2 + t][:, c * P:(c + 1) * P], ot[:, t, c * HG:(c + 1) * HG, :].rearrange("p h v -> p (h v)"), ident[:])
                        mm.then_inc(sem("otT_ps"), 1)
                    pe.wait_ge(sem("otT"), T)
                    for t in range(T):
                        for c in range(4):
                            pe.matmul(bank[1][:, t * D:(t + 1) * D], otT[:, c, t * P:(t + 1) * P], wpj[:, c, :], start=c == 0, stop=False)
                        for r in range(R1):
                            mm = pe.matmul(bank[1][:, t * D:(t + 1) * D], ri[:, r, t * P:(t + 1) * P], wc1[:, r, :], start=False, stop=r == R1 - 1)
                    mm.then_inc(sem("out_ps"), 1)
            nc.all_engine_barrier()
            sem.clear(nc)
            nc.all_engine_barrier()

        bodies = {0: layer0, 1: layer1, 2: layer2}
        for n in (0, 1):
            if n in layers:
                with nc.Fori(0, B) as b:
                    bodies[n](b)

        wqkvg3 = sb("wqkvg3", [P, 4, NH3 * DK3])
        bg3 = sb("bg3", [P, PAIRS])
        wo3 = sb("wo3", [P, PAIRS, D])
        gate3 = sb("gate3", [P, E3])
        gb3 = sb("gb3", [P, E3])
        w13 = sb("w13", [P, E3, F3])
        b13 = sb("b13", [P, E3, FC3])
        w23 = sb("w23", [P, E3, FC3, D])
        b23 = sb("b23", [E3, D])
        level3 = sb("level3", [P, len(LEVELS) * 2 * T * P // 2], U32)
        s_load3 = ctx.enter_context(nc.semaphore("loaded3"))
        loads3 = [(wqkvg3[:, n, :], w[name]) for n, name in enumerate(("W_q", "W_k", "W_v", "W_gate"))]
        loads3 += [
            (bg3[:], w["b_gateT"]),
            (wo3[:], w["W_o"].rearrange("(c p) d -> p c d", p=P)),
            (gate3[:], w["gate3T"]),
            (gb3[:], w["gb3_rep"]),
            (w13[:], w["W13"].rearrange("e d f -> d e f")),
            (b13[:], w["b13T"]),
            (w23[:], w["W23"].rearrange("e (c p) d -> p e c d", p=P)),
            (b23[:], w["b23"]),
            (level3[:], w["c_level"]),
        ]
        if 3 in layers:
            with nc.Block() as block:
                @block.sync
                def _(sp):
                    for dst, src in loads3:
                        sp.dma_start(dst, src).then_inc(s_load3, 16)
        if 2 in layers:
            with nc.Fori(0, B) as b:
                layer2(b)
        if 3 in layers:
            with nc.Block() as block:
                @block.tensor
                def _(pe):
                    pe.wait_ge(s_load3, 16 * len(loads3))

                @block.vector
                def _(dve):
                    dve.wait_ge(s_load3, 16 * len(loads3))

                @block.scalar
                def _(act):
                    act.wait_ge(s_load3, 16 * len(loads3))
            with nc.Fori(0, B) as b:
                layer3(b, wqkvg3, bg3, wo3, gate3, gb3, w13, b13, w23, b23, level3)

        with nc.Block() as block:
            @block.sync
            def _(sp):
                sp.dma_start(out.rearrange("b (t p) d -> p (b t) d", p=P), x[:]).then_inc(s_out, 16)
                sp.wait_ge(s_out, 16)


def host_layout(i):
    t = lambda a: np.ascontiguousarray(a)
    L = {}
    L["x"] = i["L0_attn_x"]
    L["w_lhs"], L["w_rhs"] = i["L0_attn_w_lhs"], i["L0_attn_w_rhs"]
    L["W_fcT"] = t(i["L0_ffn_W_fc"].T)
    L["W_projT"] = t(i["L0_ffn_W_proj"].T)
    L["ln_wT"], L["ln_bT"] = t(i["L0_ffn_ln_w"].reshape(C0, P).T), t(i["L0_ffn_ln_b"].reshape(C0, P).T)
    for n in ("w_cq", "w_ckv", "w_krope", "w_gate", "g_qnorm", "g_kvnorm", "w_dk_nope", "w_dv", "w_imp", "w_selv", "w_winv", "w_proj"):
        L[n] = i["L1_attn_" + n]
    nope = i["L1_attn_w_dq_nope"].reshape(QL, NH, NOPE)
    rope = i["L1_attn_w_dq_rope"].reshape(QL, NH, ROPE)
    L["w_dq"] = t(np.concatenate([rope, nope], 2).reshape(QL, NH * QK))
    for n in ("w_selk", "w_wink"):
        a = i["L1_attn_" + n].reshape(D, NH, QK)
        L[n] = t(np.concatenate([a[..., NOPE:], a[..., :NOPE]], 2).reshape(D, NH * QK))
    for n in ("W1", "b1", "W2", "b2", "Wout"):
        L[n] = i["L1_ffn_" + n]
    L["bin_rep"] = t(np.repeat(i["L1_ffn_bin_"], J1)[:, None])
    L["Win_rep"] = t(np.repeat(i["L1_ffn_Win"][:, :, None], J1, axis=2))
    L["Wout_rep"] = t(np.repeat(i["L1_ffn_Wout"], J1, axis=0))
    L["bout_rep"] = t(np.broadcast_to(i["L1_ffn_bout"], (P, D)))
    for n in "QKV":
        L[f"W{n}T"] = t(i[f"L2_attn_W{n}"].T)
    L["gate2T"] = t(i["L2_ffn_gate_w"].T)
    L["bias2_rep"] = t(np.broadcast_to(i["L2_ffn_bias_e"], (P, E2)))
    L["up2T"] = t(i["L2_ffn_up_w"].transpose(2, 0, 1).reshape(D, E2 * I2))
    L["down2"] = t(i["L2_ffn_down_w"].transpose(0, 2, 1).reshape(E2 * I2, D))
    L["sup2T"] = t(i["L2_ffn_shared_up"].T)
    L["sdown2T"] = t(i["L2_ffn_shared_down"].T)
    for n in ("W_q", "W_k", "W_v", "W_gate", "W_o"):
        L[n] = i["L3_attn_" + n]
    L["b_gateT"] = t(i["L3_attn_b_gate"].reshape(PAIRS, P).T)
    L["gate3T"] = t(i["L3_ffn_gate_w"].T)
    L["gb3_rep"] = t(np.broadcast_to(i["L3_ffn_gate_b"], (P, E3)))
    L["b13T"] = t(i["L3_ffn_b1"].reshape(E3, FC3, P).transpose(2, 0, 1))
    L["W13"], L["W23"], L["b23"] = i["L3_ffn_W1"], i["L3_ffn_W2"], i["L3_ffn_b2"]
    for n, a in constants().items():
        L["c_" + n] = a
    return L


def kernel(**inputs):
    import concourse.bacc as _bacc
    from concourse.bass_utils import run_bass_kernel_spmd as _run

    arrays = {f"in_{n}": np.ascontiguousarray(a) for n, a in host_layout({k: np.asarray(v) for k, v in inputs.items()}).items()}
    nc = _bacc.Bacc("TRN2", target_bir_lowering=False, num_devices=1)
    w = {n[3:]: nc.dram_tensor(n, a.shape, mybir.dt.from_np(a.dtype), kind="ExternalInput").ap() for n, a in arrays.items()}
    out = nc.dram_tensor("out_x", (B, S, D), F32, kind="ExternalOutput").ap()
    program(nc, w, out)
    r = _run(nc, [arrays], core_ids=[0])
    return r.results[0]["out_x"]
```

```python
from contextlib import ExitStack

import numpy as np

import concourse.bass as bass
from concourse import mybir

F32 = mybir.dt.float32
BF16 = mybir.dt.bfloat16
U32 = mybir.dt.uint32
ALU = mybir.AluOpType
ACT = mybir.ActivationFunctionType
X = mybir.AxisListType.X

P = 128
B, S, D = 8, 256, 128
T = S // P
PB = 2
PT = PB * T
LN_EPS = 1e-5

H0 = 512
C0 = H0 // P
NH, NOPE, ROPE, VH = 16, 32, 64, 32
QK = NOPE + ROPE
QL, KVL = 96, 32
KEEP = 32
HG = 4
G1 = NH // HG
M1, INNER = 64, 16
J1 = P // M1
R1 = INNER // J1
NEG = -1e30
E2, K2, GR2, I2, SH2 = 16, 4, 4, 64, 256
EP2 = E2 * I2 // P
SP2 = SH2 // P
ROUTED_SCALE = 2.5
NH3, DK3 = 16, 64
PAIRS = NH3 * DK3 // P
LEVELS = [1, 2, 4, 8, 16, 32, 64]
E3, F3 = 8, 512
FC3 = F3 // P
CAP3 = -(-5 * 4 * 256 * 2 // (4 * E3))


def constants():
    i = np.arange(P)
    out = {}
    out["ident"] = np.eye(P, dtype=np.float32)
    out["causal"] = (i[:, None] >= i[None, :]).astype(np.float32)
    out["tri"] = (i[:, None] <= i[None, :]).astype(np.float32)
    out["negmask"] = np.where(i[:, None] >= i[None, :], 0.0, NEG).astype(np.float32)
    out["iota"] = np.broadcast_to(np.arange(1, KEEP + 1, dtype=np.float32), (P, KEEP)).copy()
    e = np.arange(E2)
    out["before"] = np.broadcast_to((e[None, :] < e[:, None]).astype(np.float32).reshape(-1), (P, E2 * E2)).copy()
    spread = np.zeros((3, E2, EP2, P), np.float32)
    for p in range(EP2):
        for m in range(P):
            spread[:, (P // I2) * p + m // I2, p, m] = 1
    out["spread"] = spread.reshape(3 * E2, -1)
    level = np.zeros((P, len(LEVELS), 2 * T, P // 2), np.uint32)
    for n, h in enumerate(LEVELS):
        right = i[(i // h) % 2 == 1]
        level[:, n, :, :] = (((i[:, None] // h) % 2 == 0) & (i[:, None] // (2 * h) == right[None, :] // (2 * h)))[:, None, :]
    out["level"] = level.reshape(P, -1)
    f = (np.float32(1.0) / np.float32(10000.0) ** (np.arange(0, ROPE, 2, dtype=np.float32) / np.float32(ROPE))).astype(np.float32)
    a = np.outer(np.arange(S, dtype=np.float32), f).astype(np.float32)
    c, s = np.cos(a), np.sin(a)
    out["cosT"] = np.concatenate([c.T, c.T, np.ones((P - ROPE, S))]).astype(np.float32)
    out["sinT"] = np.concatenate([s.T, -s.T]).astype(np.float32)
    return out


class Chain:

    def __init__(self, eng, sem):
        self.eng, self.sem, self.n = eng, sem, 0

    def tell(self, ins):
        self.n += 1
        ins.then_inc(self.sem, 1)

    def wait(self):
        self.eng.wait_ge(self.sem, self.n)

    def __call__(self, ins):
        self.tell(ins)
        self.wait()


class Sems:

    def __init__(self, nc, ctx, count):
        self.free = [ctx.enter_context(nc.semaphore(f"s{n}")) for n in range(count)]
        self.named = {}

    def __call__(self, name):
        if name not in self.named:
            self.named[name] = self.free[len(self.named)]
        return self.named[name]

    def clear(self, nc):
        engines = (nc.sync, nc.scalar, nc.vector, nc.tensor, nc.gpsimd)
        for n, s in enumerate(self.named.values()):
            engines[n % len(engines)].sem_clear(s)
        self.named = {}


def program(nc, w, out, layers=(0, 1, 2, 3)):
    ctx = ExitStack()
    with ctx:
        def sb(name, shape, dt=F32):
            return ctx.enter_context(nc.sbuf_tensor(name, shape, dt))

        def pb(name):
            return ctx.enter_context(nc.psum_tensor(name, [P, 512], F32))

        bank = [pb(f"bank{n}") for n in range(8)]
        sem = Sems(nc, ctx, 60)
        s_load = ctx.enter_context(nc.semaphore("loaded"))
        s_load12 = ctx.enter_context(nc.semaphore("loaded12"))
        s_out = ctx.enter_context(nc.semaphore("stored"))

        x = sb("x", [P, (B + PB) * T, D])
        cst = {}
        for name, width, dt in (("ident", P, F32), ("causal", P, F32), ("tri", P, F32), ("negmask", P, F32),
                                ("iota", KEEP, F32), ("before", E2 * E2, F32),
                                ("cosT", S, F32)):
            cst[name] = sb("c_" + name, [P, width], dt)
        spread_b = sb("spread_b", [3 * E2, EP2 * P], BF16)
        ident = cst["ident"]
        cosT = cst["cosT"]
        sinT = sb("sinT", [ROPE, S])
        ident_b = sb("ident_b", [P, P], BF16)
        ones = sb("ones", [P, P])
        mhalf = sb("mhalf", [P, 8])

        xn = sb("xn", [P, PT, D])
        xnT_all = sb("xnT", [P, PT * P])
        xnT = xnT_all[:, 0:S]
        stats = sb("stats", [P, PT, 6])
        mv = sb("mv", [P, PT, 2])
        ve = sb("ve", [P, PT])
        rstd = sb("rstd", [P, PT])

        w_lr = sb("w_lr", [P, 2])
        w_lrp = sb("w_lrp", [P, 1])
        fcw = sb("fcw", [P, H0])
        pjw = sb("pjw", [P, C0, D + 1])
        lnw = sb("lnw", [P, C0])
        lnb = sb("lnb", [P, C0])
        wsum = sb("wsum", [P, D])
        bias0 = sb("bias0", [P, D])
        small1 = sb("small1", [P, QL + KVL + 3])
        wkr = sb("wkr", [P, ROPE])
        wdq = sb("wdq", [QL, NH * P])
        gq = sb("gq", [P, 1])
        wdv = sb("wdv", [P, NH * VH])
        wimp = sb("wimp", [P, 1])
        selk = sb("selk", [P, NH * QK])
        selv = sb("selv", [P, NH * VH])
        wink = sb("wink", [P, NH * QK])
        winv = sb("winv", [P, NH * VH])
        wpj = sb("wpj", [P, 4, D])
        win = sb("win", [P, M1, J1])
        f1 = sb("f1", [P, 4, R1])
        wo1 = sb("wo1", [P, D])
        wc1 = sb("wc1", [P, R1, D])
        b2o = sb("b2o", [M1, 1])
        b2b = sb("b2b", [M1, P])
        wout1 = sb("wout1", [M1, D])
        bias1 = sb("bias1", [P, D])
        wqkv2 = sb("wqkv2", [P, 3, D])
        gate2 = sb("gate2", [P, E2])
        bias2 = sb("bias2", [P, E2])
        up2 = sb("up2", [P, E2 * I2])
        down2 = sb("down2", [P, EP2, D])
        sup2 = sb("sup2", [P, SH2])
        sdown2 = sb("sdown2", [P, SP2, D])
        carry = sb("carry", [P, 2, E3])

        loads, loads12 = [], []

        def load(dst, src):
            loads.append((dst, src))

        def load12(dst, src):
            loads12.append((dst, src))

        load(x[:, 0:B * T, :], w["x"].rearrange("b (t p) d -> p (b t) d", p=P))
        for name in cst:
            (load if name == "ident" else load12)(cst[name][:], w["c_" + name])
        load12(sinT[:], w["c_sinT"])
        load(w_lr[:, 0:1], w["w_lhs"].rearrange("a b d -> d (a b)"))
        load(w_lr[:, 1:2], w["w_rhs"].rearrange("a b d -> d (a b)"))
        load(fcw[:], w["W_fcT"])
        load(pjw[:, :, 0:D], w["W_projT"].rearrange("(c p) d -> p c d", p=P))
        load(lnw[:], w["ln_wT"])
        load(lnb[:], w["ln_bT"])
        if 1 in layers:
            for a, n, name in ((0, QL, "w_cq"), (QL, KVL, "w_ckv"), (QL + KVL, 3, "w_gate")):
                load12(small1[:, a:a + n], w[name])
            load12(wkr[:], w["w_krope"])
            load12(wdq[:].rearrange("p (h c) -> p h c", h=NH)[:, :, 0:QK], w["w_dq"])
            load12(gq[0:QL, :], w["g_qnorm"].rearrange("(p a) -> p a", a=1))
            load12(gq[QL:P, :], w["g_kvnorm"].rearrange("(p a) -> p a", a=1))
            load12(wdv[QL:P, :], w["w_dv"])
            load12(wimp[:], w["w_imp"])
            load12(selk[:], w["w_selk"])
            load12(selv[:], w["w_selv"])
            load12(wink[:], w["w_wink"])
            load12(winv[:], w["w_winv"])
            load12(wpj[:], w["w_proj"].rearrange("(c p) d -> p c d", p=P))
            load12(win[:], w["Win_rep"])
            load12(f1[:, 0, :], w["W1"].rearrange("m (j r) -> (m j) r", j=J1))
            load12(f1[:, 1, :], w["b1"].rearrange("m (j r) -> (m j) r", j=J1))
            load12(f1[:, 2, :], w["W2"].rearrange("m (j r) -> (m j) r", j=J1))
            load12(f1[:, 3, 0:1], w["bin_rep"])
            load12(wo1[:], w["Wout_rep"])
            load12(b2o[:], w["b2"].rearrange("(p a) -> p a", a=1))
            load12(wout1[:], w["Wout"])
            load12(bias1[:], w["bout_rep"])
        if 2 in layers:
            for n, name in enumerate(("WQT", "WKT", "WVT")):
                load12(wqkv2[:, n, :], w[name])
            load12(gate2[:], w["gate2T"])
            load12(bias2[:], w["bias2_rep"])
            load12(up2[:], w["up2T"])
            load12(down2[:], w["down2"].rearrange("(c p) d -> p c d", p=P))
            load12(sup2[:], w["sup2T"])
            load12(sdown2[:], w["sdown2T"].rearrange("(c p) d -> p c d", p=P))
        prep = ExitStack()
        wdqT = prep.enter_context(nc.sbuf_tensor("wdqT", [NOPE, NH * QL], F32))
        wdkT = prep.enter_context(nc.sbuf_tensor("wdkT", [NOPE, NH * KVL], F32))
        spread_f = prep.enter_context(nc.sbuf_tensor("spread_f", [3 * E2, EP2 * P], F32))
        load12(spread_f[:], w["c_spread"])
        if 1 in layers:
            load12(wdqT[:], w["w_dqT"])
            load12(wdkT[:], w["w_dkT"])
        with ExitStack() as sx:
            absum = sx.enter_context(nc.sbuf_tensor("absum", [P, 2], F32))
            gamma = sx.enter_context(nc.sbuf_tensor("gamma", [P, 4], F32))
            tern = sx.enter_context(nc.sbuf_tensor("tern", [P, 3, H0], F32))
            lnb_b = sx.enter_context(nc.sbuf_tensor("lnb_b", [P, C0, P], F32))
            block = sx.enter_context(nc.Block())

            @block.sync
            def _(sp):
                for n, (dst, src) in enumerate(loads):
                    if n % 2 == 0:
                        sp.dma_start(dst, src).then_inc(s_load, 16)
                for dst, src in loads12:
                    sp.dma_start(dst, src).then_inc(s_load12, 16)

            @block.scalar
            def _(act):
                for n, (dst, src) in enumerate(loads):
                    if n % 2 == 1:
                        act.dma_start(dst, src).then_inc(s_load, 16)

            @block.gpsimd
            def _(pool):
                pool.memset(ones[:], 1.0).then_inc(sem("ones"), 1)
                pool.memset(mhalf[:], -0.5)
                pool.memset(carry[:], 0.0)
                pool.memset(x[:, B * T:, :], 0.0)

            @block.vector
            def _(dve):
                link = Chain(dve, sem("dve_chain"))
                dve.wait_ge(s_load, 16 * len(loads))
                dve.tensor_reduce(absum[:, 0:1], fcw[:], X, ALU.add, apply_absolute_value=True)
                dve.tensor_reduce(absum[:, 1:2], pjw[:, :, 0:D], mybir.AxisListType.XY, ALU.add,
                                  apply_absolute_value=True).then_inc(sem("absum"), 1)
                link(dve.tensor_tensor(w_lrp[:], w_lr[:, 0:1], w_lr[:, 1:2], ALU.mult))
                dve.wait_ge(sem("abs_all"), 1)
                dve.tensor_copy(ident_b[:], ident[:])
                link(dve.tensor_scalar(gamma[:, 0:2], bank[0][:, 0:2], 1.0 / (H0 * D), 1e-6, ALU.mult, ALU.add))
                link(dve.reciprocal(gamma[:, 2:4], gamma[:, 0:2]))
                for n, (wt, view) in enumerate(((fcw[:], tern[:, 0, :]), (pjw[:, :, 0:D], tern[:, 0, :].rearrange("p (c d) -> p c d", c=C0)))):
                    up = tern[:, 1, :] if n == 0 else tern[:, 1, :].rearrange("p (c d) -> p c d", c=C0)
                    link(dve.tensor_scalar(view, wt, gamma[:, 2 + n:3 + n], None, ALU.mult))
                    link(dve.tensor_scalar(up, view, 0.5, None, ALU.is_gt))
                    link(dve.tensor_scalar(view, view, -0.5, None, ALU.is_lt))
                    link(dve.tensor_tensor(wt, up, view, ALU.subtract))
                for c in range(C0):
                    link(dve.tensor_scalar(lnb_b[:, c, :], ident[:], 0.0, lnb[:, c:c + 1], ALU.mult, ALU.add))
                dve.sem_inc(sem("lnb_ready"), 1)
                dve.wait_ge(sem("bias0"), 1)
                dve.tensor_copy(bias0[:], bank[1][:, 0:D])
                for c in range(C0):
                    link(dve.tensor_scalar(pjw[:, c, 0:D], pjw[:, c, 0:D], lnw[:, c:c + 1], None, ALU.mult))
                link(dve.memset(pjw[:, :, D:D + 1], 1.0))
                dve.sem_inc(sem("pjw_ready"), 1)
                dve.wait_ge(sem("wsum"), 1)
                dve.tensor_copy(wsum[:], bank[2][:, 0:D])

            @block.tensor
            def _(pe):
                pe.wait_ge(sem("ones"), 1)
                pe.wait_ge(sem("absum"), 1)
                pe.matmul(bank[0][:, 0:2], ones[:], absum[:], start=True, stop=True).then_inc(sem("abs_all"), 1)
                pe.wait_ge(sem("lnb_ready"), 1)
                for c in range(C0):
                    mm = pe.matmul(bank[1][:, 0:D], lnb_b[:, c, :], pjw[:, c, 0:D], start=c == 0, stop=c == C0 - 1)
                mm.then_inc(sem("bias0"), 1)
                pe.wait_ge(sem("pjw_ready"), 1)
                for c in range(C0):
                    mm = pe.matmul(bank[2][:, 0:D], ones[:], pjw[:, c, 0:D], start=c == 0, stop=c == C0 - 1)
                mm.then_inc(sem("wsum"), 1)

        nc.all_engine_barrier()
        sem.clear(nc)
        nc.all_engine_barrier()

        def norm_stats(dve, link, xb, tiles=T):
            for t in range(tiles):
                link.tell(dve.bn_stats(stats[:, t, :], xb[:, t, :]))
            link.wait()
            for t in range(tiles):
                link.tell(dve.bn_aggr(mv[:, t, :], stats[:, t, :]))
            link.wait()
            dve.tensor_scalar(ve[:, 0:tiles], mv[:, 0:tiles, 1], LN_EPS, None, ALU.add).then_inc(sem("var"), 1)

        def norm_scale(dve, xb, tiles=T):
            dve.wait_ge(sem("rstd"), 1)
            for t in range(tiles):
                dve.tensor_scalar(xn[:, t, :], xb[:, t, :], mv[:, t, 0:1], rstd[:, t:t + 1],
                                  ALU.subtract, ALU.mult).then_inc(sem("xn"), 1)

        def norm_dve(dve, link, xb, tiles=T):
            norm_stats(dve, link, xb, tiles)
            norm_scale(dve, xb, tiles)

        def norm_pool(pool, tiles=T):
            pool.wait_ge(sem("var"), 1)
            pool.tensor_tensor(rstd[:, 0:tiles], ve[:, 0:tiles], mhalf[:, 0:tiles], ALU.pow).then_inc(sem("rstd"), 1)

        def norm_pe(pe, ps, tiles=T):
            for t in range(tiles):
                pe.wait_ge(sem("xn"), t + 1)
                mm = pe.transpose(ps[:, t * P:(t + 1) * P], xn[:, t, :], ident[:])
            mm.then_inc(sem("xnT_ps"), 1)

        def norm_act(act, ps, tiles=T, dst=None):
            act.wait_ge(sem("xnT_ps"), 1)
            act.activation(xnT_all[:, 0:tiles * P] if dst is None else dst, ps[:, 0:tiles * P], ACT.Copy).then_inc(sem("xnT"), 1)

        def prepare():
            with nc.Block() as block:
                @block.vector
                def _(dve):
                    link = Chain(dve, sem("dve_chain"))
                    dve.wait_ge(s_load12, 16 * len(loads12))
                    dve.tensor_copy(spread_b[:], spread_f[:]).then_inc(sem("loaded"), 1)
                    if 1 in layers:
                        dve.wait_ge(sem("absorbed"), 1)
                        link(dve.tensor_copy(wdq[:].rearrange("p (h c) -> p h c", h=NH)[:, :, QK:], bank[4][0:QL, :].rearrange("p (h c) -> p h c", h=NH)))
                        dve.tensor_scalar(wdq[:], wdq[:], gq[0:QL, :], float(QK) ** -0.5, ALU.mult, ALU.mult)
                        dve.tensor_scalar(wdv[QL:P, :], wdv[QL:P, :], gq[QL:P, :], None, ALU.mult)
                        link(dve.scalar_tensor_tensor(f1[:, 1, :], f1[:, 0, :], f1[:, 3, 0:1], f1[:, 1, :], ALU.mult, ALU.add))
                        for r in range(R1):
                            dve.tensor_scalar(wc1[:, r, :], wo1[:], f1[:, 2, r:r + 1], None, ALU.mult)
                        link(dve.tensor_scalar(b2b[:], ident[0:M1, :], 0.0, b2o[:], ALU.mult, ALU.add))
                        dve.sem_inc(sem("b2_ready"), 1)
                        dve.wait_ge(sem("bias1"), 1)
                        dve.tensor_tensor(bias1[:], bias1[:], bank[3][:, 0:D], ALU.add)

                @block.tensor
                def _(pe):
                    pe.wait_ge(sem("loaded"), 1)
                    if 1 in layers:
                        for h in range(NH):
                            mm = pe.matmul(bank[4][0:QL, h * KVL:(h + 1) * KVL], wdqT[:, h * QL:(h + 1) * QL], wdkT[:, h * KVL:(h + 1) * KVL], start=True, stop=True)
                        mm.then_inc(sem("absorbed"), 1)
                    if 1 in layers:
                        pe.wait_ge(sem("b2_ready"), 1)
                        pe.matmul(bank[3][:, 0:D], b2b[:], wout1[:], start=True, stop=True).then_inc(sem("bias1"), 1)
            nc.all_engine_barrier()
            sem.clear(nc)
            nc.all_engine_barrier()

        def norm_block(xb, tiles):
            with nc.Block() as block:
                @block.vector
                def _(dve):
                    norm_dve(dve, Chain(dve, sem("dve_chain")), xb, tiles)

                @block.gpsimd
                def _(pool):
                    norm_pool(pool, tiles)

                @block.scalar
                def _(act):
                    norm_act(act, bank[0], tiles)

                @block.tensor
                def _(pe):
                    norm_pe(pe, bank[0], tiles)
            nc.all_engine_barrier()
            sem.clear(nc)
            nc.all_engine_barrier()

        def layer0(b):
            with ExitStack() as lx:
                def lsb(name, shape, dt=F32):
                    return lx.enter_context(nc.sbuf_tensor(name, shape, dt))
                xwT = lsb("xwT", [P, PT * P])
                nmax = lsb("nmax", [P, PB, T])
                rsum = lsb("rsum", [P, PT])
                rinv = lsb("rinv", [P, PT])
                prob = lsb("prob", [P, PB, T, S])
                probT = lsb("probT", [P, PB, T, S])
                g = lsb("g", [P, C0, PT * P])
                g2 = lsb("g2", [P, C0, PT * P])
                x1 = lsb("x1", [P, PT, D])
                y0 = lsb("y0", [P, PT, D])
                s0 = lsb("s0", [P, PT, 6])
                block = lx.enter_context(nc.Block())
                psO, psS, psH = bank[0], bank[1:3], bank[3:7]
                psT, psY, psX = bank[1:3], (bank[7], bank[3]), bank[1]
                xb = x[:, bass.ds(b * PT, PT), :]
                x_next = x[:, bass.ds(b * PT + PT, PT), :]

                @block.vector
                def _(dve):
                    link = Chain(dve, sem("dve_chain"))
                    dve.tensor_scalar(xwT[:], xnT_all[:], w_lrp[:], None, ALU.mult).then_inc(sem("xwT"), 1)
                    for i in range(PB):
                        dve.wait_ge(sem("scores"), i + 1)
                        dve.tensor_reduce(nmax[:, i, :], psS[i][:].rearrange("p (t k) -> p t k", t=T), X, ALU.max, negate=True).then_inc(sem("nmax"), 1)
                    for i in range(PB):
                        dve.wait_ge(sem("probT_ps"), i + 1)
                        dve.tensor_copy(probT[:, i], psT[i][:].rearrange("p (t k) -> p t k", t=T)).then_inc(sem("probT"), 1)
                    link(dve.reciprocal(rinv[:], rsum[:]))
                    for c in range(C0):
                        dve.wait_ge(sem("gelu"), c + 1)
                        dve.tensor_tensor(g2[:, c, :], g[:, c, :], g[:, c, :], ALU.mult).then_inc(sem("g2"), 1)
                    dve.wait_ge(sem("pv"), 1)
                    for t in range(PT):
                        link.tell(dve.scalar_tensor_tensor(x1[:, t, :], psO[:, t * D:(t + 1) * D], rinv[:, t:t + 1], xb[:, t, :], ALU.mult, ALU.add))
                    link.wait()
                    norm_dve(dve, link, x_next, PT)
                    for i in range(PB):
                        dve.wait_ge(sem("ffn"), i + 1)
                        tt = slice(i * T, (i + 1) * T)
                        y = psY[i][:, 0:T * (D + 2)].rearrange("p (t d) -> p t d", t=T)
                        link(dve.tensor_scalar(s0[:, tt, 0:2], y[:, :, D:D + 2], 1.0 / H0, None, ALU.mult))
                        link(dve.tensor_tensor(s0[:, tt, 2:3], s0[:, tt, 0:1], s0[:, tt, 0:1], ALU.mult))
                        link(dve.scalar_tensor_tensor(s0[:, tt, 3:4], s0[:, tt, 1:2], LN_EPS, s0[:, tt, 2:3], ALU.add, ALU.subtract))
                        dve.tensor_scalar(s0[:, tt, 4:5], s0[:, tt, 0:1], -1.0, None, ALU.mult).then_inc(sem("var2"), 1)
                        dve.wait_ge(sem("var2"), i + 1)
                        for t in range(T):
                            link.tell(dve.scalar_tensor_tensor(y0[:, i * T + t, :], wsum[:], s0[:, i * T + t, 4:5], y[:, t, 0:D], ALU.mult, ALU.add))
                        link.wait()
                    dve.wait_ge(sem("rstd2"), PB)
                    for t in range(PT):
                        link.tell(dve.scalar_tensor_tensor(y0[:, t, :], y0[:, t, :], s0[:, t, 5:6], x1[:, t, :], ALU.mult, ALU.add))
                    link.wait()
                    dve.tensor_tensor(xb, y0[:], bias0[:].unsqueeze(1).broadcast_to([P, PT, D]), ALU.add)

                @block.gpsimd
                def _(pool):
                    norm_pool(pool, PT)
                    for i in range(PB):
                        tt = slice(i * T, (i + 1) * T)
                        pool.wait_ge(sem("var2"), i + 1)
                        pool.tensor_tensor(s0[:, tt, 5], s0[:, tt, 3], mhalf[:, 0:T], ALU.pow).then_inc(sem("rstd2"), 1)

                @block.scalar
                def _(act):
                    for i in range(PB):
                        act.wait_ge(sem("nmax"), i + 1)
                        for t in range(T):
                            ins = act.activation(prob[:, i, t, :], psS[i][:, t * S:(t + 1) * S], ACT.Exp, bias=nmax[:, i, t:t + 1],
                                                 accum_out=rsum[:, i * T + t:i * T + t + 1])
                        ins.then_inc(sem("prob"), 1)
                    for c in range(C0):
                        act.wait_ge(sem("hidden"), c + 1)
                        act.activation(g[:, c, :], psH[c][:], ACT.Gelu).then_inc(sem("gelu"), 1)
                    norm_act(act, psX, PT)

                @block.tensor
                def _(pe):
                    def hidden(c):
                        pe.matmul(psH[c][:], fcw[:, c * P:(c + 1) * P], xnT_all[:], start=True, stop=True).then_inc(sem("hidden"), 1)

                    hidden(0)
                    pe.wait_ge(sem("xwT"), 1)
                    for i in range(PB):
                        for t in range(T):
                            o = i * S + t * P
                            mm = pe.matmul(psS[i][:, t * S:(t + 1) * S], xwT[:, o:o + P], xnT_all[:, i * S:(i + 1) * S], start=True, stop=True)
                        mm.then_inc(sem("scores"), 1)
                    for c in range(1, C0):
                        hidden(c)
                    for i in range(PB):
                        pe.wait_ge(sem("prob"), i + 1)
                        for t in range(T):
                            for k in range(T):
                                mm = pe.transpose(psT[i][:, k * S + t * P:k * S + (t + 1) * P], prob[:, i, t, k * P:(k + 1) * P], ident[:])
                        mm.then_inc(sem("probT_ps"), 1)
                    for i in range(PB):
                        pe.wait_ge(sem("probT"), i + 1)
                        for t in range(T):
                            o = (i * T + t) * D
                            for k in range(T):
                                mm = pe.matmul(psO[:, o:o + D], probT[:, i, k, t * P:(t + 1) * P], xn[:, i * T + k, :], start=k == 0, stop=k == T - 1)
                    mm.then_inc(sem("pv"), 1)
                    pe.wait_ge(sem("gelu"), C0)
                    for i in range(PB):
                        for t in range(T):
                            tok = slice((i * T + t) * P, (i * T + t + 1) * P)
                            y = psY[i][:, t * (D + 2):(t + 1) * (D + 2)]
                            for c in range(C0):
                                pe.matmul(y[:, 0:D + 1], g[:, c, tok], pjw[:, c, :], start=c == 0, stop=c == C0 - 1)
                            pe.wait_ge(sem("g2"), C0)
                            for c in range(C0):
                                mm = pe.matmul(y[:, D + 1:D + 2], g2[:, c, tok], ones[:, 0:1], start=c == 0, stop=c == C0 - 1)
                        mm.then_inc(sem("ffn"), 1)
                    norm_pe(pe, psX, PT)
            nc.all_engine_barrier()
            sem.clear(nc)
            nc.all_engine_barrier()

        def rank_dve(dve, link, v, n, gt, eq, rank, tiles=T):
            other = v.unsqueeze(2).broadcast_to([P, tiles, n, n])
            own = v.unsqueeze(3).broadcast_to([P, tiles, n, n])
            before = cst["before"][:].rearrange("p (a b) -> p a b", a=E2)[:, 0:n, 0:n]
            link.tell(dve.tensor_tensor(gt[:], other, own, ALU.is_gt))
            link(dve.tensor_tensor(eq[:], other, own, ALU.is_equal))
            link(dve.tensor_tensor(eq[:], eq[:], before.unsqueeze(1).broadcast_to([P, tiles, n, n]), ALU.mult))
            link(dve.tensor_tensor(gt[:], gt[:], eq[:], ALU.add))
            link(dve.tensor_reduce(rank[:], gt[:], X, ALU.add))

        def layer2(b):
            with ExitStack() as lx:
                def lsb(name, shape, dt=F32):
                    return lx.enter_context(nc.sbuf_tensor(name, shape, dt))
                SCALE = float(D) ** -0.5
                W = P + S
                NT2 = EP2 + SP2
                RING = 4
                q2 = lsb("q2", [P, PT * P])
                k2 = lsb("k2", [P, PT * P])
                v2 = lsb("v2", [P, PT, D])
                sm = lsb("sm", [P, PB, W])
                zero = lsb("zero", [P, PB, W])
                nmax = lsb("nmax2", [P, PB, T])
                rsum = lsb("rsum2", [P, PB, T])
                rinv = lsb("rinv2", [P, PB, T])
                alive = lsb("alive", [P, PB, T])
                prob = lsb("prob2", [P, PB, W])
                probT = lsb("probT2", [P, PB, W])
                x1 = lsb("x12", [P, PT, D])
                r = {n: lsb("r_" + n, [P, PT, E2]) for n in ("e", "s", "sc", "rank", "m", "c", "rest")}
                pair = lsb("pair", [P, PT, GR2, 6])
                gs = lsb("gs", [P, PT, GR2])
                grank = lsb("grank", [P, PT, GR2])
                gt = lsb("gt", [P, PT, E2, E2])
                eq = lsb("eq", [P, PT, E2, E2])
                ggt = lsb("ggt", [P, PT, GR2, GR2])
                geq = lsb("geq", [P, PT, GR2, GR2])
                csum = lsb("csum", [P, PT])
                parts = lsb("parts", [P, PT, 3, E2], BF16)
                cT = lsb("cT", [3 * E2, PT * P], BF16)
                hr = lsb("hr", [P, RING, PT * P])
                hc = lsb("hc", [P, RING, PT * P])
                h2 = lsb("h2", [P, RING, PT * P])
                block = lx.enter_context(nc.Block())
                psQ, psK, psV, psG = bank[1], bank[2], bank[3], bank[4]
                psS = bank[5:7]
                psT, psO = bank[1:3], bank[3]
                psX = bank[3]
                psP = bank[6]
                psU, psC, psD = (bank[0], bank[7]), bank[5:7], bank[4]
                xb = x[:, bass.ds(b * PT, PT), :]
                x_next = x[:, bass.ds(b * PT + PT, PT), :]
                TILES = list(range(EP2, NT2)) + list(range(EP2))

                @block.vector
                def _(dve):
                    link = Chain(dve, sem("dve_chain"))
                    dve.wait_ge(sem("values_ps"), 1)
                    dve.tensor_copy(v2[:], psV[:].rearrange("p (t d) -> p t d", t=PT)).then_inc(sem("values"), 1)
                    dve.wait_ge(sem("sig_e"), 1)
                    link(dve.tensor_scalar(r["e"][:], r["e"][:], 1.0, None, ALU.add))
                    link(dve.reciprocal(r["s"][:], r["e"][:]))
                    link(dve.tensor_tensor(r["sc"][:], r["s"][:], bias2[:].unsqueeze(1).broadcast_to([P, PT, E2]), ALU.add))
                    sg = r["sc"][:].rearrange("p t (g k) -> p t g k", g=GR2)
                    link.tell(dve.tensor_tensor(pair[:, :, :, 0:3], sg[:, :, :, 0:3], sg[:, :, :, 1:4], ALU.add))
                    link.tell(dve.tensor_tensor(pair[:, :, :, 3:5], sg[:, :, :, 0:2], sg[:, :, :, 2:4], ALU.add))
                    link(dve.tensor_tensor(pair[:, :, :, 5:6], sg[:, :, :, 0:1], sg[:, :, :, 3:4], ALU.add))
                    link(dve.tensor_reduce(gs[:], pair[:], X, ALU.max))
                    for i in range(PB):
                        dve.wait_ge(sem("scores"), i + 1)
                        link.tell(dve.tensor_tensor(sm[:, i, 0:P], psS[i][:, 0:P], cst["causal"][:], ALU.mult))
                        link.tell(dve.tensor_tensor(sm[:, i, 2 * P:], psS[i][:, 2 * P:W], cst["causal"][:], ALU.mult))
                        link(dve.tensor_copy(sm[:, i, P:2 * P], psS[i][:, P:2 * P]))
                    link(dve.tensor_scalar(zero[:], sm[:], 0.0, -3e38, ALU.is_equal, ALU.mult))
                    link(dve.tensor_tensor(sm[:], zero[:], sm[:], ALU.add))
                    link.tell(dve.tensor_reduce(nmax[:, :, 0:1], sm[:, :, 0:P], X, ALU.max, negate=True))
                    link(dve.tensor_reduce(nmax[:, :, 1:2], sm[:, :, P:W], X, ALU.max, negate=True))
                    link(dve.tensor_scalar(alive[:], nmax[:], 1e38, None, ALU.is_lt))
                    dve.tensor_scalar(nmax[:], nmax[:], SCALE, None, ALU.mult).then_inc(sem("nmax"), 1)
                    rank_dve(dve, link, gs[:], GR2, ggt, geq, grank, PT)
                    link(dve.tensor_scalar(grank[:], grank[:], 2.0, None, ALU.is_lt))
                    link(dve.tensor_tensor(r["m"][:].rearrange("p t (g k) -> p t g k", g=GR2), sg,
                                           grank[:].unsqueeze(3).broadcast_to([P, PT, GR2, E2 // GR2]), ALU.mult))
                    rank_dve(dve, link, r["m"][:], E2, gt, eq, r["rank"], PT)
                    link(dve.tensor_scalar(r["rank"][:], r["rank"][:], float(K2), None, ALU.is_lt))
                    link(dve.tensor_tensor(r["c"][:], r["rank"][:], r["s"][:], ALU.mult))
                    link(dve.tensor_reduce(csum[:], r["c"][:], X, ALU.add))
                    link(dve.tensor_scalar(csum[:], csum[:], 1e-20, None, ALU.add))
                    link(dve.reciprocal(csum[:], csum[:]))
                    link(dve.tensor_scalar(csum[:], csum[:], ROUTED_SCALE, None, ALU.mult))
                    link(dve.tensor_tensor(r["c"][:], r["c"][:], csum[:].unsqueeze(2).broadcast_to([P, PT, E2]), ALU.mult))
                    link(dve.tensor_copy(parts[:, :, 0, :], r["c"][:]))
                    link(dve.tensor_tensor(r["rest"][:], r["c"][:], parts[:, :, 0, :], ALU.subtract))
                    link(dve.tensor_copy(parts[:, :, 1, :], r["rest"][:]))
                    link(dve.tensor_tensor(r["rest"][:], r["rest"][:], parts[:, :, 1, :], ALU.subtract))
                    dve.tensor_copy(parts[:, :, 2, :], r["rest"][:]).then_inc(sem("parts"), 1)
                    dve.wait_ge(sem("prob"), PB)
                    link(dve.tensor_tensor(rinv[:], rsum[:], alive[:], ALU.mult))
                    link(dve.reciprocal(rinv[:], rinv[:]))
                    link(dve.tensor_tensor(rinv[:], rinv[:], alive[:], ALU.mult))

                    def attended():
                        dve.wait_ge(sem("pv"), 1)
                        for t in range(PT):
                            i, tt = divmod(t, T)
                            ins = dve.scalar_tensor_tensor(x1[:, t, :], psO[:, t * D:(t + 1) * D], rinv[:, i, tt:tt + 1], xb[:, t, :], ALU.mult, ALU.add)
                        ins.then_inc(sem("attended"), 1)

                    for n, c in enumerate(TILES):
                        if c < EP2:
                            dve.wait_ge(sem("relu"), n + 1)
                            dve.wait_ge(sem("spread"), c + 1)
                            dve.tensor_tensor(hc[:, n % RING, :], hr[:, n % RING, :], psC[c % 2][:], ALU.mult).then_inc(sem("weighted"), 1)
                            if c == 0:
                                attended()
                            if c == 3:
                                norm_stats(dve, link, x_next, PT)
                            if c == 5:
                                norm_scale(dve, x_next, PT)
                    dve.wait_ge(sem("down"), NT2)
                    dve.wait_ge(sem("attended"), 1)
                    dve.tensor_tensor(xb, x1[:], psD[:].rearrange("p (t d) -> p t d", t=PT), ALU.add)

                @block.gpsimd
                def _(pool):
                    for n, c in enumerate(TILES):
                        if n >= RING:
                            pool.wait_ge(sem("down"), n - RING + 1)
                        if c == 4:
                            norm_pool(pool, PT)
                            pool.wait_ge(sem("rstd"), 1)
                        if c < EP2:
                            pool.wait_ge(sem("weighted"), c + 1)
                            pool.tensor_tensor(h2[:, n % RING, :], hr[:, n % RING, :], hc[:, n % RING, :], ALU.mult).then_inc(sem("squared"), 1)
                        else:
                            pool.wait_ge(sem("relu"), n + 1)
                            pool.tensor_tensor(h2[:, n % RING, :], hr[:, n % RING, :], hr[:, n % RING, :], ALU.mult).then_inc(sem("squared"), 1)

                @block.scalar
                def _(act):
                    act.wait_ge(sem("qk_ps"), 1)
                    act.activation(q2[:], psQ[:], ACT.Copy).then_inc(sem("qk"), 1)
                    act.wait_ge(sem("qk_ps"), 2)
                    act.activation(k2[:], psK[:], ACT.Copy).then_inc(sem("qk"), 1)
                    act.wait_ge(sem("logits"), 1)
                    act.activation(r["e"][:], psG[:, 0:PT * E2].rearrange("p (t e) -> p t e", t=PT), ACT.Exp, scale=-1.0).then_inc(sem("sig_e"), 1)
                    for n, c in enumerate(TILES):
                        act.wait_ge(sem("up"), n + 1)
                        if n >= RING:
                            act.wait_ge(sem("squared"), n - RING + 1)
                        act.activation(hr[:, n % RING, :], psU[n % 2][:], ACT.Relu).then_inc(sem("relu"), 1)
                        if n == 1:
                            act.wait_ge(sem("nmax"), 1)
                            for i in range(PB):
                                for t, (a, e) in enumerate(((0, P), (P, W))):
                                    ins = act.activation(prob[:, i, a:e], sm[:, i, a:e], ACT.Exp, bias=nmax[:, i, t:t + 1], scale=SCALE,
                                                         accum_out=rsum[:, i, t:t + 1])
                                ins.then_inc(sem("prob"), 1)
                        if n == 3:
                            for i in range(PB):
                                act.wait_ge(sem("probT_ps"), i + 1)
                                act.activation(probT[:, i], psT[i][:, 0:W], ACT.Copy).then_inc(sem("probT"), 1)
                        if n == 5:
                            act.wait_ge(sem("cT_ps"), 1)
                            act.activation(cT[:], psP[0:3 * E2, :], ACT.Copy).then_inc(sem("cT"), 1)
                    norm_act(act, psX, PT)

                @block.tensor
                def _(pe):
                    for t in range(PT):
                        mm = pe.matmul(psG[:, t * E2:(t + 1) * E2], xnT_all[:, t * P:(t + 1) * P], gate2[:], start=True, stop=True)
                    mm.then_inc(sem("logits"), 1)
                    for ps, n in ((psQ, 0), (psK, 1)):
                        pe.matmul(ps[:], wqkv2[:, n, :], xnT_all[:], start=True, stop=True).then_inc(sem("qk_ps"), 1)
                    for t in range(PT):
                        mm = pe.matmul(psV[:, t * D:(t + 1) * D], xnT_all[:, t * P:(t + 1) * P], wqkv2[:, 2, :], start=True, stop=True)
                    mm.then_inc(sem("values_ps"), 1)
                    pe.wait_ge(sem("qk"), 2)
                    for i in range(PB):
                        o = i * S
                        pe.matmul(psS[i][:, 0:P], q2[:, o:o + P], k2[:, o:o + P], start=True, stop=True)
                        pe.matmul(psS[i][:, P:W], q2[:, o + P:o + S], k2[:, o:o + S], start=True, stop=True).then_inc(sem("scores"), 1)

                    def up(n):
                        if n >= 2:
                            pe.wait_ge(sem("relu"), n - 1)
                        c = TILES[n]
                        wt = up2[:, c * P:(c + 1) * P] if c < EP2 else sup2[:, (c - EP2) * P:(c - EP2 + 1) * P]
                        pe.matmul(psU[n % 2][:], wt, xnT_all[:], start=True, stop=True).then_inc(sem("up"), 1)

                    def down(n):
                        c = TILES[n]
                        wt = down2[:, c, :] if c < EP2 else sdown2[:, c - EP2, :]
                        pe.wait_ge(sem("squared"), n + 1)
                        if n == 0:
                            pe.wait_ge(sem("sig_e"), 1)
                        for t in range(PT):
                            mm = pe.matmul(psD[:, t * D:(t + 1) * D], h2[:, n % RING, t * P:(t + 1) * P], wt,
                                           start=n == 0 and t == 0, stop=n == NT2 - 1, skip_group_check=True)
                        mm.then_inc(sem("down"), 1)

                    for n in range(4):
                        up(n)
                    for n in range(SP2):
                        down(n)
                    pe.wait_ge(sem("values"), 1)
                    for i in range(PB):
                        pe.wait_ge(sem("prob"), i + 1)
                        for n in range(W // P):
                            mm = pe.transpose(psT[i][:, n * P:(n + 1) * P], prob[:, i, n * P:(n + 1) * P], ident[:])
                        mm.then_inc(sem("probT_ps"), 1)
                    up(4)
                    pe.wait_ge(sem("probT"), PB)
                    for i in range(PB):
                        o = i * T * D
                        pe.matmul(psO[:, o:o + D], probT[:, i, 0:P], v2[:, i * T, :], start=True, stop=True)
                        pe.matmul(psO[:, o + D:o + 2 * D], probT[:, i, P:2 * P], v2[:, i * T, :], start=True, stop=False)
                        mm = pe.matmul(psO[:, o + D:o + 2 * D], probT[:, i, 2 * P:W], v2[:, i * T + 1, :], start=False, stop=True)
                    mm.then_inc(sem("pv"), 1)
                    up(5)
                    up(6)
                    pe.wait_ge(sem("parts"), 1)
                    for t in range(PT):
                        mm = pe.matmul(psP[0:3 * E2, t * P:(t + 1) * P], parts[:, t].rearrange("p a e -> p (a e)"), ident_b[:], start=True, stop=True)
                    mm.then_inc(sem("cT_ps"), 1)

                    def spread(c):
                        if c >= 2:
                            pe.wait_ge(sem("weighted"), c - 1)
                        pe.matmul(psC[c % 2][:], spread_b[:, c * P:(c + 1) * P], cT[:], start=True, stop=True).then_inc(sem("spread"), 1)

                    pe.wait_ge(sem("cT"), 1)
                    spread(0)
                    spread(1)
                    for n in range(SP2, NT2):
                        if n + 5 < NT2:
                            up(n + 5)
                        if n < EP2:
                            spread(n)
                        down(n)
                        if n == NT2 - 2:
                            pe.wait_ge(sem("attended"), 1)
                            norm_pe(pe, psX, PT)
            nc.all_engine_barrier()
            sem.clear(nc)
            nc.all_engine_barrier()

        def layer3(wqkvg3, bg3, wo3, gate3, gb3, w13, b13, w23, b23, level3):
            with ExitStack() as lx:
                def lsb(name, shape, dt=F32):
                    return lx.enter_context(nc.sbuf_tensor(name, shape, dt))
                r = {n: lsb("t_" + n, [P, T, E3]) for n in ("l", "e", "p", "rank", "w", "next")}
                oh = lsb("oh", [P, 2, T, E3])
                pos = lsb("pos", [P, 2, T, E3])
                tmx = lsb("tmx", [P, T])
                tsum = lsb("tsum", [P, T])
                gt = lsb("gt3", [P, T, E3, E3])
                eq = lsb("eq3", [P, T, E3, E3])
                wT = lsb("wT", [E3, S])
                hm = lsb("hm", [P, 2, FC3, S])
                acc = lsb("acc", [P, T, D])
                v3 = lsb("v3", [P, T, NH3 * DK3])
                edge = [lsb(f"edge{h}", [P, PAIRS, S // h]) for h in LEVELS + [P]]
                NB = 4
                qp = lsb("qp", [P, NB, 2, S])
                kk = lsb("kk", [P, NB, S])
                pT = lsb("pT", [P, NB, T, 2, P])
                pX = lsb("pX", [P, NB, 2, P])
                oT = lsb("oT", [P, 2, S])
                xnT_next = xnT_all[:, S:2 * S]
                psA, psL, psV, psO, psH, psY = bank[1], bank[2:4], bank[4], bank[5], (bank[6], bank[0]), bank[7]
                psX = psA
                level = level3[:].rearrange("p (l c) -> p l c", l=len(LEVELS))
                STEPS = [0] + LEVELS + [P]
                NL, NSTEP = len(LEVELS), len(LEVELS) + 2
                COUPLES = PAIRS // 2
                ORDER = [(jj, n, m) for jj in range(COUPLES) for n in range(NSTEP) for m in range(2)]
                STEP_AT = {o: i for i, o in enumerate(ORDER)}
                KEYED = [o for o in ORDER if 1 <= o[1] <= NL]
                KEYED_AT = {o: i for i, o in enumerate(KEYED)}
                PIECES = [(e, c) for e in range(E3) for c in range(FC3 + T)]
                SHARES = [1 if c < FC3 else FC3 // T for _, c in PIECES]
                FIRST = 1
                piece_at = {}
                for n, p in enumerate(PIECES):
                    piece_at.setdefault(FIRST + sum(SHARES[:n]) * (len(ORDER) - FIRST) // sum(SHARES), []).append(p)
                VALUES = {4 * n + 2: n for n in range(4)}
                LAST = 2 * NSTEP * (COUPLES - 1)
                A_NORM, A_TOKENS, A_LOGITS, A_RANK, A_PLACES, A_KEEP, A_TURN, A_TAKE = (LAST + n for n in (-8, 1, 3, 4, 7, 8, 11, 12))
                AHEAD = PAIRS - 2
                GATES = {len(ORDER) - 2 * (AHEAD - j) + 1: j for j in range(AHEAD)}
                PAIR_OF = lambda jj, m: 2 * jj + m

                def outs(j):
                    return psO if j < PAIRS - 1 else psL[0]

                def halves(a, h):
                    return a.rearrange("p (n two h) -> p n two h", two=2, h=h)

                def route_logits(dve, link):
                    dve.wait_ge(sem("logits"), 1)
                    link(dve.tensor_tensor(r["l"][:], psX[:, 256:256 + T * E3].rearrange("p (t e) -> p t e", t=T),
                                           gb3[:].unsqueeze(1).broadcast_to([P, T, E3]), ALU.add))
                    link(dve.tensor_reduce(tmx[:], r["l"][:], X, ALU.max))
                    dve.tensor_tensor(r["l"][:], r["l"][:], tmx[:].unsqueeze(2).broadcast_to([P, T, E3]), ALU.subtract).then_inc(sem("shifted"), 1)

                def route_rank(dve, link):
                    dve.wait_ge(sem("exps"), 1)
                    link(dve.tensor_reduce(tsum[:], r["e"][:], X, ALU.add))
                    link(dve.reciprocal(tsum[:], tsum[:]))
                    link(dve.tensor_tensor(r["p"][:], r["e"][:], tsum[:].unsqueeze(2).broadcast_to([P, T, E3]), ALU.mult))
                    rank_dve(dve, link, r["p"][:], E3, gt, eq, r["rank"])
                    for c in range(2):
                        dve.tensor_scalar(oh[:, c], r["rank"][:], float(c), None, ALU.is_equal).then_inc(sem("onehot"), 1)

                def route_keep(dve, link):
                    dve.wait_ge(sem("places"), 1)
                    places = psX[:, 0:2 * T * E3].rearrange("p (c t e) -> p c t e", c=2, t=T)
                    link(dve.tensor_tensor(pos[:], places, carry[:].unsqueeze(2).broadcast_to([P, 2, T, E3]), ALU.add))
                    counts = psX[:, 128:128 + 2 * E3].rearrange("p (c e) -> p c e", c=2)
                    link.tell(dve.tensor_tensor(carry[:], carry[:], counts, ALU.add))
                    link(dve.tensor_scalar(pos[:], pos[:], float(CAP3), None, ALU.is_le))
                    link(dve.tensor_tensor(pos[:], pos[:], oh[:], ALU.mult))
                    link(dve.tensor_tensor(pos[:, 0], pos[:, 0], pos[:, 1], ALU.add))
                    dve.tensor_tensor(r["next"][:], pos[:, 0], r["p"][:], ALU.mult).then_inc(sem("weights"), 1)

                def route_turned(dve):
                    dve.wait_ge(sem("wT_ps"), 1)
                    dve.tensor_copy(wT[:], psX[0:E3, 256:256 + S]).then_inc(sem("wT"), 1)

                def route_taken(dve, link):
                    link.wait()
                    dve.wait_ge(sem("weights"), 1)
                    dve.tensor_copy(r["w"][:], r["next"][:])

                def route_exp(act):
                    act.wait_ge(sem("shifted"), 1)
                    act.activation(r["e"][:], r["l"][:], ACT.Exp).then_inc(sem("exps"), 1)

                def logits_pe(pe):
                    pe.wait_ge(sem("xnT"), 1)
                    for t in range(T):
                        mm = pe.matmul(psX[:, 256 + t * E3:256 + (t + 1) * E3], xnT_next[:, t * P:(t + 1) * P], gate3[:], start=True, stop=True)
                    mm.then_inc(sem("logits"), 1)

                def places_pe(pe):
                    pe.wait_ge(sem("onehot"), 2)
                    places = psX[:, 0:2 * T * E3].rearrange("p (c t e) -> p c t e", c=2, t=T)
                    pe.matmul(places, cst["tri"][:], oh[:], start=True, stop=False, skip_group_check=True)
                    pe.matmul(places[:, :, 1, :], ones[:], oh[:, :, 0, :], start=False, stop=True, skip_group_check=True)
                    for t in range(T):
                        mm = pe.matmul(psX[:, 128:128 + 2 * E3].rearrange("p (c e) -> p c e", c=2), ones[:], oh[:, :, t, :], start=t == 0, stop=t == T - 1)
                    mm.then_inc(sem("places"), 1)

                def weights_T_pe(pe):
                    pe.wait_ge(sem("weights"), 1)
                    for t in range(T):
                        mm = pe.transpose(psX[0:E3, 256 + t * P:256 + (t + 1) * P], r["next"][:, t, :], ident[:])
                    mm.then_inc(sem("wT_ps"), 1)

                def gate_pe(pe, ps, j, src):
                    pe.matmul(ps[:, 0:S], wqkvg3[:, 3, j * P:(j + 1) * P], src, start=True, stop=True).then_inc(sem("gate_ps"), 1)

                def gate_act(act, ps, j, nth):
                    act.wait_ge(sem("gate_ps"), nth + 1)
                    act.activation(edge[0][:, j, :], ps[:, 0:S], ACT.Sigmoid, bias=bg3[:, j:j + 1]).then_inc(sem("gates"), 1)

                def first(block):
                    @block.vector
                    def _(dve):
                        link = Chain(dve, sem("dve_chain"))
                        norm_stats(dve, link, x[:, 0:T, :])
                        norm_scale(dve, x[:, 0:T, :])
                        route_logits(dve, link)
                        route_rank(dve, link)
                        route_keep(dve, link)
                        route_turned(dve)
                        route_taken(dve, link)

                    @block.gpsimd
                    def _(pool):
                        norm_pool(pool)
                        pool.wait_ge(sem("rstd"), 1)
                        for a in range(2):
                            pool.memset(qp[64 * (1 - a):64 * (1 - a) + 64, :, a, :], 0.0).then_inc(sem("zeros"), 1)
                            pool.wait_ge(sem("zeros"), a + 1)

                    @block.scalar
                    def _(act):
                        norm_act(act, psX, dst=xnT_next)
                        route_exp(act)
                        for j in range(AHEAD):
                            gate_act(act, psL[j % 2], j, j)
                        act.wait_ge(sem("xnT"), 1)
                        act.activation(xnT, xnT_next, ACT.Copy)

                    @block.tensor
                    def _(pe):
                        norm_pe(pe, psX)
                        logits_pe(pe)
                        for j in range(AHEAD):
                            if j >= 2:
                                pe.wait_ge(sem("gates"), j - 1)
                            gate_pe(pe, psL[j % 2], j, xnT_next)
                        places_pe(pe)
                        weights_T_pe(pe)

                def steady(block, xb, x_next):
                  @block.vector
                  def _(dve):
                    link = Chain(dve, sem("dve_chain"))

                    def expert(e):
                        dve.wait_ge(sem("expert_ps"), T * (e + 1))
                        dve.wait_ge(sem("expert_added"), e + 1)
                        for t in range(T):
                            ins = dve.scalar_tensor_tensor(acc[:, t, :], psY[:, t * D:(t + 1) * D], r["w"][:, t, e:e + 1], acc[:, t, :], ALU.mult, ALU.add)
                        ins.then_inc(sem("expert_added"), 1)

                    def block_decays(n):
                        two = edge[n][:].rearrange("p j (n two) -> p j n two", two=2)
                        if n:
                            dve.wait_ge(sem("edges"), n)
                        dve.tensor_tensor(edge[n + 1][:], two[:, :, :, 0], two[:, :, :, 1], ALU.mult).then_inc(sem("edges"), 1)

                    dve.wait_ge(sem("bias_ps"), 1)
                    dve.tensor_tensor(acc[:], psY[:, 0:T * D].rearrange("p (t d) -> p t d", t=T), xb, ALU.add).then_inc(sem("expert_added"), 1)
                    dve.wait_ge(sem("gates"), PAIRS - AHEAD)

                    def step(i):
                        jj, n, m = ORDER[i]
                        j = PAIR_OF(jj, m)
                        s = j % NB
                        h = STEPS[n]
                        ps = psL[m]
                        dve.wait_ge(sem("scored"), i + 1)
                        if n == 0:
                            if j >= NB:
                                dve.wait_ge(sem("pv"), j - NB + 1)
                            dve.tensor_tensor(pT[:, s].rearrange("p t a q -> p (t a) q"), ps[:].rearrange("p (n q) -> p n q", n=4),
                                              ident[:].unsqueeze(1).broadcast_to([P, 4, P]), ALU.mult)
                            for a in range(2):
                                rows = slice(64 * a, 64 * a + 64)
                                ins = dve.tensor_tensor(qp[rows, s, a, :], qp[rows, s, a, :], edge[0][rows, j, :], ALU.mult)
                            ins.then_inc(sem("levelled"), 1)
                        elif h < P:
                            if jj == 0 and n >= 2:
                                dve.wait_ge(sem("edges"), n - 1)
                            dve.wait_ge(sem("levelled"), STEP_AT[jj, n - 1, m] + 1)
                            right = halves(pT[:, s].rearrange("p t a q -> p (t a q)"), h)[:, :, 1, :]
                            dve.copy_predicated(right, level[:, n - 1, :].rearrange("p (c h) -> p c h", h=h),
                                                ps[:, 0:S].rearrange("p (c h) -> p c h", h=h))
                            two = edge[n - 1][:, j, :].rearrange("p (n two) -> p n two", two=2)
                            for a in range(2):
                                rows = slice(64 * a, 64 * a + 64)
                                q = halves(qp[rows, s, a, :], h)[:, :, 1, :]
                                ins = dve.tensor_tensor(q, q, two[rows, :, 0:1].broadcast_to([64, S // (2 * h), h]), ALU.mult)
                            ins.then_inc(sem("levelled"), 1)
                        else:
                            dve.tensor_copy(pX[:, s], ps[:, 0:2 * P].rearrange("p (a q) -> p a q", a=2)).then_inc(sem("levelled"), 1)

                    for i in range(len(ORDER)):
                        step(i)
                        if ORDER[i][0] == 0 and ORDER[i][2] == 1 and ORDER[i][1] < NL:
                            block_decays(ORDER[i][1])
                        if i == A_NORM:
                            norm_stats(dve, link, x_next)
                        if i == A_NORM + 3:
                            norm_scale(dve, x_next)
                        if i == A_LOGITS:
                            route_logits(dve, link)
                        if i == A_RANK:
                            route_rank(dve, link)
                        if i == A_KEEP:
                            route_keep(dve, link)
                        if i == A_TAKE:
                            route_turned(dve)
                        for e, c in piece_at.get(i - 2, []):
                            if c == FC3 + T - 1:
                                expert(e)
                    for i in range(len(ORDER) - 2, len(ORDER)):
                        for e, c in piece_at.get(i, []):
                            if c == FC3 + T - 1:
                                expert(e)
                    dve.wait_ge(sem("projected"), PAIRS)
                    dve.wait_ge(sem("expert_added"), E3 + 1)
                    route_taken(dve, link)
                    dve.tensor_tensor(xb, acc[:], psV[:, 0:T * D].rearrange("p (t d) -> p t d", t=T), ALU.add)

                  @block.gpsimd
                  def _(pool):
                    for jj, n, m in KEYED:
                        j = PAIR_OF(jj, m)
                        h = STEPS[n]
                        pool.wait_ge(sem("scored"), STEP_AT[jj, n, m] + 1)
                        if n >= 2:
                            pool.wait_ge(sem("edges"), n - 1)
                        if (jj, n, m) == (COUPLES - 2, NL - 1, 0):
                            norm_pool(pool)
                            pool.wait_ge(sem("rstd"), 1)
                        k = halves(kk[:, j % NB, :], h)[:, :, 0, :]
                        two = edge[n - 1][:, j, :].rearrange("p (n two) -> p n two", two=2)
                        if n >= 2:
                            pool.wait_ge(sem("keyed"), KEYED_AT[jj, n - 1, m] + 1)
                        pool.tensor_tensor(k, k, two[:, :, 1:2].broadcast_to([P, S // (2 * h), h]), ALU.mult).then_inc(sem("keyed"), 1)

                  @block.scalar
                  def _(act):
                    def queries_keys(j):
                        s = j % NB
                        act.wait_ge(sem("qk_ps"), j + 1)
                        act.activation(kk[:, s, :], psA[:, S:2 * S], ACT.Copy)
                        for a in range(2):
                            rows = slice(64 * a, 64 * a + 64)
                            ins = act.activation(qp[rows, s, a, :], psA[rows, 0:S], ACT.Copy)
                        ins.then_inc(sem("qk"), 1)

                    def outputs(j):
                        act.wait_ge(sem("pv"), j + 1)
                        if j >= 2:
                            act.wait_ge(sem("projected"), j - 1)
                        act.activation(oT[:, j % 2, :], outs(j)[:, 0:S], ACT.Copy).then_inc(sem("oT"), 1)

                    queries_keys(0)
                    for j in range(AHEAD, PAIRS):
                        gate_act(act, psL[j % 2], j, j - AHEAD)
                    queries_keys(1)
                    for i, (jj, n, m) in enumerate(ORDER):
                        if i in VALUES:
                            v = VALUES[i]
                            act.wait_ge(sem("values_ps"), v + 1)
                            act.activation(v3[:, v // 2, (v % 2) * 512:(v % 2 + 1) * 512], bank[4 + v % 2][:], ACT.Copy).then_inc(sem("values"), 1)
                        for e, c in piece_at.get(i, []):
                            if c < FC3:
                                if c == 0 and e >= 2:
                                    act.wait_ge(sem("expert_ps"), T * (e - 1))
                                act.wait_ge(sem("hidden_ps"), e * FC3 + c + 1)
                                act.activation(hm[:, e % 2, c, :], psH[(e * FC3 + c) % 2][:, 0:S], ACT.Relu, bias=b13[:, e, c:c + 1]).then_inc(sem("hidden"), 1)
                        if n == NSTEP - 3 and jj + 1 < COUPLES:
                            queries_keys(PAIR_OF(jj + 1, m))
                        if n == 1 and jj >= 1:
                            outputs(PAIR_OF(jj - 1, m))
                        if i == A_TOKENS:
                            norm_act(act, psX, dst=xnT_next)
                        if i == A_LOGITS:
                            route_exp(act)
                        if i in GATES:
                            gate_act(act, psO, GATES[i], PAIRS - AHEAD + GATES[i])
                    act.wait_ge(sem("hidden_ps"), E3 * FC3)
                    act.wait_ge(sem("xnT"), 1)
                    act.activation(xnT, xnT_next, ACT.Copy)
                    for m in range(2):
                        outputs(PAIR_OF(COUPLES - 1, m))

                  @block.tensor
                  def _(pe):
                    for t in range(T):
                        mm = pe.matmul(psY[:, t * D:(t + 1) * D], wT[:, t * P:(t + 1) * P], b23[:], start=True, stop=True)
                    mm.then_inc(sem("bias_ps"), 1)
                    def queries_keys(j):
                        if j >= 1:
                            pe.wait_ge(sem("qk"), j)
                        for n in range(2):
                            mm = pe.matmul(psA[:, n * S:(n + 1) * S], wqkvg3[:, n, j * P:(j + 1) * P], xnT[:], start=True, stop=True)
                        mm.then_inc(sem("qk_ps"), 1)

                    queries_keys(0)
                    for j in range(AHEAD, PAIRS):
                        gate_pe(pe, psL[j % 2], j, xnT)
                    queries_keys(1)

                    def piece(e, c):
                        n = e * FC3 + c
                        if c < FC3:
                            if n >= 2:
                                pe.wait_ge(sem("hidden"), n - 1)
                            pe.matmul(psH[n % 2][:, 0:S], w13[:, e, c * P:(c + 1) * P], xnT[:], start=True, stop=True).then_inc(sem("hidden_ps"), 1)
                        else:
                            t = c - FC3
                            if t == 0:
                                pe.wait_ge(sem("hidden"), (e + 1) * FC3)
                                pe.wait_ge(sem("expert_added"), e + 1)
                            for c4 in range(FC3):
                                mm = pe.matmul(psY[:, t * D:(t + 1) * D], hm[:, e % 2, c4, t * P:(t + 1) * P], w23[:, e, c4, :], start=c4 == 0, stop=c4 == FC3 - 1)
                            mm.then_inc(sem("expert_ps"), 1)

                    def step(i):
                        jj, n, m = ORDER[i]
                        j = PAIR_OF(jj, m)
                        s = j % NB
                        h = STEPS[n]
                        ps = psL[m]
                        if n == 0:
                            pe.wait_ge(sem("qk"), j + 1)
                            if jj:
                                pe.wait_ge(sem("levelled"), STEP_AT[jj - 1, NSTEP - 1, m] + 1)
                            else:
                                pe.wait_ge(sem("gates"), PAIRS - AHEAD)
                            for t in range(T):
                                mm = pe.matmul(ps[:, t * S:(t + 1) * S], kk[:, s, t * P:(t + 1) * P], qp[:, s, :, t * P:(t + 1) * P], start=True, stop=True)
                        else:
                            pe.wait_ge(sem("levelled"), STEP_AT[jj, n - 1, m] + 1)
                            if n >= 2:
                                pe.wait_ge(sem("keyed"), KEYED_AT[jj, n - 1, m] + 1)
                            if h < P:
                                for t in range(T):
                                    q = qp[:, s, :, t * P:(t + 1) * P].rearrange("p a (c two h) -> p a c two h", two=2, h=h)[:, :, :, 1, :]
                                    mm = pe.matmul(ps[:, t * P:(t + 1) * P], kk[:, s, t * P:(t + 1) * P], q, start=True, stop=True)
                            else:
                                mm = pe.matmul(ps[:, 0:2 * P], kk[:, s, 0:P], qp[:, s, :, P:S], start=True, stop=True)
                        mm.then_inc(sem("scored"), 1)

                    def values(j):
                        s = j % NB
                        if j == 0:
                            pe.wait_ge(sem("values"), 4)
                        elif j < PAIRS - 1:
                            pe.wait_ge(sem("oT"), j)
                        if j == PAIRS - 2:
                            pe.wait_ge(sem("gates"), PAIRS)
                        pe.wait_ge(sem("levelled"), STEP_AT[j // 2, NSTEP - 1, j % 2] + 1)
                        for a in range(2):
                            ch = slice(j * P + 64 * a, j * P + 64 * a + 64)
                            o = outs(j)[64 * a:64 * a + 64, :]
                            pe.matmul(o[:, 0:P], v3[:, 0, ch], pT[:, s, 0, a, :], start=True, stop=True)
                            pe.matmul(o[:, P:S], v3[:, 1, ch], pT[:, s, 1, a, :], start=True, stop=False)
                            mm = pe.matmul(o[:, P:S], v3[:, 0, ch], pX[:, s, a, :], start=False, stop=True)
                        mm.then_inc(sem("pv"), 1)

                    def project(j):
                        pe.wait_ge(sem("oT"), j + 1)
                        for t in range(T):
                            mm = pe.matmul(psV[:, t * D:(t + 1) * D], oT[:, j % 2, t * P:(t + 1) * P], wo3[:, j, :],
                                           start=j == 0 and t == 0, stop=j == PAIRS - 1, skip_group_check=True)
                        mm.then_inc(sem("projected"), 1)

                    for i, (jj, n, m) in enumerate(ORDER):
                        step(i)
                        if i in VALUES:
                            v = VALUES[i]
                            if v >= 2:
                                pe.wait_ge(sem("values"), v - 1)
                            pe.matmul(bank[4 + v % 2][:], xnT[:, v // 2 * P:(v // 2 + 1) * P], wqkvg3[:, 2, v % 2 * 512:(v % 2 + 1) * 512], start=True, stop=True).then_inc(sem("values_ps"), 1)
                        if i == A_TOKENS:
                            pe.wait_ge(sem("qk"), PAIRS)
                            norm_pe(pe, psX)
                        if i == A_TOKENS + 1:
                            logits_pe(pe)
                        if i == A_PLACES:
                            places_pe(pe)
                        if i == A_TURN:
                            weights_T_pe(pe)
                        if i in GATES:
                            pe.wait_ge(sem("oT"), PAIRS - 2)
                            pe.wait_ge(sem("gates"), PAIRS - AHEAD + GATES[i])
                            gate_pe(pe, psO, GATES[i], xnT_next)
                        for e, c in piece_at.get(i, []):
                            piece(e, c)
                        if n == NSTEP - 3 and jj + 1 < COUPLES:
                            queries_keys(PAIR_OF(jj + 1, m))
                        if n == 1 and jj >= 1:
                            values(PAIR_OF(jj - 1, m))
                        if n == 2 and jj >= 1:
                            project(PAIR_OF(jj - 1, m))
                    for m in range(2):
                        values(PAIR_OF(COUPLES - 1, m))
                    for m in range(2):
                        project(PAIR_OF(COUPLES - 1, m))
                with nc.Block() as block:
                    first(block)
                nc.all_engine_barrier()
                sem.clear(nc)
                nc.all_engine_barrier()
                with nc.Fori(0, B) as b:
                    with nc.Block() as block:
                        steady(block, x[:, bass.ds(b * T, T), :], x[:, bass.ds(b * T + T, T), :])
                    nc.all_engine_barrier()
                    sem.clear(nc)
                    nc.all_engine_barrier()

        def layer1():
            with ExitStack() as lx:
                def lsb(name, shape, dt=F32):
                    return lx.enter_context(nc.sbuf_tensor(name, shape, dt))
                NV = VH + 1
                cc = lsb("cc", [P, T, P])
                ss = lsb("ss", [P, T, 4])
                lat = lsb("lat", [P, T, QL + KVL + 3])
                junk = lsb("junk", [P, T, P])
                ccT = lsb("ccT", [P, S])
                k1T = lsb("k1T", [P, S])
                krt = lsb("krt", [ROPE, S])
                gate = lsb("gate", [P, 4, 3])
                gsum = lsb("gsum", [P, 1])
                imp = lsb("imp", [1, 5, S])
                imp0 = lsb("imp0", [1, S])
                top8 = lsb("top8", [1, 4, 8])
                selc = lsb("selc", [P, T])
                selm = lsb("selm", [P, T, KEEP])
                selT = lsb("selT", [P, HG, KEEP])
                qT = lsb("qT", [P, 2, HG, S])
                k3T = lsb("k3T", [QK, 2, HG, S])
                tq = lsb("tq", [ROPE, HG, S])
                tk = lsb("tk", [ROPE, HG, S])
                k2T = lsb("k2T", [QK, NH, KEEP])
                t2 = lsb("t2", [ROPE, NH, KEEP])
                vv = lsb("vv", [P, 2, T, NH, NV])
                v2 = lsb("vsel", [P, G1, HG, NV])
                sc = lsb("sc", [P, 3, 512])
                nmax = lsb("nmax1", [P, 3, T * HG])
                pT = lsb("probT1", [P, 2, 512])
                rr = lsb("rr", [P, 3, HG])
                oo = lsb("oo", [P, T, 3, HG, VH])
                ot = lsb("ot", [P, 2, T, HG * VH])
                otT = lsb("otT", [P, G1, S])
                uk = lsb("uk", [P, 2, S])
                ri = lsb("ri", [P, R1, S])
                xr = lsb("xr", [P, T, D])
                NS = QL + KVL + 3
                SPARE = bank[4]
                GU = [(0, 0, 0), (1, 0, 0), (0, 1, 0), (1, 1, 0), (2, 0, 0), (0, 1, 2), (1, 1, 2)]
                NG = len(GU)
                UNITS = [(g,) + u for g in range(G1) for u in GU]
                NU = len(UNITS)
                LAST = NU + 4
                PIECES = [("k", 0), ("k", 2), ("q", 0), ("q", 2)]
                BESIDE = [0, 2, 4, 5]
                NPC = len(PIECES)
                EXTRA = ["tokens", "keys", "values"]
                VALUES = [(0, 0), (0, 1), (1, 0), (1, 1)]
                MERGE_AT = {g * NG + d: (g, t) for g in range(G1) for t, d in ((0, 8), (1, 10))}
                TURN_AT = {g * NG + 13: g for g in range(G1 - 1)}
                LARGEST_AT = {19: 0, 20: 1, 22: 2, 24: 3}
                F_AT = {13: 0, 14: 1}
                A_NORM, A_TOKENS, A_UNITS, A_SMALL, A_ROOTS, A_LATENTS, A_PLACES, A_SHARED = 13, 17, 18, 19, 20, 23, 27, NU

                def piece_of(i):
                    g, k = divmod(i, NG)
                    return g * NPC + BESIDE.index(k) if g < G1 and k in BESIDE else None

                def outs(t):
                    return bank[7 * t][:, 0:3 * HG * NV].rearrange("p (a h v) -> p a h v", a=3, h=HG)

                def bc(a, n):
                    return a.unsqueeze(1).broadcast_to([a.shape[0], n, a.shape[-1]])

                def unit_ps(u):
                    return bank[2 + u % 2]

                def half(a):
                    return slice(a * ROPE // 2, (a + 1) * ROPE // 2)

                def turned(dve, g, i):
                    kind, h = PIECES[i]
                    ps = bank[1][:].rearrange("p (h s) -> p h s", h=2)
                    tmp, dst, n = (tk, k3T, QK) if kind[0] == "k" else (tq, qT, P)
                    ins = dve.tensor_tensor(dst[:, g % 2, h:h + 2, :], ps[0:n], bc(cosT[0:n], 2), ALU.mult)
                    for a in range(2):
                        ins = dve.tensor_tensor(tmp[half(1 - a), h:h + 2, :], ps[half(a)], bc(sinT[half(a)], 2), ALU.mult)
                    ins.then_inc(sem("turned"), 1)

                def project(pe, g, i):
                    kind, h = PIECES[i]
                    h += g % G1 * HG
                    for n in range(2):
                        o = bank[1][:, n * S:(n + 1) * S]
                        if kind == "k":
                            mm = pe.matmul(o[0:QK, :], wink[:, (h + n) * QK:(h + n + 1) * QK], xnT[:], start=True, stop=True)
                        else:
                            mm = pe.matmul(o, wdq[:, (h + n) * P:(h + n + 1) * P], ccT[0:QL, :], start=True, stop=True)
                    mm.then_inc(sem("piece_ps"), 1)

                def add_turned(pool, g, i, done):
                    kind, h = PIECES[i]
                    tmp, dst = (tk, k3T) if kind == "k" else (tq, qT)
                    to = dst[0:ROPE, g % 2, h:h + 2]
                    pool.tensor_tensor(to, to, tmp[:, h:h + 2], ALU.add).then_inc(sem(kind + "_added"), 1)
                    pool.wait_ge(sem(kind + "_added"), done)

                def largest(dve, link, n):
                    link(dve.max(top8[:, n, :], imp[:, n, :]))
                    link(dve.match_replace(imp[:, n + 1, :], top8[:, n, :], imp[:, n, :], -3e38))

                def mean_squares(dve):
                    dve.wait_ge(sem("squares"), T)
                    dve.tensor_scalar(ss[:, :, 2:3], ss[:, :, 0:1], 1.0 / QL, 1e-6, ALU.mult, ALU.add)
                    dve.tensor_scalar(ss[:, :, 3:4], ss[:, :, 1:2], 1.0 / KVL, 1e-6, ALU.mult, ALU.add).then_inc(sem("ms"), 1)

                def latents(dve):
                    dve.wait_ge(sem("rms"), 1)
                    for t in range(T):
                        dve.tensor_scalar(cc[:, t, 0:QL], lat[:, t, 0:QL], ss[:, t, 0:1], None, ALU.mult)
                        ins = dve.tensor_scalar(cc[:, t, QL:P], lat[:, t, QL:P], ss[:, t, 1:2], None, ALU.mult)
                    ins.then_inc(sem("latents"), 1)

                def shared_keys(dve, link):
                    dve.wait_ge(sem("uk"), 1)
                    link.tell(dve.scalar_tensor_tensor(k1T[0:ROPE, :], uk[0:ROPE, 1, :], 1.0 / NH, cosT[0:ROPE, :], ALU.mult, ALU.mult))
                    for a in range(2):
                        link.tell(dve.scalar_tensor_tensor(krt[half(1 - a), :], uk[half(a), 1, :], 1.0 / NH, sinT[half(a), :], ALU.mult, ALU.mult))
                    link.wait()
                    link(dve.tensor_tensor(k1T[0:ROPE, :], k1T[0:ROPE, :], krt[:], ALU.add))

                def places(dve, link):
                    link(dve.tensor_scalar(imp[:, 0, :], imp[:, 4, :], -2.9e38, None, ALU.is_lt))
                    link(dve.tensor_tensor_scan(imp[:, 2, :], imp[:, 0, :], imp0[:], 0.0, ALU.add, ALU.add))
                    dve.tensor_tensor(imp[:, 3, :], imp[:, 2, :], imp[:, 0, :], ALU.mult).then_inc(sem("places"), 1)

                def select(dve, link):
                    dve.wait_ge(sem("places_ps"), 1)
                    link(dve.tensor_copy(selc[:], SPARE[:, 0:T]))
                    for t in range(T):
                        link.tell(dve.tensor_scalar(selm[:, t, :], cst["iota"][:], selc[:, t:t + 1], None, ALU.is_equal))

                def root_mean_squares(pool):
                    pool.wait_ge(sem("ms"), 1)
                    pool.tensor_tensor(ss[:, :, 0:2], ss[:, :, 2:4], mhalf[:, 0:4].rearrange("p (t a) -> p t a", t=T), ALU.pow).then_inc(sem("rms"), 1)
                    pool.wait_ge(sem("rms"), 1)

                def latent_keys(pool, link):
                    pool.wait_ge(sem("latT"), 1)
                    link(pool.tensor_scalar(k1T[QL:P, :], ccT[QL:P, :], gq[QL:P, :], None, ALU.mult))

                def squares(act):
                    act.wait_ge(sem("small"), 1)
                    act.activation(lat[:], SPARE[:].rearrange("p (t c) -> p t c", t=T)[:, :, 0:NS], ACT.Copy).then_inc(sem("lat"), 1)
                    act.wait_ge(sem("lat"), 1)
                    for t in range(T):
                        act.activation(junk[:, t, 0:QL], lat[:, t, 0:QL], ACT.Square, accum_out=ss[:, t, 0:1])
                        act.activation(junk[:, t, QL:P], lat[:, t, QL:P], ACT.Square, accum_out=ss[:, t, 1:2]).then_inc(sem("squares"), 1)

                def units_keys(act):
                    act.wait_ge(sem("units_ps"), 1)
                    act.activation(uk[:, 0, :], SPARE[:, 0:S], ACT.Copy)
                    act.activation(imp[:, 0, :], SPARE[ROPE:ROPE + 1, S:2 * S], ACT.Copy)
                    act.activation(uk[0:ROPE, 1, :], SPARE[0:ROPE, S:2 * S], ACT.Copy).then_inc(sem("uk"), 1)

                def latents_T(act):
                    act.wait_ge(sem("latT_ps"), 1)
                    act.activation(ccT[:], SPARE[:, 0:S], ACT.Copy).then_inc(sem("latT"), 1)

                def small_pe(pe):
                    pe.wait_ge(sem("uk"), 1)
                    for t in range(T):
                        mm = pe.matmul(SPARE[:, t * S:t * S + NS], xnT[:, t * P:(t + 1) * P], small1[:], start=True, stop=True)
                    mm.then_inc(sem("small"), 1)

                def units_pe(pe):
                    pe.wait_ge(sem("xnT"), 1)
                    pe.matmul(SPARE[:, 0:S], win[:].rearrange("p m j -> p (m j)"), xnT[:], start=True, stop=True)
                    pe.matmul(SPARE[0:ROPE, S:2 * S], wkr[:], xnT[:], start=True, stop=True)
                    pe.matmul(SPARE[ROPE:ROPE + 1, S:2 * S], wimp[:], xnT[:], start=True, stop=True).then_inc(sem("units_ps"), 1)

                def latents_pe(pe):
                    pe.wait_ge(sem("latents"), 1)
                    for t in range(T):
                        mm = pe.transpose(SPARE[:, t * P:(t + 1) * P], cc[:, t, :], ident[:])
                    mm.then_inc(sem("latT_ps"), 1)

                def places_pe(pe):
                    pe.wait_ge(sem("places"), 1)
                    pe.wait_ge(sem("latT"), 1)
                    for t in range(T):
                        mm = pe.matmul(SPARE[:, t:t + 1], imp[0:1, 3, t * P:(t + 1) * P], ones[0:1, 0:1], start=True, stop=True)
                    mm.then_inc(sem("places_ps"), 1)

                def merge(dve, link, g, t):
                    u = g * NG + (4 if t == 0 else 6)
                    n = g * T + t
                    dve.wait_ge(sem("pv"), u + 1)
                    o = outs(t)
                    if n:
                        dve.wait_ge(sem("merged"), n)
                    link(dve.reciprocal(rr[:], o[:, :, :, VH]))
                    link(dve.tensor_tensor(rr[:], rr[:], gate[:, 3, :].unsqueeze(2).broadcast_to([P, 3, HG]), ALU.mult))
                    if g:
                        dve.wait_ge(sem("summed"), n - T + 1)
                    dve.tensor_tensor(oo[:, t], o[:, :, :, 0:VH], rr[:].unsqueeze(3).broadcast_to([P, 3, HG, VH]), ALU.mult).then_inc(sem("merged"), 1)

                def first(block):
                    @block.vector
                    def _(dve):
                        link = Chain(dve, sem("dve_chain"))
                        norm_stats(dve, link, x[:, 0:T, :])
                        norm_scale(dve, x[:, 0:T, :])
                        mean_squares(dve)
                        latents(dve)
                        shared_keys(dve, link)
                        for n in range(KEEP // 8):
                            largest(dve, link, n)
                        places(dve, link)
                        for i in range(NPC):
                            dve.wait_ge(sem("piece_ps"), i + 1)
                            turned(dve, 0, i)
                        select(dve, link)
                        link.wait()

                    @block.gpsimd
                    def _(pool):
                        link = Chain(pool, sem("pool_chain"))
                        norm_pool(pool)
                        pool.wait_ge(sem("rstd"), 1)
                        link(pool.memset(imp0[:], 0.0))
                        link(pool.memset(k1T[ROPE:QL, :], 0.0))
                        link(pool.memset(vv[:, :, :, :, VH:NV], 1.0))
                        root_mean_squares(pool)
                        link(pool.memset(v2[:], 0.0))
                        for h in range(HG):
                            link(pool.memset(v2[h * KEEP:(h + 1) * KEEP, :, h, VH:NV], 1.0))
                        latent_keys(pool, link)
                        for i in range(NPC):
                            pool.wait_ge(sem("turned"), i + 1)
                            add_turned(pool, 0, i, i % 2 + 1)

                    @block.scalar
                    def _(act):
                        norm_act(act, SPARE)
                        units_keys(act)
                        squares(act)
                        latents_T(act)

                    @block.tensor
                    def _(pe):
                        norm_pe(pe, SPARE)
                        units_pe(pe)
                        small_pe(pe)
                        latents_pe(pe)
                        for i in range(NPC):
                            if i:
                                pe.wait_ge(sem("turned"), i)
                            if PIECES[i][0] == "q":
                                pe.wait_ge(sem("latT"), 1)
                            project(pe, 0, i)
                        places_pe(pe)

                def steady(block, xb, x_next):
                  @block.vector
                  def _(dve):
                    link = Chain(dve, sem("dve_chain"))
                    dve.wait_ge(sem("gate_ps"), 1)
                    link(dve.tensor_scalar(gate[:, 0, :], bank[7][:, 0:3], 1.0 / S, None, ALU.mult))
                    link(dve.tensor_reduce(gsum[:], gate[:, 0, :], X, ALU.max, negate=True))
                    dve.tensor_scalar(gate[:, 1, :], gate[:, 0, :], gsum[:], None, ALU.add).then_inc(sem("gate_in"), 1)

                    for i in range(LAST):
                        if i < NU:
                            g, k, t, h = UNITS[i]
                            ps = unit_ps(i)
                            dve.wait_ge(sem("scores"), i + 1)
                            if i >= 3:
                                dve.wait_ge(sem("probT_ps"), i - 2)
                            if k < 2:
                                hn = HG if t == 0 else 2
                                diag = ps[:].rearrange("p (h k) -> p h k", h=hn)[:, :, t * P:(t + 1) * P]
                                link(dve.tensor_tensor(diag, diag, bc(cst["negmask"][:], hn), ALU.add))
                                dve.tensor_reduce(nmax[:, i % 3, 0:hn], ps[:].rearrange("p (h k) -> p h k", h=hn), X, ALU.max,
                                                  negate=True).then_inc(sem("shift"), 1)
                            else:
                                s2 = ps[:, 0:S].rearrange("p (n k) -> p n k", k=KEEP)
                                link(dve.tensor_reduce(nmax[:, i % 3, :], s2, X, ALU.max))
                                dve.tensor_tensor(sc[:, i % 3, 0:S].rearrange("p (n k) -> p n k", k=KEEP), s2,
                                                  nmax[:, i % 3, :].unsqueeze(2).broadcast_to([P, T * HG, KEEP]), ALU.subtract).then_inc(sem("shift"), 1)
                        if i == 1:
                            dve.wait_ge(sem("extra_ps"), 2)
                            ps = bank[7][:].rearrange("p (h k) -> p h k", h=NH)
                            dve.tensor_tensor(k2T[:], ps[0:QK], bc(cosT[0:QK, 0:KEEP], NH), ALU.mult)
                            for a in range(2):
                                ins = dve.tensor_tensor(t2[half(1 - a)], ps[half(a)], bc(sinT[half(a), 0:KEEP], NH), ALU.mult)
                            ins.then_inc(sem("extra"), 1)
                        p = piece_of(i)
                        if p is not None:
                            g, n = divmod(p, NPC)
                            if n == 0 and g:
                                dve.wait_ge(sem("scores"), g * NG)
                            if g:
                                dve.wait_ge(sem(PIECES[n][0] + "_added"), (g - 1) * 2 + n % 2 + 1)
                            dve.wait_ge(sem("piece_ps"), p + 1)
                            turned(dve, g + 1, n)
                        if i == 3:
                            dve.wait_ge(sem("gate_exp"), 1)
                            link(dve.tensor_reduce(gsum[:], gate[:, 2, :], X, ALU.add))
                            link(dve.reciprocal(gsum[:], gsum[:]))
                            link(dve.tensor_scalar(gate[:, 3, :], gate[:, 2, :], gsum[:], None, ALU.mult))
                        if i in MERGE_AT:
                            merge(dve, link, *MERGE_AT[i])
                        if i == A_NORM:
                            norm_stats(dve, link, x_next)
                        if i == A_NORM + 1:
                            norm_scale(dve, x_next)
                        if i == A_ROOTS:
                            mean_squares(dve)
                        if i == A_ROOTS + 1:
                            latents(dve)
                        if i in LARGEST_AT:
                            if LARGEST_AT[i] == 0:
                                dve.wait_ge(sem("uk"), 1)
                            largest(dve, link, LARGEST_AT[i])
                        if i == A_PLACES - 2:
                            places(dve, link)
                        if i == max(F_AT) + 1:
                            dve.wait_ge(sem("ffn_ps"), 1)
                            dve.tensor_tensor(xr[:], SPARE[:, 0:T * D].rearrange("p (t d) -> p t d", t=T), xb, ALU.add).then_inc(sem("ffn"), 1)
                            dve.wait_ge(sem("ffn"), 1)
                            link(dve.tensor_tensor(xr[:], xr[:], bias1[:].unsqueeze(1).broadcast_to([P, T, D]), ALU.add))
                        if i == A_SHARED:
                            dve.wait_ge(sem("scores"), NU)
                            shared_keys(dve, link)
                        if i == A_PLACES + 1:
                            select(dve, link)
                    dve.wait_ge(sem("out_ps"), 1)
                    dve.tensor_tensor(xb, xr[:], bank[1][:, 0:T * D].rearrange("p (t d) -> p t d", t=T), ALU.add)

                  @block.gpsimd
                  def _(pool):
                    link = Chain(pool, sem("pool_chain"))
                    for i in range(LAST):
                        if i == 2:
                            pool.wait_ge(sem("extra"), 2)
                            pool.tensor_tensor(k2T[0:ROPE], k2T[0:ROPE], t2[:], ALU.add).then_inc(sem("k2T"), 1)
                            pool.wait_ge(sem("k2T"), 1)
                        p = piece_of(i)
                        if p is not None:
                            g, n = divmod(p, NPC)
                            pool.wait_ge(sem("turned"), p + 1)
                            add_turned(pool, g + 1, n, g * 2 + n % 2 + 1)
                        if i == A_NORM:
                            norm_pool(pool)
                            pool.wait_ge(sem("rstd"), 1)
                        if i == A_ROOTS:
                            root_mean_squares(pool)
                        if i == A_SHARED:
                            pool.wait_ge(sem("scores"), NU)
                            latent_keys(pool, link)
                        if i in MERGE_AT:
                            g, t = MERGE_AT[i]
                            pool.wait_ge(sem("merged"), g * T + t + 1)
                            a = oo[:, t].rearrange("p a h v -> p a (h v)")
                            link(pool.tensor_tensor(a[:, 0], a[:, 0], a[:, 1], ALU.add))
                            if g >= 2:
                                pool.wait_ge(sem("otT_ps"), g - 1)
                            pool.tensor_tensor(ot[:, g % 2, t], a[:, 0], a[:, 2], ALU.add).then_inc(sem("summed"), 1)
                            pool.wait_ge(sem("summed"), g * T + t + 1)

                  @block.scalar
                  def _(act):
                    def copy_values(n):
                        k, t = VALUES[n]
                        act.wait_ge(sem("values_ps"), n + 1)
                        act.activation(vv[:, k, t, :, 0:VH], (SPARE, bank[0])[n % 2][:].rearrange("p (h v) -> p h v", h=NH), ACT.Copy).then_inc(sem("values"), 1)

                    def copy_probT(u):
                        n = 512 if UNITS[u][1] < 2 else 2 * P
                        act.wait_ge(sem("probT_ps"), u + 1)
                        if u >= 2:
                            act.wait_ge(sem("pv"), u - 1)
                        act.activation(pT[:, u % 2, 0:n], bank[5 + u % 2][:, 0:n], ACT.Copy).then_inc(sem("probT"), 1)

                    copy_values(0)
                    copy_values(1)
                    act.wait_ge(sem("extra_ps"), 1)
                    act.activation(selT[:].rearrange("p h k -> p (h k)"), bank[7][:, 0:P], ACT.Copy).then_inc(sem("extra"), 1)
                    for i in range(LAST):
                        if i < NU:
                            g, k, t, h = UNITS[i]
                            ps = unit_ps(i)
                            act.wait_ge(sem("shift"), i + 1)
                            if k < 2:
                                hn = HG if t == 0 else 2
                                kn = (t + 1) * P
                                for h in range(hn):
                                    ins = act.activation(sc[:, i % 3, h * kn:(h + 1) * kn], ps[:, h * kn:(h + 1) * kn], ACT.Exp, bias=nmax[:, i % 3, h:h + 1])
                            else:
                                ins = act.activation(sc[:, i % 3, 0:S], sc[:, i % 3, 0:S], ACT.Exp)
                            ins.then_inc(sem("prob"), 1)
                        if i in (1, 2):
                            copy_values(i + 1)
                        if i == 2:
                            act.wait_ge(sem("gate_in"), 1)
                            act.activation(gate[:, 2, :], gate[:, 1, :], ACT.Exp).then_inc(sem("gate_exp"), 1)
                        if 2 <= i < NU + 2:
                            copy_probT(i - 2)
                        if i == 3:
                            act.wait_ge(sem("extra_ps"), len(EXTRA))
                            for h in range(HG):
                                r = slice(h * KEEP, (h + 1) * KEEP)
                                ins = act.activation(v2[r, :, h, 0:VH], bank[7][r, :].rearrange("p (g h v) -> p g h v", g=G1, h=HG)[:, :, h, :], ACT.Copy)
                            ins.then_inc(sem("extra"), 1)
                        if 5 <= i < 5 + R1:
                            r = i - 5
                            act.activation(ri[:, r, :], uk[:, 0, :], ACT.Relu, scale=f1[:, 0, r:r + 1], bias=f1[:, 1, r:r + 1]).then_inc(sem("inner"), 1)
                        if i in TURN_AT:
                            g = TURN_AT[i]
                            act.wait_ge(sem("otT_ps"), g + 1)
                            act.activation(otT[:, g, :], bank[1][:, 0:S], ACT.Copy).then_inc(sem("otT"), 1)
                        if i == A_TOKENS:
                            norm_act(act, SPARE)
                        if i == A_SMALL:
                            squares(act)
                        if i == A_UNITS:
                            units_keys(act)
                        if i == A_LATENTS:
                            latents_T(act)
                    act.wait_ge(sem("otT_ps"), G1)
                    act.activation(otT[:, G1 - 1, :], bank[2][:, 0:S], ACT.Copy).then_inc(sem("otT"), 1)

                  @block.tensor
                  def _(pe):
                    def values_in(n):
                        k, t = VALUES[n]
                        if n >= 2:
                            pe.wait_ge(sem("values"), n - 1)
                        src, wt = (ccT[QL:P, :], wdv[QL:P, :]) if k == 0 else (xnT, winv[:])
                        pe.matmul((SPARE, bank[0])[n % 2][:], src[:, t * P:(t + 1) * P], wt, start=True, stop=True).then_inc(sem("values_ps"), 1)

                    def extra(i):
                        ps = bank[7]
                        if EXTRA[i] == "tokens":
                            pe.wait_ge(sem("gate_in"), 1)
                            for t in range(T):
                                mm = pe.matmul(ps[:, 0:P], xn[:, t, :], selm[:, t, :].unsqueeze(1).broadcast_to([P, HG, KEEP]), start=t == 0, stop=t == T - 1)
                        else:
                            pe.wait_ge(sem("extra"), i)
                        if EXTRA[i] == "keys":
                            for h in range(NH):
                                mm = pe.matmul(ps[0:QK, h * KEEP:(h + 1) * KEEP], selk[:, h * QK:(h + 1) * QK], selT[:, 0, :], start=True, stop=True)
                        if EXTRA[i] == "values":
                            mm = pe.matmul(ps[:], selT[:].rearrange("p h k -> p (h k)"), selv[:], start=True, stop=True)
                        mm.then_inc(sem("extra_ps"), 1)

                    def scores(u):
                        g, k, t, h = UNITS[u]
                        ps = unit_ps(u)
                        s = g % 2
                        kn = (t + 1) * P
                        if u >= 2:
                            pe.wait_ge(sem("prob"), u - 1)
                        if u % NG == 0 and g:
                            pe.wait_ge(sem("q_added"), 2 * g)
                        if u % NG == 1 and g:
                            pe.wait_ge(sem("k_added"), 2 * g)
                        if k == 2:
                            if g == 0:
                                pe.wait_ge(sem("k2T"), 1)
                            for n in range(T * HG):
                                tt, h = divmod(n, HG)
                                mm = pe.matmul(ps[:, n * KEEP:(n + 1) * KEEP], qT[0:QK, s, h, tt * P:(tt + 1) * P], k2T[:, g * HG + h, :], start=True, stop=True)
                        else:
                            for n in range(HG if t == 0 else 2):
                                o = n * kn
                                n += h
                                if k == 0:
                                    mm = pe.matmul(ps[:, o:o + kn], qT[:, s, n, t * P:(t + 1) * P], k1T[:, 0:kn], start=True, stop=True)
                                else:
                                    mm = pe.matmul(ps[:, o:o + kn], qT[0:QK, s, n, t * P:(t + 1) * P], k3T[:, s, n, 0:kn], start=True, stop=True)
                        mm.then_inc(sem("scores"), 1)

                    def turn(u):
                        pe.wait_ge(sem("prob"), u + 1)
                        if u >= 2:
                            pe.wait_ge(sem("probT"), u - 1)
                        for n in range(4 if UNITS[u][1] < 2 else 2):
                            mm = pe.transpose(bank[5 + u % 2][:, n * P:(n + 1) * P], sc[:, u % 3, n * P:(n + 1) * P], ident[:])
                        mm.then_inc(sem("probT_ps"), 1)

                    def values(u):
                        g, k, t, h = UNITS[u]
                        pe.wait_ge(sem("probT"), u + 1)
                        if g and u % NG in (0, 2):
                            pe.wait_ge(sem("merged"), (g - 1) * T + t + 1)
                        if u == 0:
                            pe.wait_ge(sem("values"), len(VALUES))
                        if u == 2:
                            pe.wait_ge(sem("extra"), len(EXTRA))
                        if k == 2:
                            for t in range(T):
                                mm = pe.matmul(outs(t)[:, 1], pT[:, u % 2, t * P:(t + 1) * P], v2[:, g].rearrange("p h v -> p (h v)"), start=True, stop=True)
                        else:
                            for n in range(4):
                                hh, j = (n, 0) if t == 0 else (h + n // 2, n % 2)
                                mm = pe.matmul(outs(t)[:, 2 * k, hh, :], pT[:, u % 2, n * P:(n + 1) * P], vv[:, k, j, g * HG + hh, :], start=j == 0, stop=j == t)
                        mm.then_inc(sem("pv"), 1)

                    def turn_outputs(g, ps):
                        pe.wait_ge(sem("summed"), (g + 1) * T)
                        for t in range(T):
                            mm = pe.transpose(ps[:, t * P:(t + 1) * P], ot[:, g % 2, t, :], ident[:])
                        mm.then_inc(sem("otT_ps"), 1)

                    for t in range(T):
                        mm = pe.matmul(bank[7][:, 0:3], ones[:], lat[:, t, QL + KVL:NS], start=t == 0, stop=t == T - 1)
                    mm.then_inc(sem("gate_ps"), 1)
                    scores(0)
                    values_in(0)
                    values_in(1)
                    extra(0)
                    for i in range(LAST):
                        if 0 < i < NU:
                            scores(i)
                        if i in (1, 2):
                            values_in(i + 1)
                        if 2 <= i < NU + 2:
                            turn(i - 2)
                        if 0 < i < len(EXTRA):
                            extra(i)
                        p = piece_of(i)
                        if p is not None:
                            g, n = divmod(p, NPC)
                            if p:
                                pe.wait_ge(sem("turned"), p)
                            if n == 0 and g >= 2:
                                pe.wait_ge(sem("otT"), g - 1)
                            if p == (G1 - 1) * NPC + 2:
                                pe.wait_ge(sem("latT"), 1)
                            project(pe, g + 1, n)
                        if i in TURN_AT:
                            pe.wait_ge(sem("turned"), (i // NG + 1) * NPC)
                            if TURN_AT[i]:
                                pe.wait_ge(sem("otT"), TURN_AT[i])
                            turn_outputs(TURN_AT[i], bank[1])
                        if i == A_TOKENS:
                            pe.wait_ge(sem("ffn"), 1)
                            norm_pe(pe, SPARE)
                        if i == A_UNITS:
                            units_pe(pe)
                        if i == A_SMALL:
                            small_pe(pe)
                        if i in F_AT:
                            if F_AT[i] == 0:
                                pe.wait_ge(sem("inner"), R1)
                            t = F_AT[i]
                            for r in range(R1):
                                mm = pe.matmul(SPARE[:, t * D:(t + 1) * D], ri[:, r, t * P:(t + 1) * P], wc1[:, r, :], start=r == 0, stop=r == R1 - 1)
                            if t == T - 1:
                                mm.then_inc(sem("ffn_ps"), 1)
                        if i == A_LATENTS:
                            latents_pe(pe)
                        if i == A_PLACES:
                            places_pe(pe)
                        if 3 <= i < NU + 3:
                            values(i - 3)
                    pe.wait_ge(sem("otT"), G1 - 1)
                    for t in range(T):
                        for g in range(G1 - 1):
                            pe.matmul(bank[1][:, t * D:(t + 1) * D], otT[:, g, t * P:(t + 1) * P], wpj[:, g, :], start=g == 0 and t == 0, stop=False, skip_group_check=True)
                    turn_outputs(G1 - 1, bank[2])
                    pe.wait_ge(sem("otT"), G1)
                    for t in range(T):
                        mm = pe.matmul(bank[1][:, t * D:(t + 1) * D], otT[:, G1 - 1, t * P:(t + 1) * P], wpj[:, G1 - 1, :], start=False, stop=True, skip_group_check=True)
                    mm.then_inc(sem("out_ps"), 1)
                with nc.Block() as block:
                    first(block)
                nc.all_engine_barrier()
                sem.clear(nc)
                nc.all_engine_barrier()
                with nc.Fori(0, B) as b:
                    with nc.Block() as block:
                        steady(block, x[:, bass.ds(b * T, T), :], x[:, bass.ds(b * T + T, T), :])
                    nc.all_engine_barrier()
                    sem.clear(nc)
                    nc.all_engine_barrier()

        if 0 in layers:
            norm_block(x[:, 0:PT, :], PT)
            with nc.Fori(0, B // PB) as b:
                layer0(b)
        prepare()
        prep.close()
        if 1 in layers:
            layer1()

        wqkvg3 = sb("wqkvg3", [P, 4, NH3 * DK3])
        bg3 = sb("bg3", [P, PAIRS])
        wo3 = sb("wo3", [P, PAIRS, D])
        gate3 = sb("gate3", [P, E3])
        gb3 = sb("gb3", [P, E3])
        w13 = sb("w13", [P, E3, F3])
        b13 = sb("b13", [P, E3, FC3])
        w23 = sb("w23", [P, E3, FC3, D])
        b23 = sb("b23", [E3, D])
        level3 = sb("level3", [P, len(LEVELS) * 2 * T * P // 2], U32)
        s_load3 = ctx.enter_context(nc.semaphore("loaded3"))
        loads3 = [(wqkvg3[:, n, :], w[name]) for n, name in enumerate(("W_q", "W_k", "W_v", "W_gate"))]
        loads3 += [
            (bg3[:], w["b_gateT"]),
            (wo3[:], w["W_o"].rearrange("(c p) d -> p c d", p=P)),
            (gate3[:], w["gate3T"]),
            (gb3[:], w["gb3_rep"]),
            (w13[:], w["W13"].rearrange("e d f -> d e f")),
            (b13[:], w["b13T"]),
            (w23[:], w["W23"].rearrange("e (c p) d -> p e c d", p=P)),
            (b23[:], w["b23"]),
            (level3[:], w["c_level"]),
        ]
        if 3 in layers:
            with nc.Block() as block:
                @block.sync
                def _(sp):
                    for dst, src in loads3:
                        sp.dma_start(dst, src).then_inc(s_load3, 16)
        if 2 in layers:
            norm_block(x[:, 0:PT, :], PT)
            with nc.Fori(0, B // PB) as b:
                layer2(b)
        if 3 in layers:
            with nc.Block() as block:
                @block.tensor
                def _(pe):
                    pe.wait_ge(s_load3, 16 * len(loads3))

                @block.vector
                def _(dve):
                    dve.wait_ge(s_load3, 16 * len(loads3))

                @block.scalar
                def _(act):
                    act.wait_ge(s_load3, 16 * len(loads3))
            layer3(wqkvg3, bg3, wo3, gate3, gb3, w13, b13, w23, b23, level3)

        with nc.Block() as block:
            @block.sync
            def _(sp):
                sp.dma_start(out.rearrange("b (t p) d -> p (b t) d", p=P), x[:, 0:B * T, :]).then_inc(s_out, 16)
                sp.wait_ge(s_out, 16)


def host_layout(i):
    t = lambda a: np.ascontiguousarray(a)
    L = {}
    L["x"] = i["L0_attn_x"]
    L["w_lhs"], L["w_rhs"] = i["L0_attn_w_lhs"], i["L0_attn_w_rhs"]
    L["W_fcT"] = t(i["L0_ffn_W_fc"].T)
    L["W_projT"] = t(i["L0_ffn_W_proj"].T)
    L["ln_wT"], L["ln_bT"] = t(i["L0_ffn_ln_w"].reshape(C0, P).T), t(i["L0_ffn_ln_b"].reshape(C0, P).T)
    for n in ("w_cq", "w_ckv", "w_gate", "g_qnorm", "g_kvnorm", "w_dv", "w_imp", "w_selv", "w_winv", "w_proj"):
        L[n] = i["L1_attn_" + n]
    nope = i["L1_attn_w_dq_nope"].reshape(QL, NH, NOPE)
    rope = i["L1_attn_w_dq_rope"].reshape(QL, NH, ROPE)
    L["w_dq"] = t(np.concatenate([rope, nope], 2))
    L["w_krope"] = i["L1_attn_w_krope"]
    L["w_dqT"] = t(nope.transpose(2, 1, 0).reshape(NOPE, -1))
    L["w_dkT"] = t(i["L1_attn_w_dk_nope"].reshape(KVL, NH, NOPE).transpose(2, 1, 0).reshape(NOPE, -1))
    for n in ("w_selk", "w_wink"):
        a = i["L1_attn_" + n].reshape(D, NH, QK)
        L[n] = t(np.concatenate([a[..., NOPE:], a[..., :NOPE]], 2).reshape(D, NH * QK))
    for n in ("W1", "b1", "W2", "b2", "Wout"):
        L[n] = i["L1_ffn_" + n]
    L["bin_rep"] = t(np.repeat(i["L1_ffn_bin_"], J1)[:, None])
    L["Win_rep"] = t(np.repeat(i["L1_ffn_Win"][:, :, None], J1, axis=2))
    L["Wout_rep"] = t(np.repeat(i["L1_ffn_Wout"], J1, axis=0))
    L["bout_rep"] = t(np.broadcast_to(i["L1_ffn_bout"], (P, D)))
    for n in "QKV":
        L[f"W{n}T"] = t(i[f"L2_attn_W{n}"].T)
    L["gate2T"] = t(i["L2_ffn_gate_w"].T)
    L["bias2_rep"] = t(np.broadcast_to(i["L2_ffn_bias_e"], (P, E2)))
    L["up2T"] = t(i["L2_ffn_up_w"].transpose(2, 0, 1).reshape(D, E2 * I2))
    L["down2"] = t(i["L2_ffn_down_w"].transpose(0, 2, 1).reshape(E2 * I2, D))
    L["sup2T"] = t(i["L2_ffn_shared_up"].T)
    L["sdown2T"] = t(i["L2_ffn_shared_down"].T)
    for n in ("W_q", "W_k", "W_v", "W_gate", "W_o"):
        L[n] = i["L3_attn_" + n]
    L["b_gateT"] = t(i["L3_attn_b_gate"].reshape(PAIRS, P).T)
    L["gate3T"] = t(i["L3_ffn_gate_w"].T)
    L["gb3_rep"] = t(np.broadcast_to(i["L3_ffn_gate_b"], (P, E3)))
    L["b13T"] = t(i["L3_ffn_b1"].reshape(E3, FC3, P).transpose(2, 0, 1))
    L["W13"], L["W23"], L["b23"] = i["L3_ffn_W1"], i["L3_ffn_W2"], i["L3_ffn_b2"]
    for n, a in constants().items():
        L["c_" + n] = a
    return L


def kernel(**inputs):
    import concourse.bacc as _bacc
    from concourse.bass_utils import run_bass_kernel_spmd as _run

    arrays = {f"in_{n}": np.ascontiguousarray(a) for n, a in host_layout({k: np.asarray(v) for k, v in inputs.items()}).items()}
    nc = _bacc.Bacc("TRN2", target_bir_lowering=False, num_devices=1)
    w = {n[3:]: nc.dram_tensor(n, a.shape, mybir.dt.from_np(a.dtype), kind="ExternalInput").ap() for n, a in arrays.items()}
    out = nc.dram_tensor("out_x", (B, S, D), F32, kind="ExternalOutput").ap()
    program(nc, w, out)
    r = _run(nc, [arrays], core_ids=[0])
    return r.results[0]["out_x"]
```
